# Optimizing a Trainium2 kernel written in Bass

```python
import numpy as np
import jax
import jax.numpy as jnp

def _softmax(x, axis=-1):
    return jax.nn.softmax(x, axis=axis)

def _gelu(x):
    return jax.nn.gelu(x, approximate=True)

def _silu(x):
    return jax.nn.silu(x)

def _sigmoid(x):
    return jax.nn.sigmoid(x)

def _layernorm(x, axis=-1, eps=1e-05):
    m = jnp.mean(x, axis=axis, keepdims=True)
    v = jnp.var(x, axis=axis, keepdims=True)
    return (x - m) / jnp.sqrt(v + eps)

def _scatter_add(tgt, idx, src, axis=0):
    return tgt.at[idx].add(src)

def _segment_sum(src, seg, n):
    return jax.ops.segment_sum(src, seg, n)
kernel_name = 'mk_gnn_ffn_d1_gnn_r32_a14cb3'

def setup_inputs(seed: int=0):
    np.random.seed(seed)
    _w = jnp.asarray

    def _rec_inputs():
        import jax
        import jax.numpy as jnp
        _gk = jax.random.key(seed)
        x = -0.0003713 + 1 * jax.random.normal(jax.random.fold_in(_gk, 1), (3125, 256), jnp.float32)
        src = jax.random.randint(jax.random.fold_in(_gk, 2), (50000,), 0, 3125, jnp.int32)
        dst = jax.random.randint(jax.random.fold_in(_gk, 3), (50000,), 0, 3125, jnp.int32)
        _o = jnp.argsort(dst, stable=True)
        src = src[_o]
        dst = dst[_o]
        edge_attr_194 = 0.000189139 + 1.00015 * jax.random.normal(jax.random.fold_in(_gk, 11), (50000, 194), jnp.float32)
        return (x, src, dst, edge_attr_194)
    x, src, dst, edge_attr_194 = _rec_inputs()

    def _L0_gnn_setup():
        import jax, jax.numpy as jnp
        import numpy as np
        N = 50000
        E = 250000
        IN = 256
        OUT = 256
        H = 4
        C = OUT // H
        MSG = 128
        TIME = 64
        ED = MSG + TIME + 2

        def _glorot(k, shape):
            return (jax.random.normal(k, shape, jnp.float32) / np.sqrt(shape[0])).astype(jnp.float32)

        def _tconv(x, src, dst, edge_attr, Wq, bq, Wk, bk, Wv, bv, We, Ws, bs):
            n = x.shape[0]
            q = (x @ Wq + bq).reshape(n, H, C)
            k = (x @ Wk + bk).reshape(n, H, C)
            v = (x @ Wv + bv).reshape(n, H, C)
            e = (edge_attr @ We).reshape(-1, H, C)
            kj = k[src] + e
            vj = v[src] + e
            logits = jnp.einsum('ehc,ehc->eh', q[dst], kj) / np.sqrt(C)
            m = jax.lax.stop_gradient(jax.ops.segment_max(logits, dst, num_segments=n))
            ex = jnp.exp(logits - m[dst])
            denom = jax.ops.segment_sum(ex, dst, num_segments=n)
            a = ex / (denom[dst] + 1e-16)
            agg = jax.ops.segment_sum(vj * a[:, :, None], dst, num_segments=n)
            return agg.reshape(n, H * C) + x @ Ws + bs
        ks = jax.random.split(jax.random.key(seed), 16)
        z = lambda: jnp.zeros((H * C,), jnp.float32)
        inp = {'x': jax.random.normal(ks[0], (N, IN), jnp.float32), 'edge_index': jax.random.randint(ks[1], (2, E), 0, N), 'edge_attr': jax.random.normal(ks[2], (E, ED), jnp.float32), 'Wq1': _glorot(ks[3], (IN, H * C)), 'bq1': z(), 'Wk1': _glorot(ks[4], (IN, H * C)), 'bk1': z(), 'Wv1': _glorot(ks[5], (IN, H * C)), 'bv1': z(), 'We1': _glorot(ks[6], (ED, H * C)), 'Ws1': _glorot(ks[7], (IN, H * C)), 'bs1': z(), 'Wq2': _glorot(ks[8], (OUT, H * C)), 'bq2': z(), 'Wk2': _glorot(ks[9], (OUT, H * C)), 'bk2': z(), 'Wv2': _glorot(ks[10], (OUT, H * C)), 'bv2': z(), 'We2': _glorot(ks[11], (ED, H * C)), 'Ws2': _glorot(ks[12], (OUT, H * C)), 'bs2': z()}
        return inp
    _L0_gnn_all = _L0_gnn_setup()
    _L0_gnn_in = {k: v for k, v in _L0_gnn_all.items() if k in ('Wq1', 'bq1', 'Wk1', 'bk1', 'Wv1', 'bv1', 'We1', 'Ws1', 'bs1', 'Wq2', 'bq2', 'Wk2', 'bk2', 'Wv2', 'bv2', 'We2', 'Ws2', 'bs2')}
    del _L0_gnn_all

    def _L0_ffn_setup():
        import jax, jax.numpy as jnp
        import numpy as np
        B, S, D, E, H, K = (4, 128, 256, 8, 512, 2)
        key = jax.random.key(seed)
        ks = jax.random.split(key, 6)
        x = jax.random.normal(ks[0], (B, S, D), jnp.float32)
        Wg = jax.random.normal(ks[1], (D, E), jnp.float32) * 0.02
        bg = jnp.zeros((E,), jnp.float32)
        W1 = jax.random.normal(ks[2], (E, D, H), jnp.float32) * 0.02
        b1 = jnp.zeros((E, H), jnp.float32)
        W2 = jax.random.normal(ks[3], (E, H, D), jnp.float32) * 0.02
        b2 = jnp.zeros((E, D), jnp.float32)
        return {'x': x, 'Wg': Wg, 'bg': bg, 'W1': W1, 'b1': b1, 'W2': W2, 'b2': b2}
    _L0_ffn_all = _L0_ffn_setup()
    _L0_ffn_in = {k: v for k, v in _L0_ffn_all.items() if k in ('Wg', 'bg', 'W1', 'b1', 'W2', 'b2')}
    del _L0_ffn_all
    return {'x': x, 'src': src, 'dst': dst, 'edge_attr_194': edge_attr_194, 'L0_gnn_Wq1': _L0_gnn_in['Wq1'], 'L0_gnn_bq1': _L0_gnn_in['bq1'], 'L0_gnn_Wk1': _L0_gnn_in['Wk1'], 'L0_gnn_bk1': _L0_gnn_in['bk1'], 'L0_gnn_Wv1': _L0_gnn_in['Wv1'], 'L0_gnn_bv1': _L0_gnn_in['bv1'], 'L0_gnn_We1': _L0_gnn_in['We1'], 'L0_gnn_Ws1': _L0_gnn_in['Ws1'], 'L0_gnn_bs1': _L0_gnn_in['bs1'], 'L0_gnn_Wq2': _L0_gnn_in['Wq2'], 'L0_gnn_bq2': _L0_gnn_in['bq2'], 'L0_gnn_Wk2': _L0_gnn_in['Wk2'], 'L0_gnn_bk2': _L0_gnn_in['bk2'], 'L0_gnn_Wv2': _L0_gnn_in['Wv2'], 'L0_gnn_bv2': _L0_gnn_in['bv2'], 'L0_gnn_We2': _L0_gnn_in['We2'], 'L0_gnn_Ws2': _L0_gnn_in['Ws2'], 'L0_gnn_bs2': _L0_gnn_in['bs2'], 'L0_ffn_Wg': _L0_ffn_in['Wg'], 'L0_ffn_bg': _L0_ffn_in['bg'], 'L0_ffn_W1': _L0_ffn_in['W1'], 'L0_ffn_b1': _L0_ffn_in['b1'], 'L0_ffn_W2': _L0_ffn_in['W2'], 'L0_ffn_b2': _L0_ffn_in['b2']}

def reference(x, src, dst, edge_attr_194, L0_gnn_Wq1, L0_gnn_bq1, L0_gnn_Wk1, L0_gnn_bk1, L0_gnn_Wv1, L0_gnn_bv1, L0_gnn_We1, L0_gnn_Ws1, L0_gnn_bs1, L0_gnn_Wq2, L0_gnn_bq2, L0_gnn_Wk2, L0_gnn_bk2, L0_gnn_Wv2, L0_gnn_bv2, L0_gnn_We2, L0_gnn_Ws2, L0_gnn_bs2, L0_ffn_Wg, L0_ffn_bg, L0_ffn_W1, L0_ffn_b1, L0_ffn_W2, L0_ffn_b2):
    import jax
    import jax.numpy as jnp

    def _L0_gnn_ref(x, edge_index, edge_attr, Wq1, bq1, Wk1, bk1, Wv1, bv1, We1, Ws1, bs1, Wq2, bq2, Wk2, bk2, Wv2, bv2, We2, Ws2, bs2):
        import jax, jax.numpy as jnp
        import numpy as np
        N = 50000
        E = 250000
        IN = 256
        OUT = 256
        H = 4
        C = OUT // H
        MSG = 128
        TIME = 64
        ED = MSG + TIME + 2

        def _glorot(k, shape):
            return (jax.random.normal(k, shape, jnp.float32) / np.sqrt(shape[0])).astype(jnp.float32)

        def _tconv(x, src, dst, edge_attr, Wq, bq, Wk, bk, Wv, bv, We, Ws, bs):
            n = x.shape[0]
            q = (x @ Wq + bq).reshape(n, H, C)
            k = (x @ Wk + bk).reshape(n, H, C)
            v = (x @ Wv + bv).reshape(n, H, C)
            e = (edge_attr @ We).reshape(-1, H, C)
            kj = k[src] + e
            vj = v[src] + e
            logits = jnp.einsum('ehc,ehc->eh', q[dst], kj) / np.sqrt(C)
            m = jax.lax.stop_gradient(jax.ops.segment_max(logits, dst, num_segments=n))
            ex = jnp.exp(logits - m[dst])
            denom = jax.ops.segment_sum(ex, dst, num_segments=n)
            a = ex / (denom[dst] + 1e-16)
            agg = jax.ops.segment_sum(vj * a[:, :, None], dst, num_segments=n)
            return agg.reshape(n, H * C) + x @ Ws + bs
        src, dst = (edge_index[0], edge_index[1])
        h = jax.nn.relu(_tconv(x, src, dst, edge_attr, Wq1, bq1, Wk1, bk1, Wv1, bv1, We1, Ws1, bs1))
        return _tconv(h, src, dst, edge_attr, Wq2, bq2, Wk2, bk2, Wv2, bv2, We2, Ws2, bs2)

    def _L0_ffn_ref(x, Wg, bg, W1, b1, W2, b2):
        import jax, jax.numpy as jnp
        import numpy as np
        B, S, D, E, H, K = (4, 128, 256, 8, 512, 2)
        Bv, Sv, Dv = x.shape
        gate_scores = x @ Wg + bg
        _, idx = jax.lax.top_k(gate_scores, K)
        mask = jax.nn.one_hot(idx, E, dtype=x.dtype).sum(axis=-2)
        xf = x.reshape(-1, Dv)
        mf = mask.reshape(-1, E)
        h = jax.nn.gelu(jnp.einsum('td,edh->teh', xf, W1) + b1[None], approximate=False)
        y = jnp.einsum('teh,ehd->ted', h, W2) + b2[None]
        out = jnp.einsum('ted,te->td', y, mf)
        return out.reshape(Bv, Sv, Dv)
    edge_index = jnp.stack([src, dst])
    x = x + _L0_gnn_ref(_layernorm(x, axis=-1), edge_index, edge_attr_194, L0_gnn_Wq1, L0_gnn_bq1, L0_gnn_Wk1, L0_gnn_bk1, L0_gnn_Wv1, L0_gnn_bv1, L0_gnn_We1, L0_gnn_Ws1, L0_gnn_bs1, L0_gnn_Wq2, L0_gnn_bq2, L0_gnn_Wk2, L0_gnn_bk2, L0_gnn_Wv2, L0_gnn_bv2, L0_gnn_We2, L0_gnn_Ws2, L0_gnn_bs2)
    x = x + _L0_ffn_ref(_layernorm(x, axis=-1)[None], L0_ffn_Wg, L0_ffn_bg, L0_ffn_W1, L0_ffn_b1, L0_ffn_W2, L0_ffn_b2)[0]
    return x

_drawn_inputs = setup_inputs


def setup_inputs(seed=0):
    import zlib

    import numpy as np

    out = dict(_drawn_inputs(seed))
    spreads = {'L0_gnn_bq1': (0.0, 0.1),
     'L0_gnn_bk1': (0.0, 0.8),
     'L0_gnn_bv1': (0.0, 0.1),
     'L0_gnn_bs1': (0.0, 0.1),
     'L0_gnn_bq2': (0.0, 0.1),
     'L0_gnn_bk2': (0.0, 0.8),
     'L0_gnn_bv2': (0.0, 0.1),
     'L0_gnn_bs2': (0.0, 0.1),
     'L0_ffn_bg': (0.0, 0.1),
     'L0_ffn_b1': (0.0, 0.339),
     'L0_ffn_b2': (0.0, 0.1)}
    factors = {}
    for name, (base, spread) in spreads.items():
        noise = np.random.default_rng([zlib.crc32(name.encode()), seed]).standard_normal(out[name].shape)
        drawn = base * np.exp(spread * noise) if base else spread * noise
        out[name] = jnp.asarray(drawn.astype(out[name].dtype))
    for name, factor in factors.items():
        out[name] = (out[name] * factor).astype(out[name].dtype)
    return out
```

```python
from contextlib import ExitStack

import numpy as np

import concourse.bass as bass
from concourse import mybir
from concourse.alu_op_type import AluOpType as ALU

P = 128
N, D, H, C = 3125, 256, 4, 64
NB = -(-N // P)
NP = NB * P
E_REAL, ED = 50000, 194
G = 14
PAIRS = G // 2
T = 392
HALVES = T // G
EDGES = T * P
ED0, ED1 = P, ED - P
ED1_MANY = 64
HW = C + 1
ROW = H * HW + H
MAXAT = H * HW
SLOT = 4 + 2 * D
KAT, VAT = 4, 4 + D
NULL = EDGES
CH, CR = 4, T // 4
XN, XD, XH = 8, 256, 512
HC = XH // P
GT = 5
GN = GT * P
LOW = -1e30
INV = 1.0 / 8.0
EPS = 1e-5

ACT = mybir.ActivationFunctionType
AX = mybir.AxisListType
F32 = mybir.dt.float32
BF16 = mybir.dt.bfloat16
I32 = mybir.dt.int32
U32 = mybir.dt.uint32
ds = bass.ds


class Chain:

    def __init__(self, eng, sem, passed=None):
        self.eng, self.sem, self.passed, self.base, self.n = eng, sem, passed, 0, 0

    def after(self, ins, alone=False):
        ins.then_inc(self.sem, 1)
        self.n += 1
        if alone:
            wait_alone(self.eng, self.sem, self.base + self.n, self.passed)
        else:
            self.eng.wait_ge(self.sem, self.base + self.n)


def wait_alone(eng, sem, value, passed):
    eng.wait_ge(sem, value)
    eng.sem_inc(passed, 1)


def kernel_program(nc, a):
    with ExitStack() as ctx:
        dram = lambda name, shape: nc.dram_tensor(name, shape, F32, kind="Internal").ap()
        tables = {"kv": dram("kv_table", (NP, 2 * D)), "q": dram("q_table", (NP, D)),
                  "skip": dram("skip_table", (NP, D)), "part": dram("partials", (EDGES + 1 + T, ROW))}
        keep = lambda name, shape, dt=F32: ctx.enter_context(nc.sbuf_tensor(name, shape, dt))
        k = {
            "ident": keep("ident", [P, P]),
            "dst_col": keep("dst_col", [P, T]),
            "new_fwd": keep("new_fwd", [4 * G, HALVES, P]),
            "new_bwd": keep("new_bwd", [4 * G, HALVES, P]),
            "chain_mask": keep("chain_mask", [CR, CH, T]),
            "chain_new": keep("chain_new", [H, T]),
            "row_end": keep("row_end", [P, NB], U32),
            "row_before": keep("row_before", [P, NB], U32),
            "head_row": keep("head_row", [H, H, CR]),
        }
        setup(nc, a, tables, k)
        node_blocks(nc, a, tables, k, "first")
        for layer in (1, 2):
            edge_pass(nc, a, tables, k, layer)
            chain_pass(nc, a, tables, k, layer)
            if layer == 1:
                node_blocks(nc, a, tables, k, "middle")
        x1 = keep("x1", [P, NB, D])
        xfT = keep("xfT", [P, 2, NP])
        gate = keep("gate", [P, NB, XN])
        k.update(x1=x1, xfT=xfT, gate=gate)
        node_blocks(nc, a, tables, k, "last")
        experts(nc, a, k)


def setup(nc, a, tables, k):
    with ExitStack() as ctx:
        sb = lambda name, shape, dt=F32: ctx.enter_context(nc.sbuf_tensor("su_" + name, shape, dt))
        sem = lambda name: ctx.enter_context(nc.semaphore("su_" + name))
        dcol = sb("dcol", [P, T], I32)
        lo_i, hi_i = sb("lo_i", [P, T], I32), sb("hi_i", [P, T], I32)
        lo, hi = sb("lo", [P, T]), sb("hi", [P, T])
        drow = sb("drow", [4 * G, HALVES, P], I32)
        iota_p, iota_b = sb("iota_p", [P, P]), sb("iota_b", [P, P], BF16)
        hot_hi = sb("hot_hi", [P, T, NB], BF16)
        U = 8
        hot_lo = sb("hot_lo", [P, U, P], BF16)
        tri, ones = sb("tri", [P, P]), sb("ones", [P, P])
        cnt, tot, off, cum = sb("cnt", [P, NB]), sb("tot", [P, NB]), sb("off", [P, NB]), sb("cum", [P, NB])
        zero = sb("zero", [P, NB])
        t1, t2, g1 = sb("t1", [P, NB]), sb("t2", [P, NB]), sb("g1", [P, NB])
        ti, tf = sb("ti", [P, NB], I32), sb("tf", [P, NB])
        null = sb("null", [1, ROW])
        dlb, dlc = sb("dlb", [CR, T], I32), sb("dlc", [CR, CH], I32)
        dl4 = sb("dl4", [H, T], I32)
        ps = ctx.enter_context(nc.psum_tensor("su_ps", [P, 512], F32))
        ps2 = ctx.enter_context(nc.psum_tensor("su_ps2", [P, 512], F32))
        ps3 = ctx.enter_context(nc.psum_tensor("su_ps3", [P, 512], F32))
        s_in, s_pool, s_v, s_hot, s_mm, s_cnt, s_cum, s_null, s_nulled = (
            sem(n) for n in ("loaded", "pool", "vec", "hot", "hist", "counted", "cum", "null", "nulled"))
        block = ctx.enter_context(nc.Block())

        @block.sync
        def _(sp):
            sp.dma_start(dcol[:], a["dst_cols"]).then_inc(s_in, 16)
            for h in range(H):
                sp.dma_start(drow[h * G:(h + 1) * G], a["dst"].rearrange("(u t e) -> t u e", t=G, e=P)
                             ).then_inc(s_in, 16)
            sp.dma_start(dlb[:], a["dst_last"][None, :].to_broadcast([CR, T])).then_inc(s_in, 16)
            sp.dma_start(dlc[:], a["dst_last_cols"]).then_inc(s_in, 16)
            sp.dma_start(dl4[:], a["dst_last"][None, :].to_broadcast([H, T])).then_inc(s_in, 16)
            sp.wait_ge(s_null, 2)
            sp.dma_start(tables["part"][NULL:NULL + 1], null[:]).then_inc(s_nulled, 16)
            sp.wait_ge(s_nulled, 16)

        @block.gpsimd
        def _(pool):
            c = Chain(pool, s_pool)
            c.after(nc.gpsimd.memset(k["ident"][:], 0.0))
            c.after(nc.gpsimd.affine_select(out=k["ident"][:], in_=k["ident"][:], compare_op=ALU.not_equal,
                                            fill=1.0, base=0, pattern=[[-1, P]], channel_multiplier=1))
            c.after(nc.gpsimd.memset(ones[:], 1.0))
            c.after(nc.gpsimd.affine_select(out=tri[:], in_=ones[:], compare_op=ALU.is_ge, fill=0.0, base=0,
                                            pattern=[[1, P]], channel_multiplier=-1))
            c.after(nc.gpsimd.iota(iota_p[:], pattern=[[1, P]], base=0, channel_multiplier=0,
                                   allow_small_or_imprecise_dtypes=True))
            c.after(nc.gpsimd.memset(k["chain_mask"][:], 1.0))
            c.after(nc.gpsimd.affine_select(out=k["chain_mask"][:], in_=k["chain_mask"][:],
                                            compare_op=ALU.is_ge, fill=0.0, base=0,
                                            pattern=[[-CR, CH], [1, T]], channel_multiplier=-1))
            c.after(nc.gpsimd.memset(k["head_row"][:], 0.0))
            c.after(nc.gpsimd.affine_select(out=k["head_row"][:], in_=k["head_row"][:], compare_op=ALU.not_equal,
                                            fill=1.0, base=0, pattern=[[-1, H], [0, CR]], channel_multiplier=1))

        @block.vector
        def _(v):
            c = Chain(v, s_v)
            nc.vector.memset(null[:, 0:MAXAT], 0.0).then_inc(s_null, 1)
            nc.vector.memset(null[:, MAXAT:ROW], LOW).then_inc(s_null, 1)
            c.after(nc.vector.memset(zero[:], 0.0))
            v.wait_ge(s_in, 16 * 8)
            c.after(nc.vector.tensor_copy(k["dst_col"][:], dcol[:]))
            c.after(nc.vector.tensor_single_scalar(lo_i[:], dcol[:], P - 1, ALU.bitwise_and))
            c.after(nc.vector.tensor_single_scalar(hi_i[:], dcol[:], 7, ALU.arith_shift_right))
            c.after(nc.vector.tensor_copy(lo[:], lo_i[:]))
            c.after(nc.vector.tensor_copy(hi[:], hi_i[:]))
            v.wait_ge(s_pool, 9)
            c.after(nc.vector.tensor_copy(iota_b[:], iota_p[:]))
            nc.vector.tensor_tensor(hot_hi[:], hi[:].unsqueeze(2).to_broadcast([P, T, NB]),
                                    iota_p[:, None, 0:NB].to_broadcast([P, T, NB]), ALU.is_equal
                                    ).then_inc(s_hot, 1)
            for i in range(U):
                nc.vector.tensor_scalar(hot_lo[:, i], iota_b[:], lo[:, i:i + 1], None, ALU.is_equal
                                        ).then_inc(s_hot, 1)
            with v.Fori(1, T // U) as it:
                for i in range(U):
                    v.wait_ge(s_mm, it * U + (i - U + 1))
                    nc.vector.tensor_scalar(hot_lo[:, i], iota_b[:], lo[:, ds(it * U + i, 1)], None, ALU.is_equal
                                            ).then_inc(s_hot, 1)
            c.after(nc.vector.memset(k["new_fwd"][:], 0.0))
            c.after(nc.vector.memset(k["new_bwd"][:], 0.0))
            c.after(nc.vector.tensor_tensor(k["new_fwd"][:, :, 1:P], drow[:, :, 1:P], drow[:, :, 0:P - 1],
                                            ALU.not_equal))
            c.after(nc.vector.tensor_scalar(k["new_fwd"][:], k["new_fwd"][:], LOW, None, ALU.mult))
            c.after(nc.vector.tensor_copy(k["new_bwd"][:, :, 1:P], k["new_fwd"][:, :, P - 1:0:-1]))
            dl_b = dlb[:, None, :].to_broadcast([CR, CH, T])
            dl_c = dlc[:].unsqueeze(2).to_broadcast([CR, CH, T])
            same = hot_hi[0:CR].rearrange("p t n -> p (t n)")[:, 0:CH * T].rearrange("p (c t) -> p c t", c=CH)
            v.wait_ge(s_mm, T)
            c.after(nc.vector.tensor_tensor(same, dl_b, dl_c, ALU.is_equal))
            c.after(nc.vector.tensor_tensor(k["chain_mask"][:], k["chain_mask"][:], same, ALU.mult))
            c.after(nc.vector.memset(k["chain_new"][:], 0.0))
            c.after(nc.vector.tensor_tensor(k["chain_new"][:, 1:T], dl4[:, 1:T], dl4[:, 0:T - 1], ALU.not_equal))
            c.after(nc.vector.tensor_scalar(k["chain_new"][:], k["chain_new"][:], LOW, None, ALU.mult))
            nc.vector.tensor_copy(cnt[:], ps[:, 0:NB]).then_inc(s_cnt, 1)
            v.wait_ge(s_cum, 2)
            c.after(nc.vector.tensor_copy(tot[:], ps3[:, 0:NB]))
            c.after(nc.vector.tensor_tensor_scan(off[:], tot[:], zero[:], 0.0, ALU.add, ALU.add))
            c.after(nc.vector.tensor_tensor(off[:], off[:], tot[:], ALU.subtract))
            c.after(nc.vector.tensor_tensor(cum[:], ps2[:, 0:NB], off[:], ALU.add))
            v.wait_ge(s_cnt, 1)
            c.after(nc.vector.tensor_scalar(g1[:], cnt[:], 0.0, None, ALU.is_gt))
            c.after(nc.vector.tensor_scalar(t1[:], cum[:], -1.0, None, ALU.add))
            c.after(nc.vector.tensor_copy(ti[:], t1[:]))
            c.after(nc.vector.tensor_scalar(t1[:], t1[:], -float(NULL), None, ALU.add))
            c.after(nc.vector.tensor_tensor(t1[:], t1[:], g1[:], ALU.mult))
            c.after(nc.vector.tensor_scalar(t1[:], t1[:], float(NULL), None, ALU.add))
            c.after(nc.vector.tensor_copy(k["row_end"][:], t1[:]))
            c.after(nc.vector.tensor_scalar(t2[:], cum[:], -1.0, 0.0, ALU.add, ALU.max))
            c.after(nc.vector.tensor_copy(ti[:], t2[:]))
            c.after(nc.vector.tensor_single_scalar(ti[:], ti[:], 7, ALU.arith_shift_right))
            c.after(nc.vector.tensor_copy(tf[:], ti[:]))
            c.after(nc.vector.tensor_tensor(t2[:], cum[:], cnt[:], ALU.subtract))
            c.after(nc.vector.scalar_tensor_tensor(out=t2[:], in0=tf[:], scalar=float(P), in1=t2[:],
                                                   op0=ALU.mult, op1=ALU.is_gt))
            c.after(nc.vector.tensor_tensor(t2[:], t2[:], g1[:], ALU.mult))
            c.after(nc.vector.tensor_tensor(t2[:], t2[:], tf[:], ALU.mult))
            c.after(nc.vector.tensor_scalar(t2[:], t2[:], float(NULL), None, ALU.add))
            c.after(nc.vector.tensor_copy(k["row_before"][:], t2[:]))

        @block.tensor
        def _(te):
            def count(n, i):
                te.wait_ge(s_hot, n + 2)
                hi_rows = hot_hi[:, n] if isinstance(n, int) else hot_hi[:, ds(n, 1)].rearrange("p t n -> p (t n)")
                nc.tensor.matmul(ps[:, 0:NB], hot_lo[:, i], hi_rows, start=first(n), stop=last(n)).then_inc(s_mm, 1)

            first = lambda n: isinstance(n, int) and n == 0
            last = lambda n: isinstance(n, int) and n == T - 1
            for i in range(U):
                count(i, i)
            with te.Fori(1, T // U - 1) as it:
                for i in range(U):
                    count(it * U + i, i)
            for i in range(U):
                count(T - U + i, i)
            te.wait_ge(s_cnt, 1)
            nc.tensor.matmul(ps2[:, 0:NB], tri[:], cnt[:], start=True, stop=True).then_inc(s_cum, 1)
            nc.tensor.matmul(ps3[:, 0:NB], ones[:], cnt[:], start=True, stop=True).then_inc(s_cum, 1)


def each(eng, step):
    step(0, 0, 1)
    step(1, 1, 1)
    step(2, 0, 2)
    with eng.Fori(1, (NB - 1) // 2) as it:
        step(it * 2 + 1, 1, it + 1)
        step(it * 2 + 2, 0, it + 2)


def later(j):
    return not isinstance(j, int) or j >= 2


def block_of(ap, j):
    if isinstance(j, int):
        return ap[:, j]
    return ap[:, ds(j, 1)].rearrange("p o d -> p (o d)")


def blocks(table):
    return table.rearrange("(b p) d -> p b d", p=P)


def rows_of(table, j):
    return table[ds(j * P, P)] if not isinstance(j, int) else table[j * P:(j + 1) * P]


def node_blocks(nc, a, tables, k, kind):
    gather, proj, norm = kind != "first", kind != "last", kind != "middle"
    layer = 1 if kind == "first" else 2
    with ExitStack() as ctx:
        sb = lambda name, shape, dt=F32: ctx.enter_context(nc.sbuf_tensor(kind + "_" + name, shape, dt))
        sem = lambda name: ctx.enter_context(nc.semaphore(kind + "_" + name))
        ps_turn = ctx.enter_context(nc.psum_tensor(kind + "_turn", [P, 2, 512], F32))
        ps_out = ctx.enter_context(nc.psum_tensor(kind + "_out", [P, 2, 2, 512], F32))
        z, zT = sb("z", [P, 2, D]), sb("zT", [P, 2, 2, P])
        s_w, s_vec, s_z, s_turn, s_zT, s_mm, s_out = (
            sem(n) for n in ("weights", "vec", "z", "turned", "zT", "products", "outs"))
        s_in = [sem(f"in{i}") for i in range(2)]
        s_passed, s_ppassed = sem("passed"), sem("ppassed")
        if gather:
            skip, part = sb("skip", [P, NB, D]), sb("part", [P, 2, 2, ROW])
            idx = sb("idx", [P, 2, 2], U32)
            mx, dm, sc = sb("mx", [P, H]), sb("dm", [P, 2, H]), sb("sc", [P, 2, H])
            scaled, den = sb("scaled", [P, 2, H, HW]), sb("den", [P, H])
            joined = sb("joined", [P, D])
            s_idx, s_dm, s_sc = sem("idx"), sem("dm"), sem("sc")
            s_part = [sem(f"part{i}") for i in range(2)]
        if norm:
            xin = k["x1"] if kind == "last" else sb("x", [P, NB, D])
            stats, mv, rs, std = sb("stats", [P, 6]), sb("mv", [P, 2]), sb("rs", [P, 1]), sb("std", [P, 1])
            s_var, s_std = sem("var"), sem("std")
        if proj:
            w, bias = sb("w", [P, 2, 4 * D]), sb("bias", [P, 4 * D])
            outs = sb("outs", [P, 2, 4 * D])
            s_st = [sem(f"stored{i}") for i in range(2)]
        else:
            wg, bg, b2 = sb("wg", [P, 2, XN]), sb("bg", [P, XN]), sb("b2", [XN, D])
            sco, top = sb("sco", [P, XN]), sb("top", [P, 8])
            at_i, at_f, iota = sb("at_i", [P, 8], U32), sb("at_f", [P, 8]), sb("iota", [P, XN])
            hit, gT = sb("hit", [P, 2, XN]), sb("gT", [XN, P])
            s_iota, s_gate, s_hit, s_hitT, s_gT, s_mb, s_x1 = (
                sem(n) for n in ("iota", "gvec", "hit", "hitT", "gT", "maskb2", "x1"))
        loads = 16 * (int(norm) + int(gather))
        block = ctx.enter_context(nc.Block())

        @block.sync
        def _(sp):
            if proj:
                sp.dma_start(w[:], a[f"w{layer}"].rearrange("(c p) n -> p c n", p=P)).then_inc(s_w, 16)
                sp.dma_start(bias[:], a[f"bias{layer}"][None, :].to_broadcast([P, 4 * D])).then_inc(s_w, 16)
            else:
                sp.dma_start(wg[:], a["wg"].rearrange("(c p) n -> p c n", p=P)).then_inc(s_w, 16)
                sp.dma_start(bg[:], a["bg"][None, :].to_broadcast([P, XN])).then_inc(s_w, 16)
                sp.dma_start(b2[:], a["b2"]).then_inc(s_w, 16)

            for part_of, lo, hi in ((0, 0, 3), (1, 3, NB)):
                if norm:
                    sp.dma_start(xin[:, lo:hi], blocks(a["x"])[:, lo:hi]).then_inc(s_in[part_of], 16)
                if gather:
                    sp.dma_start(skip[:, lo:hi], blocks(tables["skip"])[:, lo:hi]).then_inc(s_in[part_of], 16)

            def store(j, s):
                sp.wait_ge(s_out, j + 1)
                for t, c0, c1 in (("kv", 0, 2 * D), ("q", 2 * D, 3 * D), ("skip", 3 * D, 4 * D)):
                    sp.dma_start(rows_of(tables[t], j), outs[:, s, c0:c1]).then_inc(s_st[s], 16)

            if proj:
                each(sp, lambda j, s, use: store(j, s))
                sp.wait_ge(s_st[0], 48 * (NB // 2 + 1))
                sp.wait_ge(s_st[1], 48 * (NB // 2))

        @block.gpsimd
        def _(pool):
            if kind == "last":
                nc.gpsimd.iota(iota[:], pattern=[[1, XN]], base=0, channel_multiplier=0,
                               allow_small_or_imprecise_dtypes=True).then_inc(s_iota, 1)
            if gather:
                def step(j, s, use):
                    if later(j):
                        pool.wait_ge(s_z, j - 1)
                    col = slice(j, j + 1) if isinstance(j, int) else ds(j, 1)
                    nc.gpsimd.tensor_copy(idx[:, s, 0:1], k["row_end"][:, col]).then_inc(s_idx, 1)
                    nc.gpsimd.tensor_copy(idx[:, s, 1:2], k["row_before"][:, col]).then_inc(s_idx, 1)
                    wait_alone(pool, s_idx, j * 2 + 2, s_ppassed)
                    for r in range(2):
                        nc.gpsimd.indirect_dma_start(
                            part[:, s, r], None, tables["part"],
                            bass.IndirectOffsetOnAxis(idx[:, s, r:r + 1], 0)).then_inc(s_part[s], 16)
                each(pool, step)

        FRONT = {"first": 3, "middle": 6, "last": 11}[kind]
        BACK = 6

        @block.vector
        def _(v):
            c = Chain(v, s_vec, s_passed)

            def front(j, s, use):
                c.base, c.n = j * FRONT, 0
                if isinstance(j, int) and j == 0:
                    v.wait_ge(s_in[0], loads)
                if later(j):
                    v.wait_ge(s_turn, j - 1)
                src = block_of(xin, j) if norm else None
                if gather:
                    v.wait_ge(s_part[s], use * 32)
                    c.after(nc.vector.tensor_tensor(mx[:], part[:, s, 0, MAXAT:ROW], part[:, s, 1, MAXAT:ROW],
                                                    ALU.max))
                    nc.vector.tensor_tensor(dm[:], part[:, s, :, MAXAT:ROW],
                                            mx[:, None, :].to_broadcast([P, 2, H]), ALU.subtract
                                            ).then_inc(s_dm, 1)
                    v.wait_ge(s_sc, j + 1)
                    c.after(nc.vector.tensor_tensor(
                        scaled[:], part[:, s, :, 0:MAXAT].rearrange("p r (h c) -> p r h c", h=H),
                        sc[:].unsqueeze(3).to_broadcast([P, 2, H, HW]), ALU.mult))
                    c.after(nc.vector.tensor_tensor(scaled[:, 0], scaled[:, 0], scaled[:, 1], ALU.add))
                    c.after(nc.vector.tensor_scalar(den[:], scaled[:, 0, :, C], 1e-16, None, ALU.add))
                    c.after(nc.vector.reciprocal(den[:], den[:]))
                    c.after(nc.vector.tensor_tensor(
                        joined[:].rearrange("p (h c) -> p h c", h=H), scaled[:, 0, :, 0:C],
                        den[:].unsqueeze(2).to_broadcast([P, H, C]), ALU.mult))
                    if kind == "middle":
                        nc.vector.tensor_tensor(z[:, s], joined[:], block_of(skip, j), ALU.add).then_inc(s_z, 1)
                    else:
                        c.after(nc.vector.tensor_tensor(joined[:], joined[:], block_of(skip, j), ALU.add))
                        c.after(nc.vector.tensor_tensor(src, joined[:], src, ALU.add), alone=True)
                if norm:
                    c.after(nc.vector.bn_stats(stats[:], src), alone=True)
                    c.after(nc.vector.bn_aggr(mv[:], stats[:]))
                    nc.vector.tensor_scalar(rs[:], mv[:, 1:2], EPS, None, ALU.add).then_inc(s_var, 1)
                    v.wait_ge(s_std, j + 1)
                    c.after(nc.vector.reciprocal(rs[:], std[:]))
                    nc.vector.tensor_scalar(z[:, s], src, mv[:, 0:1], rs[:, 0:1], ALU.subtract, ALU.mult
                                            ).then_inc(s_z, 1)
                assert c.n == FRONT, c.n

            def back_proj(j, s, use):
                v.wait_ge(s_mm, j + 1)
                if later(j):
                    v.wait_ge(s_st[s], (use - 1) * 48)
                nc.vector.tensor_tensor(outs[:, s], ps_out[:, s].rearrange("p b n -> p (b n)"), bias[:], ALU.add
                                        ).then_inc(s_out, 1)

            def back_gate(j, s, use):
                v.wait_ge(s_mm, j + 1)
                g.base, g.n = j * BACK, 0
                g.after(nc.vector.tensor_tensor(sco[:], ps_out[:, s, 0, 0:XN], bg[:], ALU.add), alone=True)
                g.after(nc.vector.max(top[:], sco[:]), alone=True)
                g.after(nc.vector.max_index(at_i[:], top[:], sco[:]))
                g.after(nc.vector.tensor_copy(at_f[:], at_i[:]))
                g.after(nc.vector.tensor_scalar(hit[:, 0], iota[:], at_f[:, 0:1], None, ALU.is_equal))
                g.after(nc.vector.tensor_scalar(hit[:, 1], iota[:], at_f[:, 1:2], None, ALU.is_equal))
                nc.vector.tensor_tensor(block_of(k["gate"], j), hit[:, 0], hit[:, 1], ALU.add)
                nc.vector.tensor_tensor(hit[:, 0], hit[:, 0], hit[:, 1], ALU.add).then_inc(s_hit, 1)
                v.wait_ge(s_hitT, j + 1)
                nc.vector.tensor_copy(gT[:], ps_out[0:XN, s, 0, P:2 * P]).then_inc(s_gT, 1)
                v.wait_ge(s_mb, j + 1)
                nc.vector.tensor_tensor(block_of(k["x1"], j), block_of(k["x1"], j), ps_out[:, s, 1, 0:D], ALU.add
                                        ).then_inc(s_x1, 1)

            v.wait_ge(s_w, 32 if proj else 48)
            if not proj:
                g = Chain(v, s_gate, s_passed)
                v.wait_ge(s_iota, 1)
            back = back_proj if proj else back_gate
            front(0, 0, 1)
            front(1, 1, 1)
            front(2, 0, 2)
            back(0, 0, 1)
            v.wait_ge(s_in[1], loads)
            front(3, 1, 2)
            back(1, 1, 1)
            with v.Fori(2, (NB - 1) // 2) as it:
                front(it * 2, 0, it + 1)
                back(it * 2 - 2, 0, it)
                front(it * 2 + 1, 1, it + 1)
                back(it * 2 - 1, 1, it)
            front(NB - 1, 0, NB // 2 + 1)
            back(NB - 3, 0, NB // 2)
            back(NB - 2, 1, NB // 2)
            back(NB - 1, 0, NB // 2 + 1)

        @block.scalar
        def _(act):
            def step(j, s, use):
                if gather:
                    act.wait_ge(s_dm, j + 1)
                    nc.scalar.activation(sc[:], dm[:], ACT.Exp, scale=INV).then_inc(s_sc, 1)
                if norm:
                    act.wait_ge(s_var, j + 1)
                    nc.scalar.activation(std[:], rs[:], ACT.Sqrt).then_inc(s_std, 1)
                act.wait_ge(s_turn, j + 1)
                turned = ps_turn[:, s, 0:D].rearrange("p (c n) -> p c n", c=2)
                if kind == "last":
                    nc.scalar.copy(k["xfT"][:, :, ds(j * P, P) if not isinstance(j, int) else slice(j * P, j * P + P)], turned)
                if later(j):
                    act.wait_ge(s_mm, j - 1)
                nc.scalar.activation(zT[:, s], turned, ACT.Relu if kind == "middle" else ACT.Copy
                                     ).then_inc(s_zT, 1)
            each(act, step)

        @block.tensor
        def _(te):
            def turn(j, s):
                te.wait_ge(s_z, j + 1)
                if later(j):
                    te.wait_ge(s_zT, j - 1)
                nc.tensor.transpose(ps_turn[:, s, 0:P], z[:, s, 0:P], k["ident"][:])
                nc.tensor.transpose(ps_turn[:, s, P:D], z[:, s, P:D], k["ident"][:]).then_inc(s_turn, 1)

            def products(j, s):
                te.wait_ge(s_zT, j + 1)
                if later(j):
                    te.wait_ge(s_out if proj else s_x1, j - 1)
                if proj:
                    for b in range(2):
                        for c in range(2):
                            mm = nc.tensor.matmul(ps_out[:, s, b], zT[:, s, c], w[:, c, b * 512:(b + 1) * 512],
                                                  start=(c == 0), stop=(c == 1))
                    mm.then_inc(s_mm, 1)
                else:
                    for c in range(2):
                        mm = nc.tensor.matmul(ps_out[:, s, 0, 0:XN], zT[:, s, c], wg[:, c],
                                              start=(c == 0), stop=(c == 1))
                    mm.then_inc(s_mm, 1)
                    te.wait_ge(s_hit, j + 1)
                    nc.tensor.transpose(ps_out[0:XN, s, 0, P:2 * P], hit[:, 0], k["ident"][:]).then_inc(s_hitT, 1)
                    te.wait_ge(s_gT, j + 1)
                    nc.tensor.matmul(ps_out[:, s, 1, 0:D], gT[:], b2[:], start=True, stop=True).then_inc(s_mb, 1)

            te.wait_ge(s_w, 32 if proj else 48)
            turn(0, 0)
            turn(1, 1)
            products(0, 0)
            turn(2, 0)
            products(1, 1)
            turn(3, 1)
            products(2, 0)
            with te.Fori(1, (NB - 1) // 2 - 1) as it:
                turn(it * 2 + 2, 0)
                products(it * 2 + 1, 1)
                turn(it * 2 + 3, 1)
                products(it * 2 + 2, 0)
            turn(NB - 1, 0)
            products(NB - 2, 1)
            products(NB - 1, 0)


def edge_pass(nc, a, tables, k, layer):
    with ExitStack() as ctx:
        nm = f"e{layer}_"
        sb = lambda name, shape, dt=F32: ctx.enter_context(nc.sbuf_tensor(nm + name, shape, dt))
        sem = lambda name: ctx.enter_context(nc.semaphore(nm + name))
        ps = lambda name, shape: ctx.enter_context(nc.psum_tensor(nm + name, shape, F32))
        ps_e = ps("ps_e", [P, 2, 2, D])
        ps_s = ps("ps_s", [P, 2, 2, 512])
        ps_l, ps_m = ps("ps_l", [P, 512]), ps("ps_m", [P, 512])
        we = sb("we", [P, 2, D])
        ft = sb("ft", [P, 2, 2, G * P])
        si, qi = sb("si", [P, 2, G], I32), sb("qi", [P, 2, G], I32)
        drow = sb("drow", [P, 2, G * P], I32)
        work = sb("work", [P, 2, G, SLOT])
        qg, prod = sb("qg", [P, 2, 2, D]), sb("prod", [P, 2, 2, D])
        lg, mT = sb("lg", [P, 2, H, G]), sb("mT", [4 * G, 2, P])
        diff = sb("diff", [P, H, G])
        seg = sb("seg", [P, 2, 2, P])
        res = sb("res", [P, 2, G, ROW])
        s_w, s_zero, s_e, s_ee, s_prod, s_lg, s_lT, s_scan, s_mT, s_diff, s_w8, s_seg, s_wv, s_sum, s_res, s_max, s_mcol = (
            sem(n) for n in ("weights", "zeroed", "e", "eInSbuf", "prod", "logits", "turned", "scan", "maxT",
                             "diff", "expw", "seg", "weighted", "sums", "res", "maxBack", "maxcol"))
        s_ld = [sem(f"loaded{i}") for i in range(2)]
        s_tpassed, s_ppassed = sem("tpassed"), sem("ppassed")
        s_dr = [sem(f"drow{i}") for i in range(2)]
        s_g = [sem(f"gathered{i}") for i in range(2)]
        s_st = [sem(f"stored{i}") for i in range(2)]
        block = ctx.enter_context(nc.Block())
        LD = 16 * (2 * PAIRS + 3)

        def stages(eng, stage):
            stage(0, 0, 0, True, False)
            stage(1, 1, 0, True, True)
            stage(2, 0, 1, True, True)
            with eng.Fori(1, HALVES // 2 - 1) as i:
                stage(i * 2 + 1, 1, i, True, True)
                stage(i * 2 + 2, 0, i + 1, True, True)
            stage(HALVES - 1, 1, HALVES // 2 - 1, True, True)
            stage(HALVES, 0, HALVES // 2, False, True)

        def stored(par, half2):
            return half2 - 1 if par == 0 else half2

        def has_next(u):
            return not (isinstance(u, int) and u == HALVES - 1)

        def pair_slot(par, p):
            return (PAIRS * par + p) % 2

        def pair_use(par, half2, p):
            return half2 * PAIRS + ((PAIRS * par + p) // 2 + 1)

        @block.sync
        def _(sp):
            w_dram = a[f"we{layer}"]
            sp.wait_ge(s_zero, 2)
            sp.dma_start(we[:, 0], w_dram[0:ED0]).then_inc(s_w, 16)
            sp.dma_start(we[0:ED1, 1], w_dram[ED0:ED]).then_inc(s_w, 16)

            def cols(ap, u, step, lo, n):
                return ap[:, u * step + lo:u * step + lo + n] if isinstance(u, int) else ap[:, ds(u * step + lo, n)]

            def load(u, par, parts):
                for p in parts:
                    lo, n = p * 2 * P, 2 * P
                    src = lambda r0, r1: cols(a["ft"][r0:r1], u, G * P, lo, n)
                    sp.dma_start(ft[:, par, 0, lo:lo + n], src(0, ED0)).then_inc(s_ld[par], 16)
                    sp.dma_start(ft[0:ED1_MANY, par, 1, lo:lo + n], src(ED0, ED0 + ED1_MANY)).then_inc(s_ld[par], 16)
                if 0 in parts:
                    sp.dma_start(ft[ED1_MANY:ED1, par, 1], cols(a["ft"][ED0 + ED1_MANY:ED], u, G * P, 0, G * P)
                                 ).then_inc(s_ld[par], 16)
                    sp.dma_start(si[:, par], cols(a["src_cols"], u, G, 0, G)).then_inc(s_ld[par], 16)
                    sp.dma_start(qi[:, par], cols(a["dst_cols"], u, G, 0, G)).then_inc(s_ld[par], 16)

            def stage(u, par, half2, has_a, has_c):
                if isinstance(u, int) and u == 0:
                    load(0, 0, range(PAIRS))
                if has_c:
                    sp.wait_ge(s_lg, u * PAIRS)
                for p in range(PAIRS):
                    if has_a and has_next(u) and 2 * p < PAIRS:
                        load(u + 1, 1 - par, range(2 * p, min(2 * p + 2, PAIRS)))
                    if has_a and p == 4:
                        if not (isinstance(u, int) and u < 2):
                            sp.wait_ge(s_seg, (u - 1) * PAIRS)
                        row = a["dst"][u * G * P:(u + 1) * G * P] if isinstance(u, int) else a["dst"][
                            ds(u * G * P, G * P)]
                        sp.dma_start(drow[:, par], row[None, :].to_broadcast([P, G * P])).then_inc(s_dr[par], 16)
                    if has_c:
                        sp.wait_ge(s_res, (u - 1) * PAIRS + (p + 1))
                        if p == 0:
                            sp.wait_ge(s_mcol, u)
                        lo, n = (u - 1) * (G * P) + p * 2 * P, 2 * P
                        rows = tables["part"][lo:lo + n] if isinstance(u, int) else tables["part"][ds(lo, n)]
                        sp.dma_start(rows.rearrange("(t p) w -> p t w", p=P), res[:, 1 - par, 2 * p:2 * p + 2]
                                     ).then_inc(s_st[1 - par], 16)

            stages(sp, stage)
            for i in range(2):
                sp.wait_ge(s_st[i], 16 * PAIRS * (HALVES // 2))

        @block.gpsimd
        def _(pool):
            nc.gpsimd.memset(we[:], 0.0).then_inc(s_zero, 1)
            nc.gpsimd.memset(ft[:, :, 1], 0.0).then_inc(s_zero, 1)

            def stage(u, par, half2, has_a, has_c):
                if not has_a:
                    return
                wait_alone(pool, s_ld[par], half2 * LD + LD, s_ppassed)
                for p in range(PAIRS):
                    slot = pair_slot(par, p)
                    pair = u * PAIRS + p
                    if not isinstance(u, int) or pair >= 2:
                        wait_alone(pool, s_prod, pair - 1, s_ppassed)
                    for i in range(2):
                        nc.gpsimd.indirect_dma_start(
                            qg[:, slot, i], None, tables["q"],
                            bass.IndirectOffsetOnAxis(qi[:, par, 2 * p + i:2 * p + i + 1].bitcast(U32), 0)
                        ).then_inc(s_g[slot], 16)
                    wait_alone(pool, s_ee, pair + 1, s_ppassed)
                    for i in range(2):
                        nc.gpsimd.indirect_dma_start(
                            work[:, par, 2 * p + i, KAT:SLOT], None, tables["kv"],
                            bass.IndirectOffsetOnAxis(si[:, par, 2 * p + i:2 * p + i + 1].bitcast(U32), 0),
                            compute_op=ALU.add).then_inc(s_g[slot], 16)

            stages(pool, stage)

        @block.tensor
        def _(te):
            te.wait_ge(s_w, 32)

            def features(u, par, half2, p):
                pair = u * PAIRS + p
                if not isinstance(u, int) or pair >= 2:
                    te.wait_ge(s_ee, pair - 1)
                for i in range(2):
                    t = 2 * p + i
                    for c in range(2):
                        mm = nc.tensor.matmul(ps_e[:, pair_slot(par, p), i], ft[:, par, c, t * P:(t + 1) * P],
                                              we[:, c], start=(c == 0), stop=(c == 1))
                mm.then_inc(s_e, 1)

            def sums(u, par, p):
                pair = (u - 1) * PAIRS + p
                slot = pair_slot(1 - par, p)
                te.wait_ge(s_seg, pair + 1)
                te.wait_ge(s_wv, pair + 1)
                if not isinstance(u, int) or pair >= 2:
                    te.wait_ge(s_res, pair - 1)
                for i in range(2):
                    mm = nc.tensor.matmul(ps_s[:, slot, i, 0:MAXAT], seg[:, slot, i],
                                          work[:, 1 - par, 2 * p + i, 0:MAXAT], start=True, stop=True)
                mm.then_inc(s_sum, 1)

            def stage(u, par, half2, has_a, has_c):
                if isinstance(u, int) and u == 0:
                    te.wait_ge(s_ld[0], LD)
                    features(0, 0, 0, 0)
                    features(0, 0, 0, 1)
                if has_c:
                    wait_alone(te, s_lg, u * PAIRS, s_tpassed)
                    nc.tensor.transpose(ps_l[0:4 * G, 0:P], lg[:, 1 - par].rearrange("p h t -> p (h t)"),
                                        k["ident"][:]).then_inc(s_lT, 1)
                    te.wait_ge(s_mcol, u - 1)
                    wait_alone(te, s_mT, u, s_tpassed)
                    nc.tensor.transpose(ps_m[:, 0:4 * G], mT[:, 1], k["ident"][0:4 * G, 0:4 * G]).then_inc(s_max, 1)
                for p in range(PAIRS):
                    if has_a and p + 2 < PAIRS:
                        features(u, par, half2, p + 2)
                    elif has_a and has_next(u):
                        if p + 2 == PAIRS:
                            te.wait_ge(s_ld[1 - par], (half2 + par) * LD + LD)
                        features(u + 1, 1 - par, half2 + par, p + 2 - PAIRS)
                    if has_c:
                        sums(u, par, p)

            stages(te, stage)

        @block.scalar
        def _(act):
            def copy_e(u, par, p):
                pair = u * PAIRS + p
                act.wait_ge(s_e, pair + 1)
                if not isinstance(u, int) or u >= 2:
                    act.wait_ge(s_sum, pair - 2 * PAIRS + 1)
                nc.scalar.copy(
                    work[:, par, 2 * p:2 * p + 2, KAT:SLOT].rearrange("p t (o d) -> p t o d", o=2),
                    ps_e[:, pair_slot(par, p), :, None, :].to_broadcast([P, 2, 2, D])).then_inc(s_ee, 1)

            def stage(u, par, half2, has_a, has_c):
                if isinstance(u, int) and u == 0:
                    copy_e(0, 0, 0)
                    copy_e(0, 0, 1)
                if has_c:
                    act.wait_ge(s_diff, u)
                    nc.scalar.activation(work[:, 1 - par, :, C:MAXAT:HW], diff[:].rearrange("p h t -> p t h"),
                                         ACT.Exp, scale=INV).then_inc(s_w8, 1)
                for p in range(PAIRS):
                    if has_a and p + 2 < PAIRS:
                        copy_e(u, par, p + 2)
                    elif has_a and has_next(u):
                        copy_e(u + 1, 1 - par, p + 2 - PAIRS)
                    if has_c:
                        pair = (u - 1) * PAIRS + p
                        act.wait_ge(s_sum, pair + 1)
                        if p == 0 and not (isinstance(u, int) and u < 3):
                            act.wait_ge(s_st[1 - par], stored(par, half2) * (16 * PAIRS))
                        nc.scalar.copy(res[:, 1 - par, 2 * p:2 * p + 2, 0:MAXAT],
                                       ps_s[:, pair_slot(1 - par, p), :, 0:MAXAT]).then_inc(s_res, 1)

            stages(act, stage)

        @block.vector
        def _(v):
            def logits(u, par, p):
                pair = u * PAIRS + p
                slot = pair_slot(par, p)
                v.wait_ge(s_prod, pair + 1)
                nc.vector.tensor_reduce(lg[:, par, :, 2 * p:2 * p + 2].rearrange("p h t -> p t h"),
                                        prod[:, slot].rearrange("p t (h c) -> p t h c", h=H), AX.X, ALU.add
                                        ).then_inc(s_lg, 1)

            def product(u, par, half2, p):
                slot = pair_slot(par, p)
                v.wait_ge(s_g[slot], pair_use(par, half2, p) * 64)
                if not isinstance(u, int) or u * PAIRS + p >= 2:
                    v.wait_ge(s_lg, u * PAIRS + p - 1)
                nc.vector.tensor_tensor(prod[:, slot], work[:, par, 2 * p:2 * p + 2, KAT:VAT], qg[:, slot], ALU.mult
                                        ).then_inc(s_prod, 1)

            def maxima(u, par, half2):
                half = slice(u - 1, u) if isinstance(u, int) else ds(u - 1, 1)
                new_f = k["new_fwd"][:, half].rearrange("p o e -> p (o e)")
                new_b = k["new_bwd"][:, half].rearrange("p o e -> p (o e)")
                v.wait_ge(s_lT, u)
                nc.vector.tensor_tensor_scan(mT[:, 0, ::-1], new_f, ps_l[0:4 * G, 0:P], LOW, ALU.add, ALU.max
                                             ).then_inc(s_scan, 1)
                v.wait_ge(s_scan, u)
                nc.vector.tensor_tensor_scan(mT[:, 1, ::-1], new_b, mT[:, 0], LOW, ALU.add, ALU.max
                                             ).then_inc(s_mT, 1)
                v.wait_ge(s_max, u)
                col = ps_m[:, 0:4 * G].rearrange("p (h t) -> p h t", h=H)
                nc.vector.tensor_tensor(diff[:], lg[:, 1 - par], col, ALU.subtract).then_inc(s_diff, 1)
                if not (isinstance(u, int) and u < 3):
                    v.wait_ge(s_st[1 - par], stored(par, half2) * (16 * PAIRS))
                nc.vector.tensor_copy(res[:, 1 - par, :, MAXAT:ROW], col.rearrange("p h t -> p t h")
                                      ).then_inc(s_mcol, 1)

            def weigh(u, par, p):
                pair = (u - 1) * PAIRS + p
                slot = pair_slot(1 - par, p)
                n = (u - 1) * G + 2 * p
                own = k["dst_col"][:, n:n + 2] if isinstance(u, int) else k["dst_col"][:, ds(n, 2)]
                if not isinstance(u, int) or pair >= 2:
                    v.wait_ge(s_sum, pair - 1)
                nc.vector.tensor_tensor(
                    seg[:, slot], drow[:, 1 - par, 2 * p * P:(2 * p + 2) * P].rearrange("p (t e) -> p t e", t=2),
                    own.unsqueeze(2).to_broadcast([P, 2, P]), ALU.is_equal).then_inc(s_seg, 1)
                rows = work[:, 1 - par, 2 * p:2 * p + 2, 0:MAXAT].rearrange("p t (h c) -> p t h c", h=H)
                nc.vector.tensor_tensor(
                    rows[:, :, :, 0:C], work[:, 1 - par, 2 * p:2 * p + 2, VAT:SLOT].rearrange(
                        "p t (h c) -> p t h c", h=H),
                    rows[:, :, :, C:HW].to_broadcast([P, 2, H, C]), ALU.mult).then_inc(s_wv, 1)

            def stage(u, par, half2, has_a, has_c):
                if has_c:
                    maxima(u, par, half2)
                    v.wait_ge(s_w8, u)
                    v.wait_ge(s_dr[1 - par], dr_use(par, half2) * 16)
                for p in range(PAIRS):
                    if has_c:
                        weigh(u, par, p)
                    if has_a:
                        product(u, par, half2, p)
                        if p >= 1:
                            logits(u, par, p - 1)
                if has_a:
                    logits(u, par, PAIRS - 1)

            def dr_use(par, half2):
                return half2 if par == 0 else half2 + 1

            stages(v, stage)


def chain_pass(nc, a, tables, k, layer):
    with ExitStack() as ctx:
        nm = f"c{layer}_"
        sb = lambda name, shape, dt=F32: ctx.enter_context(nc.sbuf_tensor(nm + name, shape, dt))
        sem = lambda name: ctx.enter_context(nc.semaphore(nm + name))
        ps = lambda name, shape: ctx.enter_context(nc.psum_tensor(nm + name, shape, F32))
        last = sb("last", [CR, CH, ROW])
        run = sb("run", [H, T])
        wgt = sb("wgt", [CR, H, CH, T])
        out = sb("out", [CR, CH, ROW])
        ps_t, ps_r = ps("ps_t", [P, 512]), ps("ps_r", [P, 512])
        ps_b, ps_o = ps("ps_b", [P, 2, 512]), ps("ps_o", [P, 2, 512])
        s_in, s_t, s_run, s_b, s_r, s_arg, s_exp, s_wgt, s_o, s_out, s_m, s_st = (
            sem(n) for n in ("in", "turned", "run", "spread", "back", "arg", "exp", "wgt", "sums", "out", "m", "st"))
        block = ctx.enter_context(nc.Block())

        @block.sync
        def _(sp):
            rows = tables["part"][0:EDGES].rearrange("(c r p) w -> p r c w", c=CH, p=P)
            sp.dma_start(last[:], rows[P - 1]).then_inc(s_in, 16)
            sp.wait_ge(s_out, CH)
            sp.wait_ge(s_m, 1)
            sp.dma_start(tables["part"][NULL + 1:NULL + 1 + T].rearrange("(c r) w -> r c w", c=CH), out[:]
                         ).then_inc(s_st, 16)
            sp.wait_ge(s_st, 16)

        @block.tensor
        def _(te):
            te.wait_ge(s_in, 16)
            for c in range(CH):
                tr = nc.tensor.transpose(ps_t[0:H, c * CR:(c + 1) * CR], last[:, c, MAXAT:ROW],
                                         k["ident"][0:CR, 0:CR])
            tr.then_inc(s_t, 1)
            te.wait_ge(s_run, 1)
            for c in range(CH):
                tr = nc.tensor.transpose(ps_r[0:CR, c * H:(c + 1) * H], run[:, c * CR:(c + 1) * CR],
                                         k["ident"][0:H, 0:H])
            tr.then_inc(s_r, 1)
            for h in range(H):
                if h >= 2:
                    te.wait_ge(s_arg, h - 1)
                nc.tensor.matmul(ps_b[0:CR, h % 2, 0:T], k["head_row"][:, h], run[:], start=True, stop=True
                                 ).then_inc(s_b, 1)
            te.wait_ge(s_wgt, H)
            for c in range(CH):
                if c >= 2:
                    te.wait_ge(s_out, c - 1)
                for h in range(H):
                    for e in range(c + 1):
                        mm = nc.tensor.matmul(ps_o[0:CR, c % 2, h * HW:(h + 1) * HW],
                                              wgt[:, h, e, c * CR:(c + 1) * CR],
                                              last[:, e, h * HW:(h + 1) * HW], start=(e == 0), stop=(e == c))
                mm.then_inc(s_o, 1)

        @block.vector
        def _(v):
            v.wait_ge(s_t, 1)
            nc.vector.tensor_tensor_scan(run[:], k["chain_new"][:], ps_t[0:H, 0:T], LOW, ALU.add, ALU.max
                                         ).then_inc(s_run, 1)
            v.wait_ge(s_r, 1)
            nc.vector.tensor_copy(out[:, :, MAXAT:ROW], ps_r[0:CR, 0:CH * H].rearrange("p (c h) -> p c h", c=CH)
                                  ).then_inc(s_m, 1)

            def mask(h):
                v.wait_ge(s_exp, h + 1)
                nc.vector.tensor_tensor(wgt[:, h], wgt[:, h], k["chain_mask"][:], ALU.mult).then_inc(s_wgt, 1)

            for h in range(H):
                v.wait_ge(s_b, h + 1)
                for e in range(CH):
                    ins = nc.vector.tensor_scalar(wgt[:, h, e], ps_b[0:CR, h % 2, 0:T],
                                                  last[:, e, MAXAT + h:MAXAT + h + 1], 0.0,
                                                  ALU.subtract, ALU.max)
                ins.then_inc(s_arg, 1)
                if h:
                    mask(h - 1)
            mask(H - 1)

        @block.scalar
        def _(act):
            for h in range(H):
                act.wait_ge(s_arg, h + 1)
                nc.scalar.activation(wgt[:, h], wgt[:, h], ACT.Exp, scale=-INV).then_inc(s_exp, 1)
            for c in range(CH):
                act.wait_ge(s_o, c + 1)
                nc.scalar.copy(out[:, c, 0:MAXAT], ps_o[0:CR, c % 2, 0:MAXAT]).then_inc(s_out, 1)


def experts(nc, a, k):
    with ExitStack() as ctx:
        sb = lambda name, shape, dt=F32: ctx.enter_context(nc.sbuf_tensor("x_" + name, shape, dt))
        sem = lambda name: ctx.enter_context(nc.semaphore("x_" + name))
        ps = lambda name, shape: ctx.enter_context(nc.psum_tensor("x_" + name, shape, F32))
        w1, w2 = sb("w1", [P, 2, 2, XH]), sb("w2", [P, 2, HC, XD])
        b1 = sb("b1", [P, XN * HC])
        hid = sb("hid", [P, 2, HC, GN])
        ps_h, ps_y = ps("ps_h", [P, 2, 2, 512]), ps("ps_y", [P, 2, 512])
        s_b1, s_h, s_hid, s_y, s_acc, s_out = (sem(n) for n in ("b1", "h", "hid", "y", "acc", "out"))
        s_wt = [sem(f"w{i}") for i in range(2)]
        groups = NB // GT
        hn = GN // 2
        block = ctx.enter_context(nc.Block())

        def turns(eng, turn):
            for n in range(2):
                turn(n, n, 0, 0, n)
            with eng.Fori(1, XN // 2) as i:
                for s in range(2):
                    turn(i * 2 + s, s, i, 0, i * 2 + s)
            with eng.Fori(1, groups) as g:
                with eng.Fori(0, XN // 2) as i:
                    for s in range(2):
                        turn(g * XN + i * 2 + s, s, g * (XN // 2) + i, g, i * 2 + s)

        @block.sync
        def _(sp):
            sp.dma_start(b1[:], a["b1_cols"]).then_inc(s_b1, 16)

            def turn(n, s, use, g, e):
                if not isinstance(n, int):
                    sp.wait_ge(s_y, n * GT - GT)
                one = (lambda ap: ap[e]) if isinstance(e, int) else (
                    lambda ap: ap[ds(e, 1)].rearrange("o r c -> (o r) c"))
                sp.dma_start(w1[:, s], one(a["w1x"]).rearrange("(c p) h -> p c h", p=P)).then_inc(s_wt[s], 16)
                sp.dma_start(w2[:, s], one(a["w2x"]).rearrange("(c p) d -> p c d", p=P)).then_inc(s_wt[s], 16)
            turns(sp, turn)
            sp.wait_ge(s_acc, groups * XN * GT)
            full = N // P
            sp.dma_start(a["out"][0:full * P].rearrange("(b p) d -> p b d", p=P), k["x1"][:, 0:full]
                         ).then_inc(s_out, 16)
            sp.dma_start(a["out"][full * P:N], k["x1"][0:N - full * P, full]).then_inc(s_out, 16)
            sp.wait_ge(s_out, 32)

        @block.tensor
        def _(te):
            def turn(n, s, use, g, e):
                te.wait_ge(s_wt[s], use * 32 + 32)
                for hc in range(HC):
                    if not isinstance(n, int) or n * HC + hc >= 2:
                        te.wait_ge(s_hid, n * HC + hc - 1)
                    for half in range(2):
                        for c in range(2):
                            cols = slice(half * hn, half * hn + hn) if isinstance(g, int) else ds(g * GN + half * hn, hn)
                            mm = nc.tensor.matmul(ps_h[:, hc % 2, half, 0:hn], w1[:, s, c, hc * P:(hc + 1) * P],
                                                  k["xfT"][:, c, cols], start=(c == 0), stop=(c == 1))
                    mm.then_inc(s_h, 1)
                te.wait_ge(s_hid, n * HC + HC)
                for b in range(GT):
                    slot = (s * GT + b) % 2
                    if not isinstance(n, int) or n * GT + b >= 2:
                        te.wait_ge(s_acc, n * GT + b - 1)
                    for hc in range(HC):
                        mm = nc.tensor.matmul(ps_y[:, slot, 0:XD], hid[:, s, hc, b * P:(b + 1) * P], w2[:, s, hc],
                                              start=(hc == 0), stop=(hc == HC - 1))
                    mm.then_inc(s_y, 1)
            turns(te, turn)

        @block.scalar
        def _(act):
            act.wait_ge(s_b1, 16)

            def turn(n, s, use, g, e):
                for hc in range(HC):
                    act.wait_ge(s_h, n * HC + hc + 1)
                    if hc == 0 and not isinstance(n, int):
                        act.wait_ge(s_y, n * GT - GT)
                    col = slice(e * HC + hc, e * HC + hc + 1) if isinstance(e, int) else ds(e * HC + hc, 1)
                    nc.scalar.activation(hid[:, s, hc].rearrange("p (o n) -> p o n", o=2), ps_h[:, hc % 2, :, 0:hn],
                                         ACT.Gelu, bias=b1[:, col]).then_inc(s_hid, 1)
            turns(act, turn)

        @block.vector
        def _(v):
            def turn(n, s, use, g, e):
                for b in range(GT):
                    v.wait_ge(s_y, n * GT + b + 1)
                    blk = g * GT + b
                    x1 = block_of(k["x1"], blk)
                    m = block_of(k["gate"], blk)
                    if not isinstance(n, int) or n > 0:
                        v.wait_ge(s_acc, n * GT + b - GT + 1)
                    m = m[:, e:e + 1] if isinstance(e, int) else m[:, ds(e, 1)]
                    nc.vector.scalar_tensor_tensor(out=x1, in0=ps_y[:, (s * GT + b) % 2, 0:XD], scalar=m, in1=x1,
                                                   op0=ALU.mult, op1=ALU.add).then_inc(s_acc, 1)
            turns(v, turn)


def kernel(x, src, dst, edge_attr_194, **w):
    import concourse.bacc as bacc
    from concourse.bass_utils import run_bass_kernel_spmd

    g, f = (lambda n: np.asarray(w["L0_gnn_" + n])), (lambda n: np.asarray(w["L0_ffn_" + n]))
    x, src, dst, attr = (np.asarray(v) for v in (x, src, dst, edge_attr_194))
    src_p = np.concatenate([src, np.zeros(EDGES - E_REAL, src.dtype)])
    dst_p = np.concatenate([dst, np.full(EDGES - E_REAL, NP - 1, dst.dtype)])
    arrays = {
        "x": np.pad(x, ((0, NP - N), (0, 0))),
        "dst": dst_p,
        "dst_last": dst_p[P - 1::P],
        "dst_last_cols": dst_p[P - 1::P].reshape(CH, CR).T,
        "src_cols": src_p.reshape(T, P).T,
        "dst_cols": dst_p.reshape(T, P).T,
        "ft": np.pad(attr.T, ((0, 0), (0, EDGES - E_REAL))),
        "wg": f("Wg"), "bg": f("bg"), "b2": f("b2"), "w1x": f("W1"), "w2x": f("W2"),
        "b1_cols": f("b1").reshape(XN * HC, P).T,
    }
    for l in (1, 2):
        arrays[f"w{l}"] = np.concatenate([g(f"W{m}{l}") for m in "kvqs"], axis=1)
        arrays[f"bias{l}"] = np.concatenate([g(f"b{m}{l}") for m in "kvqs"])
        arrays[f"we{l}"] = g(f"We{l}")
    nc = bacc.Bacc("TRN2", target_bir_lowering=False, num_devices=1)
    arrays = {"in_" + n: np.ascontiguousarray(v) for n, v in arrays.items()}
    aps = {n[3:]: nc.dram_tensor(n, v.shape, mybir.dt.from_np(v.dtype), kind="ExternalInput").ap()
           for n, v in arrays.items()}
    aps["out"] = nc.dram_tensor("out", (N, D), F32, kind="ExternalOutput").ap()
    kernel_program(nc, aps)
    r = run_bass_kernel_spmd(nc, [arrays], core_ids=[0])
    return r.results[0]["out"]
```

```python
from contextlib import ExitStack

import numpy as np

import concourse.bass as bass
from concourse import mybir
from concourse.alu_op_type import AluOpType as ALU

P = 128
N, D, H, C = 3125, 256, 4, 64
NB = -(-N // P)
NP = NB * P
E_REAL, ED = 50000, 194
G = 14
PAIRS = G // 2
T = 392
HALVES = T // G
EDGES = T * P
ED0, ED1 = P, ED - P
ED1_MANY = 64
HW = C + 1
ROW = H * HW + H
MAXAT = H * HW
SLOT = 4 + 2 * D
KAT, VAT = 4, 4 + D
NULL = EDGES
CH, CR = 4, T // 4
XN, XH = 8, 512
HC = XH // P
TX = (2 * NP + XN * (P - 1)) // P
HUGE = 3e38
LOW = -1e30
INV = 1.0 / 8.0
EPS = 1e-5

ACT = mybir.ActivationFunctionType
AX = mybir.AxisListType
F32 = mybir.dt.float32
BF16 = mybir.dt.bfloat16
I32 = mybir.dt.int32
U32 = mybir.dt.uint32
ds = bass.ds


class Chain:

    def __init__(self, eng, sem, passed=None):
        self.eng, self.sem, self.passed, self.base, self.n = eng, sem, passed, 0, 0

    def after(self, ins, alone=False):
        ins.then_inc(self.sem, 1)
        self.n += 1
        if alone:
            wait_alone(self.eng, self.sem, self.base + self.n, self.passed)
        else:
            self.eng.wait_ge(self.sem, self.base + self.n)


def wait_alone(eng, sem, value, passed):
    eng.wait_ge(sem, value)
    eng.sem_inc(passed, 1)


def kernel_program(nc, a):
    with ExitStack() as ctx:
        dram = lambda name, shape: nc.dram_tensor(name, shape, F32, kind="Internal").ap()
        tables = {"kv": dram("kv_table", (NP, 2 * D)), "q": dram("q_table", (NP, D)),
                  "skip": dram("skip_table", (NP, D)), "part": dram("partials", (EDGES + 1 + T, ROW))}
        tables.update(z=dram("z_table", (NP + P, D)), acc=dram("acc_table", (NP + P, D)))
        keep = lambda name, shape, dt=F32: ctx.enter_context(nc.sbuf_tensor(name, shape, dt))
        graph = ctx.enter_context(ExitStack())
        k = {"ident": keep("ident", [P, P]), "tri": keep("tri", [P, P]), "ones": keep("ones", [P, P]),
             "rows": keep("rows", [P, NB, 2], U32)}
        keep = lambda name, shape, dt=F32: graph.enter_context(nc.sbuf_tensor(name, shape, dt))
        k.update({
            "dst_col": keep("dst_col", [P, T]),
            "new_fwd": keep("new_fwd", [4 * G, HALVES, P]),
            "new_bwd": keep("new_bwd", [4 * G, HALVES, P]),
            "chain_mask": keep("chain_mask", [CR, CH, T]),
            "chain_new": keep("chain_new", [H, T]),
            "head_row": keep("head_row", [H, H, CR]),
        })
        setup(nc, a, tables, k)
        node_blocks(nc, a, tables, k, "first")
        for layer in (1, 2):
            edge_pass(nc, a, tables, k, layer)
            chain_pass(nc, a, tables, k, layer)
            if layer == 1:
                node_blocks(nc, a, tables, k, "middle")
        graph.close()
        keep = lambda name, shape, dt=F32: ctx.enter_context(nc.sbuf_tensor(name, shape, dt))
        k.update(w1=keep("w1", [P, XN, 2, XH]), w2=keep("w2", [P, XN, HC, D]), b1=keep("b1", [P, XN, XH]),
                 b2=keep("b2", [P, XN, D]), scores=keep("scores", [P, NB, XN]),
                 perm=keep("perm", [P, TX], U32), expert=keep("expert", [1, TX], I32))
        last_blocks(nc, a, tables, k)
        route(nc, k)
        experts(nc, a, tables, k)


def semaphores(nc, ctx, prefix):
    mine = []

    def clear():
        nc.clear_and_free_semaphores(mine)
        nc.all_engine_barrier()
    ctx.callback(clear)

    def sem(name):
        mine.append(nc.alloc_semaphore(prefix + name))
        return mine[-1]
    return sem


def setup(nc, a, tables, k):
    with ExitStack() as ctx:
        sb = lambda name, shape, dt=F32: ctx.enter_context(nc.sbuf_tensor("su_" + name, shape, dt))
        sem = lambda name: ctx.enter_context(nc.semaphore("su_" + name))
        dcol = sb("dcol", [P, T], I32)
        drow = sb("drow", [4 * G, HALVES, P], I32)
        node_i, node = sb("node_i", [P, NB], I32), sb("node", [P, NB])
        ends, ended = sb("ends", [P, T]), sb("ended", [P, NB, T])
        tile, tile_u = sb("tile", [P, NB]), sb("tile_u", [P, NB], U32)
        inside, upto = sb("inside", [P, NB, P], I32), sb("upto", [P, NB, P])
        part = sb("part", [P, NB])
        down, wrap = sb("down", [P, P]), sb("wrap", [P, P])
        cum = sb("cum", [P, NB + 1])
        cnt, g1, t1, t2 = sb("cnt", [P, NB]), sb("g1", [P, NB]), sb("t1", [P, NB]), sb("t2", [P, NB])
        ti, tf = sb("ti", [P, NB], I32), sb("tf", [P, NB])
        null = sb("null", [1, ROW])
        dlb, dlc = sb("dlb", [P, T], I32), sb("dlc", [CR, CH], I32)
        same = sb("same", [CR, CH, T])
        ps = ctx.enter_context(nc.psum_tensor("su_ps", [P, 512], F32))
        s_in, s_pool, s_v, s_tile, s_rows, s_cum, s_prev, s_null, s_nulled = (
            sem(n) for n in ("loaded", "pool", "vec", "tile", "rows", "cum", "prev", "null", "nulled"))
        s_last = sem("lastLoaded")
        block = ctx.enter_context(nc.Block())

        @block.sync
        def _(sp):
            sp.dma_start(dlb[:], a["dst_last"][None, :].to_broadcast([P, T])).then_inc(s_last, 16)
            for h in range(H):
                sp.dma_start(drow[h * G:(h + 1) * G], a["dst"].rearrange("(u t e) -> t u e", t=G, e=P)
                             ).then_inc(s_in, 16)
            sp.dma_start(dlc[:], a["dst_last_cols"]).then_inc(s_in, 16)
            sp.dma_start(dcol[:], a["dst_cols"]).then_inc(s_in, 16)
            sp.wait_ge(s_null, 2)
            sp.dma_start(tables["part"][NULL:NULL + 1], null[:]).then_inc(s_nulled, 16)
            sp.wait_ge(s_nulled, 16)

        @block.gpsimd
        def _(pool):
            c = Chain(pool, s_pool)
            c.after(nc.gpsimd.iota(node_i[:], pattern=[[P, NB]], base=0, channel_multiplier=1,
                                   allow_small_or_imprecise_dtypes=True))
            c.after(nc.gpsimd.memset(k["ident"][:], 0.0))
            c.after(nc.gpsimd.affine_select(out=k["ident"][:], in_=k["ident"][:], compare_op=ALU.not_equal,
                                            fill=1.0, base=0, pattern=[[-1, P]], channel_multiplier=1))
            c.after(nc.gpsimd.memset(k["ones"][:], 1.0))
            c.after(nc.gpsimd.affine_select(out=k["tri"][:], in_=k["ones"][:], compare_op=ALU.is_ge, fill=0.0,
                                            base=0, pattern=[[1, P]], channel_multiplier=-1))
            c.after(nc.gpsimd.memset(down[:], 0.0))
            c.after(nc.gpsimd.affine_select(out=down[:], in_=down[:], compare_op=ALU.not_equal, fill=1.0,
                                            base=1, pattern=[[-1, P]], channel_multiplier=1))
            c.after(nc.gpsimd.memset(wrap[:], 0.0))
            c.after(nc.gpsimd.affine_select(out=wrap[:], in_=wrap[:], compare_op=ALU.not_equal, fill=1.0,
                                            base=-(P - 1), pattern=[[-1, P]], channel_multiplier=1))
            c.after(nc.gpsimd.memset(k["chain_mask"][:], 1.0))
            c.after(nc.gpsimd.affine_select(out=k["chain_mask"][:], in_=k["chain_mask"][:],
                                            compare_op=ALU.is_ge, fill=0.0, base=0,
                                            pattern=[[-CR, CH], [1, T]], channel_multiplier=-1))
            c.after(nc.gpsimd.memset(k["head_row"][:], 0.0))
            c.after(nc.gpsimd.affine_select(out=k["head_row"][:], in_=k["head_row"][:], compare_op=ALU.not_equal,
                                            fill=1.0, base=0, pattern=[[-1, H], [0, CR]], channel_multiplier=1))
            assert c.n == 13
            pool.wait_ge(s_tile, 1)
            for b in range(NB):
                nc.gpsimd.indirect_dma_start(inside[:, b], None, a["dst"].rearrange("(t e) -> t e", e=P),
                                             bass.IndirectOffsetOnAxis(tile_u[:, b:b + 1], 0)).then_inc(s_rows, 16)

        @block.vector
        def _(v):
            c = Chain(v, s_v)
            nc.vector.memset(null[:, 0:MAXAT], 0.0).then_inc(s_null, 1)
            nc.vector.memset(null[:, MAXAT:ROW], LOW).then_inc(s_null, 1)
            c.after(nc.vector.memset(cum[:, 0:1], 0.0))
            v.wait_ge(s_last, 16)
            v.wait_ge(s_pool, 1)
            c.after(nc.vector.tensor_copy(ends[:], dlb[:]))
            c.after(nc.vector.tensor_copy(node[:], node_i[:]))
            for b in range(NB):
                ins = nc.vector.tensor_scalar(ended[:, b], ends[:], node[:, b:b + 1], None, ALU.is_le)
            c.after(ins)
            c.after(nc.vector.tensor_reduce(tile[:], ended[:], AX.X, ALU.add))
            c.after(nc.vector.tensor_scalar(tile[:], tile[:], float(T - 1), None, ALU.min))
            nc.vector.tensor_copy(tile_u[:], tile[:]).then_inc(s_tile, 1)
            v.wait_ge(s_in, 16 * 6)
            c.after(nc.vector.tensor_copy(k["dst_col"][:], dcol[:]))
            nc.vector.memset(k["new_fwd"][:, :, 0:1], 0.0)
            nc.vector.memset(k["new_bwd"][:, :, 0:1], 0.0)
            c.after(nc.vector.tensor_tensor(k["new_fwd"][:, :, 1:P], drow[:, :, 1:P], drow[:, :, 0:P - 1],
                                            ALU.not_equal))
            c.after(nc.vector.tensor_scalar(k["new_fwd"][:, :, 1:P], k["new_fwd"][:, :, 1:P], LOW, None, ALU.mult))
            c.after(nc.vector.tensor_copy(k["new_bwd"][:, :, 1:P], k["new_fwd"][:, :, P - 1:0:-1]))
            v.wait_ge(s_pool, 13)
            c.after(nc.vector.tensor_tensor(same[:], dlb[0:CR, None, :].to_broadcast([CR, CH, T]),
                                            dlc[:].unsqueeze(2).to_broadcast([CR, CH, T]), ALU.is_equal))
            c.after(nc.vector.tensor_tensor(k["chain_mask"][:], k["chain_mask"][:], same[:], ALU.mult))
            nc.vector.memset(k["chain_new"][:, 0:1], 0.0)
            c.after(nc.vector.tensor_tensor(k["chain_new"][:, 1:T], dlb[0:H, 1:T], dlb[0:H, 0:T - 1],
                                            ALU.not_equal))
            c.after(nc.vector.tensor_scalar(k["chain_new"][:, 1:T], k["chain_new"][:, 1:T], LOW, None, ALU.mult))
            v.wait_ge(s_rows, 16 * NB)
            c.after(nc.vector.tensor_tensor(upto[:], inside[:], node_i[:].unsqueeze(2).to_broadcast([P, NB, P]),
                                            ALU.is_le))
            c.after(nc.vector.tensor_reduce(part[:], upto[:], AX.X, ALU.add))
            nc.vector.scalar_tensor_tensor(out=cum[:, 1:NB + 1], in0=tile[:], scalar=float(P), in1=part[:],
                                           op0=ALU.mult, op1=ALU.add).then_inc(s_cum, 1)
            v.wait_ge(s_prev, 1)
            c.after(nc.vector.tensor_tensor(cnt[:], cum[:, 1:NB + 1], ps[:, 0:NB], ALU.subtract))
            c.after(nc.vector.tensor_scalar(g1[:], cnt[:], 0.0, None, ALU.is_gt))
            c.after(nc.vector.tensor_scalar(t1[:], cum[:, 1:NB + 1], -1.0, None, ALU.add))
            c.after(nc.vector.tensor_scalar(t1[:], t1[:], -float(NULL), None, ALU.add))
            c.after(nc.vector.tensor_tensor(t1[:], t1[:], g1[:], ALU.mult))
            c.after(nc.vector.tensor_scalar(t1[:], t1[:], float(NULL), None, ALU.add))
            c.after(nc.vector.tensor_copy(k["rows"][:, :, 0], t1[:]))
            c.after(nc.vector.tensor_scalar(t2[:], cum[:, 1:NB + 1], -1.0, 0.0, ALU.add, ALU.max))
            c.after(nc.vector.tensor_copy(ti[:], t2[:]))
            c.after(nc.vector.tensor_single_scalar(ti[:], ti[:], 7, ALU.arith_shift_right))
            c.after(nc.vector.tensor_copy(tf[:], ti[:]))
            c.after(nc.vector.scalar_tensor_tensor(out=t2[:], in0=tf[:], scalar=float(P), in1=ps[:, 0:NB],
                                                   op0=ALU.mult, op1=ALU.is_gt))
            c.after(nc.vector.tensor_tensor(t2[:], t2[:], g1[:], ALU.mult))
            c.after(nc.vector.tensor_tensor(t2[:], t2[:], tf[:], ALU.mult))
            c.after(nc.vector.tensor_scalar(t2[:], t2[:], float(NULL), None, ALU.add))
            c.after(nc.vector.tensor_copy(k["rows"][:, :, 1], t2[:]))

        @block.tensor
        def _(te):
            te.wait_ge(s_cum, 1)
            te.wait_ge(s_pool, 13)
            nc.tensor.matmul(ps[:, 0:NB], down[:], cum[:, 1:NB + 1], start=True, stop=False)
            nc.tensor.matmul(ps[:, 0:NB], wrap[:], cum[:, 0:NB], start=False, stop=True).then_inc(s_prev, 1)


def each(eng, step, n=NB, ring=2):
    for j in range(ring + 1):
        step(j, j % ring, j // ring + 1)
    with eng.Fori(1, (n - 1) // ring - 1) as it:
        for i in range(ring):
            step(it * ring + (1 + i), (1 + i) % ring, it + ((1 + i) // ring + 1))
    for j in range(n - ring, n):
        step(j, j % ring, j // ring + 1)


def later(j, ring=2):
    return not isinstance(j, int) or j >= ring


def block_of(ap, j):
    if isinstance(j, int):
        return ap[:, j]
    return ap[:, ds(j, 1)].rearrange("p o d -> p (o d)")


def blocks(table):
    return table.rearrange("(b p) d -> p b d", p=P)


def rows_of(table, j):
    return table[ds(j * P, P)] if not isinstance(j, int) else table[j * P:(j + 1) * P]


def node_blocks(nc, a, tables, k, kind):
    gather, norm = kind == "middle", kind == "first"
    layer = 1 if kind == "first" else 2
    with ExitStack() as ctx:
        sb = lambda name, shape, dt=F32: ctx.enter_context(nc.sbuf_tensor(kind + "_" + name, shape, dt))
        sem = lambda name: ctx.enter_context(nc.semaphore(kind + "_" + name))
        ps_turn = ctx.enter_context(nc.psum_tensor(kind + "_turn", [P, 2, 512], F32))
        ps_out = ctx.enter_context(nc.psum_tensor(kind + "_out", [P, 2, 2, 512], F32))
        z, zT = sb("z", [P, 2, D]), sb("zT", [P, 2, 2, P])
        s_w, s_vec, s_z, s_turn, s_zT, s_mm, s_out = (
            sem(n) for n in ("weights", "vec", "z", "turned", "zT", "products", "outs"))
        s_in = [sem(f"in{i}") for i in range(2)]
        s_passed, s_ppassed = sem("passed"), sem("ppassed")
        if gather:
            skip, part = sb("skip", [P, NB, D]), sb("part", [P, 2, 2, ROW])
            idx = sb("idx", [P, 2, 2], U32)
            mx, dm, sc = sb("mx", [P, H]), sb("dm", [P, 2, H]), sb("sc", [P, 2, H])
            scaled, den = sb("scaled", [P, 2, H, HW]), sb("den", [P, H])
            joined = sb("joined", [P, D])
            s_idx, s_dm, s_sc = sem("idx"), sem("dm"), sem("sc")
            s_part = [sem(f"part{i}") for i in range(2)]
        if norm:
            xin = sb("x", [P, NB, D])
            stats, mv, rs, std = sb("stats", [P, 6]), sb("mv", [P, 2]), sb("rs", [P, 1]), sb("std", [P, 1])
            s_var, s_std = sem("var"), sem("std")
        w, bias = sb("w", [P, 2, 4 * D]), sb("bias", [P, 4 * D])
        outs = sb("outs", [P, 2, 4 * D])
        s_st = [sem(f"stored{i}") for i in range(2)]
        loads = 16 * (int(norm) + int(gather))
        block = ctx.enter_context(nc.Block())

        @block.sync
        def _(sp):
            sp.dma_start(w[:], a[f"w{layer}"].rearrange("(c p) n -> p c n", p=P)).then_inc(s_w, 16)
            sp.dma_start(bias[:], a[f"bias{layer}"][None, :].to_broadcast([P, 4 * D])).then_inc(s_w, 16)

            for part_of, lo, hi in ((0, 0, 3), (1, 3, NB)):
                if norm:
                    sp.dma_start(xin[:, lo:hi], blocks(a["x"])[:, lo:hi]).then_inc(s_in[part_of], 16)
                if gather:
                    sp.dma_start(skip[:, lo:hi], blocks(tables["skip"])[:, lo:hi]).then_inc(s_in[part_of], 16)

            def store(j, s):
                sp.wait_ge(s_out, j + 1)
                for t, c0, c1 in (("kv", 0, 2 * D), ("q", 2 * D, 3 * D), ("skip", 3 * D, 4 * D)):
                    sp.dma_start(rows_of(tables[t], j), outs[:, s, c0:c1]).then_inc(s_st[s], 16)

            each(sp, lambda j, s, use: store(j, s))
            sp.wait_ge(s_st[0], 48 * (NB // 2 + 1))
            sp.wait_ge(s_st[1], 48 * (NB // 2))

        @block.gpsimd
        def _(pool):
            if gather:
                def step(j, s, use):
                    if later(j):
                        pool.wait_ge(s_z, j - 1)
                    col = slice(j, j + 1) if isinstance(j, int) else ds(j, 1)
                    nc.gpsimd.tensor_copy(idx[:, s], k["rows"][:, col].rearrange("p o r -> p (o r)")
                                          ).then_inc(s_idx, 1)
                    wait_alone(pool, s_idx, j + 1, s_ppassed)
                    for r in range(2):
                        nc.gpsimd.indirect_dma_start(
                            part[:, s, r], None, tables["part"],
                            bass.IndirectOffsetOnAxis(idx[:, s, r:r + 1], 0)).then_inc(s_part[s], 16)
                each(pool, step)

        FRONT = {"first": 3, "middle": 6}[kind]

        @block.vector
        def _(v):
            c = Chain(v, s_vec, s_passed)

            def front(j, s, use):
                c.base, c.n = j * FRONT, 0
                if isinstance(j, int) and j == 0:
                    v.wait_ge(s_in[0], loads)
                if later(j):
                    v.wait_ge(s_turn, j - 1)
                src = block_of(xin, j) if norm else None
                if gather:
                    v.wait_ge(s_part[s], use * 32)
                    c.after(nc.vector.tensor_tensor(mx[:], part[:, s, 0, MAXAT:ROW], part[:, s, 1, MAXAT:ROW],
                                                    ALU.max))
                    nc.vector.tensor_tensor(dm[:], part[:, s, :, MAXAT:ROW],
                                            mx[:, None, :].to_broadcast([P, 2, H]), ALU.subtract
                                            ).then_inc(s_dm, 1)
                    v.wait_ge(s_sc, j + 1)
                    c.after(nc.vector.tensor_tensor(
                        scaled[:], part[:, s, :, 0:MAXAT].rearrange("p r (h c) -> p r h c", h=H),
                        sc[:].unsqueeze(3).to_broadcast([P, 2, H, HW]), ALU.mult))
                    c.after(nc.vector.tensor_tensor(scaled[:, 0], scaled[:, 0], scaled[:, 1], ALU.add))
                    c.after(nc.vector.tensor_scalar(den[:], scaled[:, 0, :, C], 1e-16, None, ALU.add))
                    c.after(nc.vector.reciprocal(den[:], den[:]))
                    c.after(nc.vector.tensor_tensor(
                        joined[:].rearrange("p (h c) -> p h c", h=H), scaled[:, 0, :, 0:C],
                        den[:].unsqueeze(2).to_broadcast([P, H, C]), ALU.mult))
                    nc.vector.tensor_tensor(z[:, s], joined[:], block_of(skip, j), ALU.add).then_inc(s_z, 1)
                if norm:
                    c.after(nc.vector.bn_stats(stats[:], src), alone=True)
                    c.after(nc.vector.bn_aggr(mv[:], stats[:]))
                    nc.vector.tensor_scalar(rs[:], mv[:, 1:2], EPS, None, ALU.add).then_inc(s_var, 1)
                    v.wait_ge(s_std, j + 1)
                    c.after(nc.vector.reciprocal(rs[:], std[:]))
                    nc.vector.tensor_scalar(z[:, s], src, mv[:, 0:1], rs[:, 0:1], ALU.subtract, ALU.mult
                                            ).then_inc(s_z, 1)
                assert c.n == FRONT, c.n

            def back(j, s, use):
                v.wait_ge(s_mm, j + 1)
                if later(j):
                    v.wait_ge(s_st[s], (use - 1) * 48)
                nc.vector.tensor_tensor(outs[:, s], ps_out[:, s].rearrange("p b n -> p (b n)"), bias[:], ALU.add
                                        ).then_inc(s_out, 1)

            v.wait_ge(s_w, 32)
            front(0, 0, 1)
            front(1, 1, 1)
            front(2, 0, 2)
            back(0, 0, 1)
            v.wait_ge(s_in[1], loads)
            front(3, 1, 2)
            back(1, 1, 1)
            with v.Fori(2, (NB - 1) // 2) as it:
                front(it * 2, 0, it + 1)
                back(it * 2 - 2, 0, it)
                front(it * 2 + 1, 1, it + 1)
                back(it * 2 - 1, 1, it)
            front(NB - 1, 0, NB // 2 + 1)
            back(NB - 3, 0, NB // 2)
            back(NB - 2, 1, NB // 2)
            back(NB - 1, 0, NB // 2 + 1)

        @block.scalar
        def _(act):
            def step(j, s, use):
                if gather:
                    act.wait_ge(s_dm, j + 1)
                    nc.scalar.activation(sc[:], dm[:], ACT.Exp, scale=INV).then_inc(s_sc, 1)
                if norm:
                    act.wait_ge(s_var, j + 1)
                    nc.scalar.activation(std[:], rs[:], ACT.Sqrt).then_inc(s_std, 1)
                act.wait_ge(s_turn, j + 1)
                turned = ps_turn[:, s, 0:D].rearrange("p (c n) -> p c n", c=2)
                if later(j):
                    act.wait_ge(s_mm, j - 1)
                nc.scalar.activation(zT[:, s], turned, ACT.Relu if kind == "middle" else ACT.Copy
                                     ).then_inc(s_zT, 1)
            each(act, step)

        @block.tensor
        def _(te):
            def turn(j, s):
                te.wait_ge(s_z, j + 1)
                if later(j):
                    te.wait_ge(s_zT, j - 1)
                nc.tensor.transpose(ps_turn[:, s, 0:P], z[:, s, 0:P], k["ident"][:])
                nc.tensor.transpose(ps_turn[:, s, P:D], z[:, s, P:D], k["ident"][:]).then_inc(s_turn, 1)

            def products(j, s):
                te.wait_ge(s_zT, j + 1)
                if later(j):
                    te.wait_ge(s_out, j - 1)
                for b in range(2):
                    for c in range(2):
                        mm = nc.tensor.matmul(ps_out[:, s, b], zT[:, s, c], w[:, c, b * 512:(b + 1) * 512],
                                              start=(c == 0), stop=(c == 1))
                mm.then_inc(s_mm, 1)

            te.wait_ge(s_w, 32)
            turn(0, 0)
            turn(1, 1)
            products(0, 0)
            turn(2, 0)
            products(1, 1)
            turn(3, 1)
            products(2, 0)
            with te.Fori(1, (NB - 1) // 2 - 1) as it:
                turn(it * 2 + 2, 0)
                products(it * 2 + 1, 1)
                turn(it * 2 + 3, 1)
                products(it * 2 + 2, 0)
            turn(NB - 1, 0)
            products(NB - 2, 1)
            products(NB - 1, 0)


def edge_pass(nc, a, tables, k, layer):
    with ExitStack() as ctx:
        nm = f"e{layer}_"
        sb = lambda name, shape, dt=F32: ctx.enter_context(nc.sbuf_tensor(nm + name, shape, dt))
        sem = semaphores(nc, ctx, nm)
        ps = lambda name, shape: ctx.enter_context(nc.psum_tensor(nm + name, shape, F32))
        ps_e = ps("ps_e", [P, 2, 2, D])
        ps_s = ps("ps_s", [P, 2, 2, 512])
        ps_l, ps_m = ps("ps_l", [P, 512]), ps("ps_m", [P, 512])
        we = sb("we", [P, 2, D])
        ft = sb("ft", [P, 2, 2, G * P])
        si, qi = sb("si", [P, 2, G], I32), sb("qi", [P, 2, G], I32)
        drow = sb("drow", [P, 2, G * P], I32)
        work = sb("work", [P, 2, G, SLOT])
        qg, prod = sb("qg", [P, 2, 2, D]), sb("prod", [P, 2, 2, D])
        lg, mT = sb("lg", [P, 2, H, G]), sb("mT", [4 * G, 2, P])
        diff = sb("diff", [P, H, G])
        seg = sb("seg", [P, 2, 2, P])
        res = sb("res", [P, 2, G, ROW])
        s_w, s_zero, s_e, s_ee, s_prod, s_lg, s_lT, s_scan, s_mT, s_diff, s_w8, s_seg, s_wv, s_sum, s_res, s_max, s_mcol = (
            sem(n) for n in ("weights", "zeroed", "e", "eInSbuf", "prod", "logits", "turned", "scan", "maxT",
                             "diff", "expw", "seg", "weighted", "sums", "res", "maxBack", "maxcol"))
        s_ld = [sem(f"loaded{i}") for i in range(2)]
        s_tpassed, s_ppassed = sem("tpassed"), sem("ppassed")
        s_dr = [sem(f"drow{i}") for i in range(2)]
        s_g = [sem(f"gathered{i}") for i in range(2)]
        s_st = [sem(f"stored{i}") for i in range(2)]
        block = ctx.enter_context(nc.Block())
        LD = 16 * (2 * PAIRS + 3)

        def stages(eng, stage):
            stage(0, 0, 0, True, False)
            stage(1, 1, 0, True, True)
            stage(2, 0, 1, True, True)
            with eng.Fori(1, HALVES // 2 - 1) as i:
                stage(i * 2 + 1, 1, i, True, True)
                stage(i * 2 + 2, 0, i + 1, True, True)
            stage(HALVES - 1, 1, HALVES // 2 - 1, True, True)
            stage(HALVES, 0, HALVES // 2, False, True)

        def stored(par, half2):
            return half2 - 1 if par == 0 else half2

        def has_next(u):
            return not (isinstance(u, int) and u == HALVES - 1)

        def pair_slot(par, p):
            return (PAIRS * par + p) % 2

        def pair_use(par, half2, p):
            return half2 * PAIRS + ((PAIRS * par + p) // 2 + 1)

        @block.sync
        def _(sp):
            w_dram = a[f"we{layer}"]
            sp.wait_ge(s_zero, 2)
            sp.dma_start(we[:, 0], w_dram[0:ED0]).then_inc(s_w, 16)
            sp.dma_start(we[0:ED1, 1], w_dram[ED0:ED]).then_inc(s_w, 16)

            def cols(ap, u, step, lo, n):
                return ap[:, u * step + lo:u * step + lo + n] if isinstance(u, int) else ap[:, ds(u * step + lo, n)]

            def load(u, par, parts):
                for p in parts:
                    lo, n = p * 2 * P, 2 * P
                    src = lambda r0, r1: cols(a["ft"][r0:r1], u, G * P, lo, n)
                    sp.dma_start(ft[:, par, 0, lo:lo + n], src(0, ED0)).then_inc(s_ld[par], 16)
                    sp.dma_start(ft[0:ED1_MANY, par, 1, lo:lo + n], src(ED0, ED0 + ED1_MANY)).then_inc(s_ld[par], 16)
                if 0 in parts:
                    sp.dma_start(ft[ED1_MANY:ED1, par, 1], cols(a["ft"][ED0 + ED1_MANY:ED], u, G * P, 0, G * P)
                                 ).then_inc(s_ld[par], 16)
                    sp.dma_start(si[:, par], cols(a["src_cols"], u, G, 0, G)).then_inc(s_ld[par], 16)
                    sp.dma_start(qi[:, par], cols(a["dst_cols"], u, G, 0, G)).then_inc(s_ld[par], 16)

            def stage(u, par, half2, has_a, has_c):
                if isinstance(u, int) and u == 0:
                    load(0, 0, range(PAIRS))
                if has_c:
                    sp.wait_ge(s_lg, u * PAIRS)
                for p in range(PAIRS):
                    if has_a and has_next(u) and 2 * p < PAIRS:
                        load(u + 1, 1 - par, range(2 * p, min(2 * p + 2, PAIRS)))
                    if has_a and p == 4:
                        if not (isinstance(u, int) and u < 2):
                            sp.wait_ge(s_seg, (u - 1) * PAIRS)
                        row = a["dst"][u * G * P:(u + 1) * G * P] if isinstance(u, int) else a["dst"][
                            ds(u * G * P, G * P)]
                        sp.dma_start(drow[:, par], row[None, :].to_broadcast([P, G * P])).then_inc(s_dr[par], 16)
                    if has_c:
                        sp.wait_ge(s_res, (u - 1) * PAIRS + (p + 1))
                        if p == 0:
                            sp.wait_ge(s_mcol, u)
                        lo, n = (u - 1) * (G * P) + p * 2 * P, 2 * P
                        rows = tables["part"][lo:lo + n] if isinstance(u, int) else tables["part"][ds(lo, n)]
                        sp.dma_start(rows.rearrange("(t p) w -> p t w", p=P), res[:, 1 - par, 2 * p:2 * p + 2]
                                     ).then_inc(s_st[1 - par], 16)

            stages(sp, stage)
            for i in range(2):
                sp.wait_ge(s_st[i], 16 * PAIRS * (HALVES // 2))

        @block.gpsimd
        def _(pool):
            nc.gpsimd.memset(we[:], 0.0).then_inc(s_zero, 1)
            nc.gpsimd.memset(ft[:, :, 1], 0.0).then_inc(s_zero, 1)

            def stage(u, par, half2, has_a, has_c):
                if not has_a:
                    return
                wait_alone(pool, s_ld[par], half2 * LD + LD, s_ppassed)
                for p in range(PAIRS):
                    slot = pair_slot(par, p)
                    pair = u * PAIRS + p
                    if not isinstance(u, int) or pair >= 2:
                        wait_alone(pool, s_prod, pair - 1, s_ppassed)
                    for i in range(2):
                        nc.gpsimd.indirect_dma_start(
                            qg[:, slot, i], None, tables["q"],
                            bass.IndirectOffsetOnAxis(qi[:, par, 2 * p + i:2 * p + i + 1].bitcast(U32), 0)
                        ).then_inc(s_g[slot], 16)
                    wait_alone(pool, s_ee, pair + 1, s_ppassed)
                    for i in range(2):
                        nc.gpsimd.indirect_dma_start(
                            work[:, par, 2 * p + i, KAT:SLOT], None, tables["kv"],
                            bass.IndirectOffsetOnAxis(si[:, par, 2 * p + i:2 * p + i + 1].bitcast(U32), 0),
                            compute_op=ALU.add).then_inc(s_g[slot], 16)

            stages(pool, stage)

        @block.tensor
        def _(te):
            te.wait_ge(s_w, 32)

            def features(u, par, half2, p):
                pair = u * PAIRS + p
                if not isinstance(u, int) or pair >= 2:
                    te.wait_ge(s_ee, pair - 1)
                for i in range(2):
                    t = 2 * p + i
                    for c in range(2):
                        mm = nc.tensor.matmul(ps_e[:, pair_slot(par, p), i], ft[:, par, c, t * P:(t + 1) * P],
                                              we[:, c], start=(c == 0), stop=(c == 1))
                mm.then_inc(s_e, 1)

            def sums(u, par, p):
                pair = (u - 1) * PAIRS + p
                slot = pair_slot(1 - par, p)
                te.wait_ge(s_seg, pair + 1)
                te.wait_ge(s_wv, pair + 1)
                if not isinstance(u, int) or pair >= 2:
                    te.wait_ge(s_res, pair - 1)
                for i in range(2):
                    mm = nc.tensor.matmul(ps_s[:, slot, i, 0:MAXAT], seg[:, slot, i],
                                          work[:, 1 - par, 2 * p + i, 0:MAXAT], start=True, stop=True)
                mm.then_inc(s_sum, 1)

            def stage(u, par, half2, has_a, has_c):
                if isinstance(u, int) and u == 0:
                    te.wait_ge(s_ld[0], LD)
                    features(0, 0, 0, 0)
                    features(0, 0, 0, 1)
                if has_c:
                    wait_alone(te, s_lg, u * PAIRS, s_tpassed)
                    nc.tensor.transpose(ps_l[0:4 * G, 0:P], lg[:, 1 - par].rearrange("p h t -> p (h t)"),
                                        k["ident"][:]).then_inc(s_lT, 1)
                    te.wait_ge(s_mcol, u - 1)
                    wait_alone(te, s_mT, u, s_tpassed)
                    nc.tensor.transpose(ps_m[:, 0:4 * G], mT[:, 1], k["ident"][0:4 * G, 0:4 * G]).then_inc(s_max, 1)
                for p in range(PAIRS):
                    if has_a and p + 2 < PAIRS:
                        features(u, par, half2, p + 2)
                    elif has_a and has_next(u):
                        if p + 2 == PAIRS:
                            te.wait_ge(s_ld[1 - par], (half2 + par) * LD + LD)
                        features(u + 1, 1 - par, half2 + par, p + 2 - PAIRS)
                    if has_c:
                        sums(u, par, p)

            stages(te, stage)

        @block.scalar
        def _(act):
            def copy_e(u, par, p):
                pair = u * PAIRS + p
                act.wait_ge(s_e, pair + 1)
                if not isinstance(u, int) or u >= 2:
                    act.wait_ge(s_sum, pair - 2 * PAIRS + 1)
                nc.scalar.copy(
                    work[:, par, 2 * p:2 * p + 2, KAT:SLOT].rearrange("p t (o d) -> p t o d", o=2),
                    ps_e[:, pair_slot(par, p), :, None, :].to_broadcast([P, 2, 2, D])).then_inc(s_ee, 1)

            def stage(u, par, half2, has_a, has_c):
                if isinstance(u, int) and u == 0:
                    copy_e(0, 0, 0)
                    copy_e(0, 0, 1)
                if has_c:
                    act.wait_ge(s_diff, u)
                    nc.scalar.activation(work[:, 1 - par, :, C:MAXAT:HW], diff[:].rearrange("p h t -> p t h"),
                                         ACT.Exp, scale=INV).then_inc(s_w8, 1)
                for p in range(PAIRS):
                    if has_a and p + 2 < PAIRS:
                        copy_e(u, par, p + 2)
                    elif has_a and has_next(u):
                        copy_e(u + 1, 1 - par, p + 2 - PAIRS)
                    if has_c:
                        pair = (u - 1) * PAIRS + p
                        act.wait_ge(s_sum, pair + 1)
                        if p == 0 and not (isinstance(u, int) and u < 3):
                            act.wait_ge(s_st[1 - par], stored(par, half2) * (16 * PAIRS))
                        nc.scalar.copy(res[:, 1 - par, 2 * p:2 * p + 2, 0:MAXAT],
                                       ps_s[:, pair_slot(1 - par, p), :, 0:MAXAT]).then_inc(s_res, 1)

            stages(act, stage)

        @block.vector
        def _(v):
            def logits(u, par, p):
                pair = u * PAIRS + p
                slot = pair_slot(par, p)
                v.wait_ge(s_prod, pair + 1)
                nc.vector.tensor_reduce(lg[:, par, :, 2 * p:2 * p + 2].rearrange("p h t -> p t h"),
                                        prod[:, slot].rearrange("p t (h c) -> p t h c", h=H), AX.X, ALU.add
                                        ).then_inc(s_lg, 1)

            def product(u, par, half2, p):
                slot = pair_slot(par, p)
                v.wait_ge(s_g[slot], pair_use(par, half2, p) * 64)
                if not isinstance(u, int) or u * PAIRS + p >= 2:
                    v.wait_ge(s_lg, u * PAIRS + p - 1)
                nc.vector.tensor_tensor(prod[:, slot], work[:, par, 2 * p:2 * p + 2, KAT:VAT], qg[:, slot], ALU.mult
                                        ).then_inc(s_prod, 1)

            def maxima(u, par, half2):
                half = slice(u - 1, u) if isinstance(u, int) else ds(u - 1, 1)
                new_f = k["new_fwd"][:, half].rearrange("p o e -> p (o e)")
                new_b = k["new_bwd"][:, half].rearrange("p o e -> p (o e)")
                v.wait_ge(s_lT, u)
                nc.vector.tensor_tensor_scan(mT[:, 0, ::-1], new_f, ps_l[0:4 * G, 0:P], LOW, ALU.add, ALU.max
                                             ).then_inc(s_scan, 1)
                v.wait_ge(s_scan, u)
                nc.vector.tensor_tensor_scan(mT[:, 1, ::-1], new_b, mT[:, 0], LOW, ALU.add, ALU.max
                                             ).then_inc(s_mT, 1)
                v.wait_ge(s_max, u)
                col = ps_m[:, 0:4 * G].rearrange("p (h t) -> p h t", h=H)
                nc.vector.tensor_tensor(diff[:], lg[:, 1 - par], col, ALU.subtract).then_inc(s_diff, 1)
                if not (isinstance(u, int) and u < 3):
                    v.wait_ge(s_st[1 - par], stored(par, half2) * (16 * PAIRS))
                nc.vector.tensor_copy(res[:, 1 - par, :, MAXAT:ROW], col.rearrange("p h t -> p t h")
                                      ).then_inc(s_mcol, 1)

            def weigh(u, par, p):
                pair = (u - 1) * PAIRS + p
                slot = pair_slot(1 - par, p)
                n = (u - 1) * G + 2 * p
                own = k["dst_col"][:, n:n + 2] if isinstance(u, int) else k["dst_col"][:, ds(n, 2)]
                if not isinstance(u, int) or pair >= 2:
                    v.wait_ge(s_sum, pair - 1)
                nc.vector.tensor_tensor(
                    seg[:, slot], drow[:, 1 - par, 2 * p * P:(2 * p + 2) * P].rearrange("p (t e) -> p t e", t=2),
                    own.unsqueeze(2).to_broadcast([P, 2, P]), ALU.is_equal).then_inc(s_seg, 1)
                rows = work[:, 1 - par, 2 * p:2 * p + 2, 0:MAXAT].rearrange("p t (h c) -> p t h c", h=H)
                nc.vector.tensor_tensor(
                    rows[:, :, :, 0:C], work[:, 1 - par, 2 * p:2 * p + 2, VAT:SLOT].rearrange(
                        "p t (h c) -> p t h c", h=H),
                    rows[:, :, :, C:HW].to_broadcast([P, 2, H, C]), ALU.mult).then_inc(s_wv, 1)

            def stage(u, par, half2, has_a, has_c):
                if has_c:
                    maxima(u, par, half2)
                    v.wait_ge(s_w8, u)
                    v.wait_ge(s_dr[1 - par], dr_use(par, half2) * 16)
                for p in range(PAIRS):
                    if has_c:
                        weigh(u, par, p)
                    if has_a:
                        product(u, par, half2, p)
                        if p >= 1:
                            logits(u, par, p - 1)
                if has_a:
                    logits(u, par, PAIRS - 1)

            def dr_use(par, half2):
                return half2 if par == 0 else half2 + 1

            stages(v, stage)


def chain_pass(nc, a, tables, k, layer):
    with ExitStack() as ctx:
        nm = f"c{layer}_"
        sb = lambda name, shape, dt=F32: ctx.enter_context(nc.sbuf_tensor(nm + name, shape, dt))
        sem = lambda name: ctx.enter_context(nc.semaphore(nm + name))
        ps = lambda name, shape: ctx.enter_context(nc.psum_tensor(nm + name, shape, F32))
        last = sb("last", [CR, CH, ROW])
        run = sb("run", [H, T])
        wgt = sb("wgt", [CR, H, CH, T])
        out = sb("out", [CR, CH, ROW])
        ps_t, ps_r = ps("ps_t", [P, 512]), ps("ps_r", [P, 512])
        ps_b, ps_o = ps("ps_b", [P, 2, 512]), ps("ps_o", [P, 2, 512])
        s_in, s_t, s_run, s_b, s_r, s_arg, s_exp, s_wgt, s_o, s_out, s_m, s_st = (
            sem(n) for n in ("in", "turned", "run", "spread", "back", "arg", "exp", "wgt", "sums", "out", "m", "st"))
        block = ctx.enter_context(nc.Block())

        @block.sync
        def _(sp):
            rows = tables["part"][0:EDGES].rearrange("(c r p) w -> p r c w", c=CH, p=P)
            sp.dma_start(last[:], rows[P - 1]).then_inc(s_in, 16)
            sp.wait_ge(s_out, CH)
            sp.wait_ge(s_m, 1)
            sp.dma_start(tables["part"][NULL + 1:NULL + 1 + T].rearrange("(c r) w -> r c w", c=CH), out[:]
                         ).then_inc(s_st, 16)
            sp.wait_ge(s_st, 16)

        @block.tensor
        def _(te):
            te.wait_ge(s_in, 16)
            for c in range(CH):
                tr = nc.tensor.transpose(ps_t[0:H, c * CR:(c + 1) * CR], last[:, c, MAXAT:ROW],
                                         k["ident"][0:CR, 0:CR])
            tr.then_inc(s_t, 1)
            te.wait_ge(s_run, 1)
            for c in range(CH):
                tr = nc.tensor.transpose(ps_r[0:CR, c * H:(c + 1) * H], run[:, c * CR:(c + 1) * CR],
                                         k["ident"][0:H, 0:H])
            tr.then_inc(s_r, 1)
            for h in range(H):
                if h >= 2:
                    te.wait_ge(s_arg, h - 1)
                nc.tensor.matmul(ps_b[0:CR, h % 2, 0:T], k["head_row"][:, h], run[:], start=True, stop=True
                                 ).then_inc(s_b, 1)
            te.wait_ge(s_wgt, H)
            for c in range(CH):
                if c >= 2:
                    te.wait_ge(s_out, c - 1)
                for h in range(H):
                    for e in range(c + 1):
                        mm = nc.tensor.matmul(ps_o[0:CR, c % 2, h * HW:(h + 1) * HW],
                                              wgt[:, h, e, c * CR:(c + 1) * CR],
                                              last[:, e, h * HW:(h + 1) * HW], start=(e == 0), stop=(e == c))
                mm.then_inc(s_o, 1)

        @block.vector
        def _(v):
            v.wait_ge(s_t, 1)
            nc.vector.tensor_tensor_scan(run[:], k["chain_new"][:], ps_t[0:H, 0:T], LOW, ALU.add, ALU.max
                                         ).then_inc(s_run, 1)
            v.wait_ge(s_r, 1)
            nc.vector.tensor_copy(out[:, :, MAXAT:ROW], ps_r[0:CR, 0:CH * H].rearrange("p (c h) -> p c h", c=CH)
                                  ).then_inc(s_m, 1)

            def mask(h):
                v.wait_ge(s_exp, h + 1)
                nc.vector.tensor_tensor(wgt[:, h], wgt[:, h], k["chain_mask"][:], ALU.mult).then_inc(s_wgt, 1)

            for h in range(H):
                v.wait_ge(s_b, h + 1)
                for e in range(CH):
                    ins = nc.vector.tensor_scalar(wgt[:, h, e], ps_b[0:CR, h % 2, 0:T],
                                                  last[:, e, MAXAT + h:MAXAT + h + 1], 0.0,
                                                  ALU.subtract, ALU.max)
                ins.then_inc(s_arg, 1)
                if h:
                    mask(h - 1)
            mask(H - 1)

        @block.scalar
        def _(act):
            for h in range(H):
                act.wait_ge(s_arg, h + 1)
                nc.scalar.activation(wgt[:, h], wgt[:, h], ACT.Exp, scale=-INV).then_inc(s_exp, 1)
            for c in range(CH):
                act.wait_ge(s_o, c + 1)
                nc.scalar.copy(out[:, c, 0:MAXAT], ps_o[0:CR, c % 2, 0:MAXAT]).then_inc(s_out, 1)


def last_blocks(nc, a, tables, k):
    RING = 4
    with ExitStack() as ctx:
        sb = lambda name, shape, dt=F32: ctx.enter_context(nc.sbuf_tensor("l_" + name, shape, dt))
        sem = lambda name: ctx.enter_context(nc.semaphore("l_" + name))
        x1, skip, z = sb("x1", [P, NB, D]), sb("skip", [P, NB, D]), sb("z", [P, RING, D])
        part, idx = sb("part", [P, RING, 2, ROW]), sb("idx", [P, RING, 2], U32)
        mx, dm, sc = sb("mx", [P, 2, H]), sb("dm", [P, 2, 2, H]), sb("sc", [P, 2, 2, H])
        scaled, den, joined = sb("scaled", [P, 2, H, HW]), sb("den", [P, H]), sb("joined", [P, D])
        stats, mv = sb("stats", [P, 6]), sb("mv", [P, 2])
        moments, var, rs = sb("moments", [P, NB, 2]), sb("var", [P, NB]), sb("rs", [P, NB])
        zT, wg, bg, zero = sb("zT", [P, 2, 2, P]), sb("wg", [P, 2, XN]), sb("bg", [P, XN]), sb("zero", [P, D])
        ps_turn = ctx.enter_context(nc.psum_tensor("l_turn", [P, 2, 512], F32))
        ps_sc = ctx.enter_context(nc.psum_tensor("l_scores", [P, 2, 512], F32))
        s_w, s_wx, s_idx, s_max, s_dm, s_sc, s_join, s_x1, s_var, s_std, s_rs, s_z, s_turn, s_zT, s_mm, s_score, s_zero, s_st = (
            sem(n) for n in ("weights", "expertWeights", "idx", "max", "dm", "sc", "join", "x1", "var", "std",
                             "rs", "z", "turned", "zT", "products", "score", "zero", "stored"))
        s_passed, s_ppassed = sem("passed"), sem("ppassed")
        s_part = [sem(f"part{i}") for i in range(RING)]
        s_zst = [sem(f"zStored{i}") for i in range(RING)]
        s_in = [sem(f"in{i}") for i in range(2)]
        JOIN = 9
        CHUNK = 5
        block = ctx.enter_context(nc.Block())

        @block.sync
        def _(sp):
            for part_of, lo, hi in ((0, 0, RING + 1), (1, RING + 1, NB)):
                sp.dma_start(x1[:, lo:hi], blocks(a["x"])[:, lo:hi]).then_inc(s_in[part_of], 16)
                sp.dma_start(skip[:, lo:hi], blocks(tables["skip"])[:, lo:hi]).then_inc(s_in[part_of], 16)
            sp.dma_start(wg[:], a["wg"].rearrange("(c p) n -> p c n", p=P)).then_inc(s_w, 16)
            sp.dma_start(bg[:], a["bg"][None, :].to_broadcast([P, XN])).then_inc(s_w, 16)
            for e in range(XN):
                sp.wait_ge(s_x1, 2 * e + 1)
                sp.dma_start(k["w1"][:, e], a["w1x"][e].rearrange("(c p) h -> p c h", p=P)).then_inc(s_wx, 16)
                sp.dma_start(k["w2"][:, e], a["w2x"][e].rearrange("(c p) d -> p c d", p=P)).then_inc(s_wx, 16)
                sp.dma_start(k["b1"][:, e], a["b1"][e:e + 1].to_broadcast([P, XH])).then_inc(s_wx, 16)
                sp.dma_start(k["b2"][:, e], a["b2"][e:e + 1].to_broadcast([P, D])).then_inc(s_wx, 16)
            sp.wait_ge(s_zero, 1)
            sp.dma_start(tables["acc"][NP:NP + P], zero[:]).then_inc(s_st, 16)
            sp.dma_start(tables["z"][NP:NP + P], zero[:]).then_inc(s_st, 16)
            for lo in range(0, NB, CHUNK):
                sp.wait_ge(s_x1, lo + CHUNK)
                sp.dma_start(blocks(tables["acc"][0:NP])[:, lo:lo + CHUNK], x1[:, lo:lo + CHUNK]
                             ).then_inc(s_st, 16)

            def store(j, s, use):
                sp.wait_ge(s_z, j + 1)
                sp.dma_start(rows_of(tables["z"], j), z[:, s]).then_inc(s_zst[s], 16)
            each(sp, store, NB, RING)
            for s in range(RING):
                sp.wait_ge(s_zst[s], 16 * len(range(s, NB, RING)))
            sp.wait_ge(s_st, 16 * (2 + NB // CHUNK))
            sp.wait_ge(s_wx, 16 * 4 * XN)

        @block.gpsimd
        def _(pool):
            nc.gpsimd.memset(zero[:], 0.0).then_inc(s_zero, 1)

            def step(j, s, use):
                if later(j, RING):
                    pool.wait_ge(s_x1, j - (RING - 1))
                col = slice(j, j + 1) if isinstance(j, int) else ds(j, 1)
                nc.gpsimd.tensor_copy(idx[:, s], k["rows"][:, col].rearrange("p o r -> p (o r)")
                                      ).then_inc(s_idx, 1)
                wait_alone(pool, s_idx, j + 1, s_ppassed)
                for r in range(2):
                    nc.gpsimd.indirect_dma_start(part[:, s, r], None, tables["part"],
                                                 bass.IndirectOffsetOnAxis(idx[:, s, r:r + 1], 0)
                                                 ).then_inc(s_part[s], 16)
            each(pool, step, NB, RING)

        @block.vector
        def _(v):
            c, m = Chain(v, s_join, s_passed), Chain(v, s_max)

            def spread(j, s, use):
                v.wait_ge(s_part[s], use * 32)
                m.base, m.n = j, 0
                m.after(nc.vector.tensor_tensor(mx[:, s % 2], part[:, s, 0, MAXAT:ROW], part[:, s, 1, MAXAT:ROW], ALU.max))
                nc.vector.tensor_tensor(dm[:, s % 2], part[:, s, :, MAXAT:ROW],
                                        mx[:, s % 2, None, :].to_broadcast([P, 2, H]), ALU.subtract).then_inc(s_dm, 1)

            def step(j, s, use):
                if not (isinstance(j, int) and j == NB - 1):
                    spread(j + 1, (s + 1) % RING, use + (s + 1) // RING)
                c.base, c.n = j * JOIN, 0
                v.wait_ge(s_sc, j + 1)
                c.after(nc.vector.tensor_tensor(
                    scaled[:], part[:, s, :, 0:MAXAT].rearrange("p r (h c) -> p r h c", h=H),
                    sc[:, s % 2].unsqueeze(3).to_broadcast([P, 2, H, HW]), ALU.mult))
                c.after(nc.vector.tensor_tensor(scaled[:, 0], scaled[:, 0], scaled[:, 1], ALU.add))
                c.after(nc.vector.tensor_scalar(den[:], scaled[:, 0, :, C], 1e-16, None, ALU.add))
                c.after(nc.vector.reciprocal(den[:], den[:]))
                c.after(nc.vector.tensor_tensor(
                    joined[:].rearrange("p (h c) -> p h c", h=H), scaled[:, 0, :, 0:C],
                    den[:].unsqueeze(2).to_broadcast([P, H, C]), ALU.mult))
                row = block_of(x1, j)
                c.after(nc.vector.tensor_tensor(joined[:], joined[:], block_of(skip, j), ALU.add))
                c.after(nc.vector.tensor_tensor(row, joined[:], row, ALU.add), alone=True)
                c.after(nc.vector.bn_stats(stats[:], row), alone=True)
                c.after(nc.vector.bn_aggr(mv[:], stats[:]))
                assert c.n == JOIN
                nc.vector.tensor_copy(block_of(moments, j), mv[:]).then_inc(s_x1, 1)
                if isinstance(j, int) and j == RING:
                    v.wait_ge(s_in[1], 32)

            v.wait_ge(s_in[0], 32)
            spread(0, 0, 1)
            each(v, step, NB, RING)

            v.wait_ge(s_x1, NB)
            nc.vector.tensor_scalar(var[:], moments[:, :, 1], EPS, None, ALU.add).then_inc(s_var, 1)
            v.wait_ge(s_std, 1)
            nc.vector.reciprocal(rs[:], rs[:]).then_inc(s_rs, 1)
            v.wait_ge(s_rs, 1)
            v.wait_ge(s_w, 32)

            def norm(j, s, use):
                if later(j, RING):
                    v.wait_ge(s_turn, j - (RING - 1))
                    v.wait_ge(s_zst[s], (use - 1) * 16)
                at = slice(j, j + 1) if isinstance(j, int) else ds(j, 1)
                nc.vector.tensor_scalar(z[:, s], block_of(x1, j), moments[:, at, 0], rs[:, at],
                                        ALU.subtract, ALU.mult).then_inc(s_z, 1)

            def score(j, s):
                v.wait_ge(s_mm, j + 1)
                nc.vector.tensor_tensor(block_of(k["scores"], j), ps_sc[:, s, 0:XN], bg[:], ALU.add
                                        ).then_inc(s_score, 1)

            def sweep(j, s, use):
                norm(j, s, use)
                if later(j):
                    score(j - 2, s % 2)
            each(v, sweep, NB, RING)
            score(NB - 2, 1)
            score(NB - 1, 0)
            v.wait_ge(s_score, NB)

        @block.scalar
        def _(act):
            def rescale(j, s, use):
                act.wait_ge(s_dm, j + 1)
                nc.scalar.activation(sc[:, s % 2], dm[:, s % 2], ACT.Exp, scale=INV).then_inc(s_sc, 1)
            each(act, rescale, NB, RING)
            act.wait_ge(s_var, 1)
            nc.scalar.activation(rs[:], var[:], ACT.Sqrt).then_inc(s_std, 1)

            def step(j, s, use):
                act.wait_ge(s_turn, j + 1)
                if later(j):
                    act.wait_ge(s_mm, j - 1)
                nc.scalar.copy(zT[:, s], ps_turn[:, s, 0:D].rearrange("p (c n) -> p c n", c=2)).then_inc(s_zT, 1)
            each(act, step)

        @block.tensor
        def _(te):
            def turn(j, slot):
                s = slot % 2
                te.wait_ge(s_z, j + 1)
                if later(j):
                    te.wait_ge(s_zT, j - 1)
                nc.tensor.transpose(ps_turn[:, s, 0:P], z[:, slot, 0:P], k["ident"][:])
                nc.tensor.transpose(ps_turn[:, s, P:D], z[:, slot, P:D], k["ident"][:]).then_inc(s_turn, 1)

            def products(j, s):
                te.wait_ge(s_zT, j + 1)
                if later(j):
                    te.wait_ge(s_score, j - 1)
                for c in range(2):
                    mm = nc.tensor.matmul(ps_sc[:, s, 0:XN], zT[:, s, c], wg[:, c], start=(c == 0), stop=(c == 1))
                mm.then_inc(s_mm, 1)

            te.wait_ge(s_w, 32)

            def step(j, s, use):
                turn(j, s)
                if not isinstance(j, int) or j >= 1:
                    products(j - 1, 1 - s % 2)
            each(te, step, NB, RING)
            products(NB - 1, 0)


def route(nc, k):
    with ExitStack() as ctx:
        sb = lambda name, shape, dt=F32: ctx.enter_context(nc.sbuf_tensor("r_" + name, shape, dt))
        sem = lambda name: ctx.enter_context(nc.semaphore("r_" + name))
        ps_pre, ps_tot, ps_perm = (ctx.enter_context(nc.psum_tensor("r_ps" + n, [P, 512], F32))
                                   for n in ("pre", "tot", "perm"))
        best, cand, low = sb("best", [P, NB]), sb("cand", [P, NB, XN]), sb("low", [P, NB])
        hit, rest = sb("hit", [P, 2, NB, XN]), sb("rest", [P, NB, XN])
        goes = sb("goes", [P, NB, XN])
        keep, tot = sb("keep", [P, XN, NB]), sb("tot", [P, XN, NB])
        upto, place = sb("upto", [P, XN, NB]), sb("place", [P, XN, NB])
        tiles_i = sb("tiles_i", [P, XN], I32)
        tiles, ends, begin, zero = (sb(n, [P, XN]) for n in ("tiles", "ends", "begin", "zero"))
        slots, slots_i = sb("slots", [P, 2, NB]), sb("slots_i", [P, 2, NB], I32)
        lo_i, hi_i = sb("lo_i", [P, 2, NB], I32), sb("hi_i", [P, 2, NB], I32)
        lo, hi = sb("lo", [P, 2, NB]), sb("hi", [P, 2, NB])
        hot_lo, hot_hi = sb("hot_lo", [P, 2, NB, P]), sb("hot_hi", [P, 2, NB, TX])
        at_e, at_t, at_p = sb("at_e", [P, XN]), sb("at_t", [P, TX]), sb("at_p", [P, P])
        node1, pad = sb("node1", [P, NB]), sb("pad", [P, 1])
        after, expert = sb("after", [1, TX, XN - 1]), sb("expert", [1, TX])
        none, perm = sb("none", [P, TX]), sb("permf", [P, TX])
        s_pool, s_v, s_goes, s_cum, s_hot, s_perm = (
            sem(n) for n in ("pool", "vec", "goes", "cum", "hot", "perm"))
        BIG = 65536.0
        block = ctx.enter_context(nc.Block())

        @block.gpsimd
        def _(pool):
            iota = lambda out, pattern, base, ch: nc.gpsimd.iota(
                out, pattern=pattern, base=base, channel_multiplier=ch,
                allow_small_or_imprecise_dtypes=True).then_inc(s_pool, 1)
            iota(at_e[:], [[1, XN]], 0, 0)
            iota(at_t[:], [[1, TX]], 0, 0)
            iota(at_p[:], [[1, P]], 0, 0)
            iota(node1[:], [[P, NB]], 1, 1)
            iota(pad[:], [[1, 1]], NP + 1, 1)
            nc.gpsimd.memset(keep[:, :, 1:NB], 1.0).then_inc(s_pool, 1)
            nc.gpsimd.memset(keep[:, :, 0:1], 0.0).then_inc(s_pool, 1)
            nc.gpsimd.memset(zero[:], 0.0).then_inc(s_pool, 1)

        @block.vector
        def _(v):
            c = Chain(v, s_v)
            tt, ts = nc.vector.tensor_tensor, nc.vector.tensor_scalar
            over_b = lambda ap: ap.unsqueeze(2).to_broadcast([P, NB, XN])
            v.wait_ge(s_pool, 8)
            score = k["scores"]
            for r in range(2):
                c.after(nc.vector.tensor_reduce(best[:], score[:], AX.X, ALU.max))
                c.after(tt(cand[:], score[:], over_b(best[:]), ALU.is_equal))
                c.after(nc.vector.scalar_tensor_tensor(
                    out=cand[:], in0=cand[:], scalar=-100.0, in1=at_e[:, None, :].to_broadcast([P, NB, XN]),
                    op0=ALU.mult, op1=ALU.add))
                c.after(nc.vector.tensor_reduce(low[:], cand[:], AX.X, ALU.min))
                c.after(tt(hit[:, r], cand[:], over_b(low[:]), ALU.is_equal))
                if r == 0:
                    c.after(nc.vector.scalar_tensor_tensor(out=rest[:], in0=hit[:, 0], scalar=-HUGE, in1=score[:],
                                                           op0=ALU.mult, op1=ALU.add))
                    score = rest
            tt(goes[:], hit[:, 0], hit[:, 1], ALU.add).then_inc(s_goes, 1)
            v.wait_ge(s_cum, 2)
            by_e = lambda ap: ap.rearrange("p b e -> p e b")
            from_ps = lambda ps: by_e(ps[:, 0:NB * XN].rearrange("p (b e) -> p b e", e=XN))
            flat = lambda t: t[:].rearrange("p e b -> p (e b)")
            c.after(nc.vector.tensor_copy(tot[:], from_ps(ps_tot)))
            c.after(nc.vector.tensor_tensor_scan(flat(upto), flat(keep), flat(tot), 0.0, ALU.mult, ALU.add))
            c.after(ts(tiles[:], upto[:, :, NB - 1], float(P - 1), None, ALU.add))
            c.after(nc.vector.tensor_copy(tiles_i[:], tiles[:]))
            c.after(nc.vector.tensor_single_scalar(tiles_i[:], tiles_i[:], 7, ALU.arith_shift_right))
            c.after(nc.vector.tensor_copy(tiles[:], tiles_i[:]))
            c.after(nc.vector.tensor_tensor_scan(ends[:], tiles[:], zero[:], 0.0, ALU.add, ALU.add))
            c.after(tt(begin[:], ends[:], tiles[:], ALU.subtract))
            c.after(ts(begin[:], begin[:], float(P), -1.0, ALU.mult, ALU.add))
            c.after(tt(place[:], upto[:], tot[:], ALU.subtract))
            c.after(tt(place[:], place[:], begin[:].unsqueeze(2).to_broadcast([P, XN, NB]), ALU.add))
            c.after(tt(place[:], place[:], from_ps(ps_pre), ALU.add))
            c.after(tt(place[:], place[:], by_e(goes[:]), ALU.mult))
            c.after(nc.vector.tensor_reduce(slots[:, 1], place[:].rearrange("p e b -> p b e"), AX.X, ALU.max))
            c.after(nc.vector.scalar_tensor_tensor(out=place[:], in0=by_e(goes[:]), scalar=-BIG, in1=place[:],
                                                   op0=ALU.mult, op1=ALU.add))
            c.after(nc.vector.tensor_reduce(slots[:, 0], place[:].rearrange("p e b -> p b e"), AX.X, ALU.min))
            c.after(ts(slots[:, 0], slots[:, 0], BIG, None, ALU.add))
            c.after(nc.vector.tensor_copy(slots_i[:], slots[:]))
            c.after(nc.vector.tensor_single_scalar(lo_i[:], slots_i[:], P - 1, ALU.bitwise_and))
            c.after(nc.vector.tensor_single_scalar(hi_i[:], slots_i[:], 7, ALU.arith_shift_right))
            c.after(nc.vector.tensor_copy(lo[:], lo_i[:]))
            c.after(nc.vector.tensor_copy(hi[:], hi_i[:]))
            for r in range(2):
                tt(hot_lo[:, r], lo[:, r].unsqueeze(2).to_broadcast([P, NB, P]),
                   at_p[:, None, :].to_broadcast([P, NB, P]), ALU.is_equal).then_inc(s_hot, 1)
                c.after(tt(hot_hi[:, r], hi[:, r].unsqueeze(2).to_broadcast([P, NB, TX]),
                           at_t[:, None, :].to_broadcast([P, NB, TX]), ALU.is_equal))
                tt(hot_hi[:, r], hot_hi[:, r], node1[:].unsqueeze(2).to_broadcast([P, NB, TX]), ALU.mult
                   ).then_inc(s_hot, 1)
            c.after(tt(after[:], at_t[0:1].unsqueeze(2).to_broadcast([1, TX, XN - 1]),
                       ends[0:1, None, 0:XN - 1].to_broadcast([1, TX, XN - 1]), ALU.is_ge))
            c.after(nc.vector.tensor_reduce(expert[:], after[:], AX.X, ALU.add))
            c.after(nc.vector.tensor_copy(k["expert"][:], expert[:]))
            v.wait_ge(s_perm, 1)
            c.after(ts(none[:], ps_perm[:, 0:TX], 0.0, pad[:, 0:1], ALU.is_equal, ALU.mult))
            c.after(nc.vector.scalar_tensor_tensor(out=perm[:], in0=ps_perm[:, 0:TX], scalar=-1.0, in1=none[:],
                                                   op0=ALU.add, op1=ALU.add))
            c.after(nc.vector.tensor_copy(k["perm"][:], perm[:]))

        @block.tensor
        def _(te):
            te.wait_ge(s_goes, 1)
            goes_f = goes[:].rearrange("p b e -> p (b e)")
            nc.tensor.matmul(ps_pre[:, 0:NB * XN], k["tri"][:], goes_f, start=True, stop=True).then_inc(s_cum, 1)
            nc.tensor.matmul(ps_tot[:, 0:NB * XN], k["ones"][:], goes_f, start=True, stop=True).then_inc(s_cum, 1)
            for r in range(2):
                te.wait_ge(s_hot, 2 * r + 2)
                for b in range(NB):
                    mm = nc.tensor.matmul(ps_perm[:, 0:TX], hot_lo[:, r, b], hot_hi[:, r, b],
                                          start=(r == 0 and b == 0), stop=(r == 1 and b == NB - 1))
            mm.then_inc(s_perm, 1)


def experts(nc, a, tables, k):
    with ExitStack() as ctx:
        sb = lambda name, shape, dt=F32: ctx.enter_context(nc.sbuf_tensor("x_" + name, shape, dt))
        sem = lambda name: ctx.enter_context(nc.semaphore("x_" + name))
        ps = lambda name: ctx.enter_context(nc.psum_tensor("x_" + name, [P, 2, 512], F32))
        RING = 4
        gi, si = sb("gi", [P, RING], U32), sb("si", [P, 2], U32)
        zg, zT = sb("zg", [P, RING, D]), sb("zT", [P, 2, 2, P])
        pre, hid, y = sb("pre", [P, 2, XH]), sb("hid", [P, 2, XH]), sb("y", [P, 2, D])
        ps_z, ps_h, ps_t, ps_y = ps("ps_z"), ps("ps_h"), ps("ps_t"), ps("ps_y")
        s_gi, s_si, s_tz, s_zT, s_h, s_pre, s_th, s_hid, s_mm, s_y, s_add, s_out, s_ppassed = (
            sem(n) for n in ("gi", "si", "turnedZ", "zT", "h", "pre", "turnedH", "hid", "products", "y", "added",
                             "out", "ppassed"))
        s_g = [sem(f"gathered{i}") for i in range(RING)]
        block = ctx.enter_context(nc.Block())

        def has_second_next(j):
            return not isinstance(j, int) or j + 2 < TX

        def has_previous(j):
            return not isinstance(j, int) or j >= 1

        def expert_of(eng, j):
            col = slice(j, j + 1) if isinstance(j, int) else ds(j, 1)
            return eng.value_load(k["expert"][0:1, col], min_val=0, max_val=XN - 1)

        @block.gpsimd
        def _(pool):
            def column(j):
                return k["perm"][:, j:j + 1] if isinstance(j, int) else k["perm"][:, ds(j, 1)]

            def gather(j, s):
                nc.gpsimd.tensor_copy(gi[:, s:s + 1], column(j)).then_inc(s_gi, 1)
                wait_alone(pool, s_gi, j + 1, s_ppassed)
                nc.gpsimd.indirect_dma_start(zg[:, s], None, tables["z"],
                                             bass.IndirectOffsetOnAxis(gi[:, s:s + 1], 0)).then_inc(s_g[s], 16)

            def add(j, s):
                if has_previous(j):
                    wait_alone(pool, s_add, j * 16, s_ppassed)
                nc.gpsimd.tensor_copy(si[:, s:s + 1], column(j)).then_inc(s_si, 1)
                wait_alone(pool, s_si, j + 1, s_ppassed)
                wait_alone(pool, s_y, j + 1, s_ppassed)
                nc.gpsimd.indirect_dma_start(tables["acc"], bass.IndirectOffsetOnAxis(si[:, s:s + 1], 0),
                                             y[:, s], None, compute_op=ALU.add).then_inc(s_add, 16)

            def step(j, s, use):
                if not isinstance(j, int) or j + RING < TX:
                    pool.wait_ge(s_tz, j + 1)
                    gather(j + RING, s)
                if has_previous(j):
                    add(j - 1, 1 - s % 2)
            for j in range(RING):
                gather(j, j)
            each(pool, step, TX, RING)
            add(TX - 1, (TX - 1) % 2)

        @block.tensor
        def _(te):
            def turn_z(j, slot, use):
                s = slot % 2
                te.wait_ge(s_g[slot], use * 16)
                if later(j):
                    te.wait_ge(s_zT, j - 1)
                for c in range(2):
                    tr = nc.tensor.transpose(ps_z[:, s, c * P:(c + 1) * P], zg[:, slot, c * P:(c + 1) * P],
                                             k["ident"][:])
                tr.then_inc(s_tz, 1)

            def hidden(j, s):
                e = expert_of(te, j)
                te.wait_ge(s_zT, j + 1)
                if later(j):
                    te.wait_ge(s_pre, j - 1)
                for c in range(2):
                    mm = nc.tensor.matmul(ps_h[:, s, 0:XH], zT[:, s, c],
                                          k["w1"][:, ds(e, 1), c].rearrange("p o h -> p (o h)"),
                                          start=(c == 0), stop=(c == 1))
                mm.then_inc(s_h, 1)

            def turn_hidden(j, s):
                te.wait_ge(s_pre, j + 1)
                if later(j):
                    te.wait_ge(s_hid, j - 1)
                for c in range(HC):
                    tr = nc.tensor.transpose(ps_t[:, s, c * P:(c + 1) * P], pre[:, s, c * P:(c + 1) * P],
                                             k["ident"][:])
                tr.then_inc(s_th, 1)

            def outputs(j, s):
                e = expert_of(te, j)
                te.wait_ge(s_hid, j + 1)
                if later(j):
                    te.wait_ge(s_y, j - 1)
                for c in range(HC):
                    mm = nc.tensor.matmul(ps_y[:, s, 0:D], hid[:, s, c * P:(c + 1) * P],
                                          k["w2"][:, ds(e, 1), c].rearrange("p o d -> p (o d)"),
                                          start=(c == 0), stop=(c == HC - 1))
                mm.then_inc(s_mm, 1)

            def step(j, slot, use):
                s = slot % 2
                hidden(j, s)
                if has_previous(j):
                    outputs(j - 1, 1 - s)
                turn_hidden(j, s)
                if has_second_next(j):
                    turn_z(j + 2, (slot + 2) % RING, use + (slot + 2) // RING)
            turn_z(0, 0, 1)
            turn_z(1, 1, 1)
            each(te, step, TX, RING)
            outputs(TX - 1, (TX - 1) % 2)

        @block.scalar
        def _(act):
            def copy_z(j, s):
                act.wait_ge(s_tz, j + 1)
                if later(j):
                    act.wait_ge(s_h, j - 1)
                nc.scalar.copy(zT[:, s], ps_z[:, s, 0:D].rearrange("p (c n) -> p c n", c=2)).then_inc(s_zT, 1)

            def step(j, s, use):
                act.wait_ge(s_th, j + 1)
                if later(j):
                    act.wait_ge(s_mm, j - 1)
                nc.scalar.activation(hid[:, s], ps_t[:, s, 0:XH], ACT.Gelu).then_inc(s_hid, 1)
                if has_second_next(j):
                    copy_z(j + 2, s)
            copy_z(0, 0)
            copy_z(1, 1)
            each(act, step, TX)

        @block.vector
        def _(v):
            def results(j, s):
                e = expert_of(v, j)
                v.wait_ge(s_mm, j + 1)
                if later(j):
                    v.wait_ge(s_add, j * 16 - 16)
                nc.vector.tensor_tensor(y[:, s], ps_y[:, s, 0:D], k["b2"][:, ds(e, 1)].rearrange("p o d -> p (o d)"),
                                        ALU.add).then_inc(s_y, 1)

            def step(j, s, use):
                e = expert_of(v, j)
                v.wait_ge(s_h, j + 1)
                if later(j):
                    v.wait_ge(s_th, j - 1)
                nc.vector.tensor_tensor(pre[:, s], ps_h[:, s, 0:XH], k["b1"][:, ds(e, 1)].rearrange("p o h -> p (o h)"),
                                        ALU.add).then_inc(s_pre, 1)
                if has_previous(j):
                    results(j - 1, 1 - s)
            each(v, step, TX)
            results(TX - 1, (TX - 1) % 2)

        @block.sync
        def _(sp):
            sp.wait_ge(s_add, 16 * TX)
            sp.dma_start(a["out"], tables["acc"][0:N]).then_inc(s_out, 16)
            sp.wait_ge(s_out, 16)


def kernel(x, src, dst, edge_attr_194, **w):
    import concourse.bacc as bacc
    from concourse.bass_utils import run_bass_kernel_spmd

    g, f = (lambda n: np.asarray(w["L0_gnn_" + n])), (lambda n: np.asarray(w["L0_ffn_" + n]))
    x, src, dst, attr = (np.asarray(v) for v in (x, src, dst, edge_attr_194))
    src_p = np.concatenate([src, np.zeros(EDGES - E_REAL, src.dtype)])
    dst_p = np.concatenate([dst, np.full(EDGES - E_REAL, NP - 1, dst.dtype)])
    arrays = {
        "x": np.pad(x, ((0, NP - N), (0, 0))),
        "dst": dst_p,
        "dst_last": dst_p[P - 1::P],
        "dst_last_cols": dst_p[P - 1::P].reshape(CH, CR).T,
        "src_cols": src_p.reshape(T, P).T,
        "dst_cols": dst_p.reshape(T, P).T,
        "ft": np.pad(attr.T, ((0, 0), (0, EDGES - E_REAL))),
        "wg": f("Wg"), "bg": f("bg"), "b2": f("b2"), "w1x": f("W1"), "w2x": f("W2"),
        "b1": f("b1"),
    }
    for l in (1, 2):
        arrays[f"w{l}"] = np.concatenate([g(f"W{m}{l}") for m in "kvqs"], axis=1)
        arrays[f"bias{l}"] = np.concatenate([g(f"b{m}{l}") for m in "kvqs"])
        arrays[f"we{l}"] = g(f"We{l}")
    nc = bacc.Bacc("TRN2", target_bir_lowering=False, num_devices=1)
    arrays = {"in_" + n: np.ascontiguousarray(v) for n, v in arrays.items()}
    aps = {n[3:]: nc.dram_tensor(n, v.shape, mybir.dt.from_np(v.dtype), kind="ExternalInput").ap()
           for n, v in arrays.items()}
    aps["out"] = nc.dram_tensor("out", (N, D), F32, kind="ExternalOutput").ap()
    kernel_program(nc, aps)
    r = run_bass_kernel_spmd(nc, [arrays], core_ids=[0])
    return r.results[0]["out"]
```

```python
from contextlib import ExitStack

import numpy as np

import concourse.bass as bass
from concourse import mybir
from concourse.alu_op_type import AluOpType as ALU

P = 128
N, D, H, C = 3125, 256, 4, 64
NB = -(-N // P)
NP = NB * P
E_REAL, ED = 50000, 194
G = 14
PAIRS = G // 2
T = 392
HALVES = T // G
EDGES = T * P
ED0, ED1 = P, ED - P
ED1_MANY = 64
HW = C + 1
ROW = H * HW + H
MAXAT = H * HW
SLOT = 4 + 2 * D
KAT, VAT = 4, 4 + D
NULL = EDGES
CH, CR = 4, T // 4
XN, XH = 8, 512
HC = XH // P
TX = (2 * NP + XN * (P - 1)) // P
HUGE = 3e38
LOW = -1e30
INV = 1.0 / 8.0
EPS = 1e-5

ACT = mybir.ActivationFunctionType
AX = mybir.AxisListType
F32 = mybir.dt.float32
BF16 = mybir.dt.bfloat16
I32 = mybir.dt.int32
U32 = mybir.dt.uint32
ds = bass.ds


class Chain:

    def __init__(self, eng, sem, passed=None):
        self.eng, self.sem, self.passed, self.base, self.n = eng, sem, passed, 0, 0

    def after(self, ins, alone=False):
        ins.then_inc(self.sem, 1)
        self.n += 1
        if alone:
            wait_alone(self.eng, self.sem, self.base + self.n, self.passed)
        else:
            self.eng.wait_ge(self.sem, self.base + self.n)


def wait_alone(eng, sem, value, passed):
    eng.wait_ge(sem, value)
    eng.sem_inc(passed, 1)


def kernel_program(nc, a):
    with ExitStack() as ctx:
        dram = lambda name, shape: nc.dram_tensor(name, shape, F32, kind="Internal").ap()
        tables = {"kv": dram("kv_table", (NP, 2 * D)), "q": dram("q_table", (NP, D)),
                  "skip": dram("skip_table", (NP, D)), "part": dram("partials", (EDGES + 1 + T, ROW))}
        tables.update(z=dram("z_table", (NP + P, D)), acc=dram("acc_table", (NP + P, D)))
        keep = lambda name, shape, dt=F32: ctx.enter_context(nc.sbuf_tensor(name, shape, dt))
        k = {"ident": keep("ident", [P, P]), "tri": keep("tri", [P, P]), "ones": keep("ones", [P, P]),
             "rows": keep("rows", [P, NB, 2], U32),
             "chain_mask": keep("chain_mask", [CR, CH, T]), "chain_new": keep("chain_new", [H, T]),
             "head_row": keep("head_row", [H, H, CR])}
        edges = ctx.enter_context(ExitStack())
        flags = lambda name, shape, dt=F32: edges.enter_context(nc.sbuf_tensor(name, shape, dt))
        k.update(dst_col=flags("dst_col", [P, T]), new_fwd=flags("new_fwd", [4 * G, HALVES, P]),
                 new_bwd=flags("new_bwd", [4 * G, HALVES, P]))
        setup_and_first(nc, a, tables, k)
        edge_pass(nc, a, tables, k, 1)
        with ExitStack() as ahead:
            early = lambda name, shape: ahead.enter_context(nc.sbuf_tensor(name, shape, F32))
            k.update(skip=early("skip1", [P, NB, D]), w2nd=early("w2nd", [P, 2, 4 * D]),
                     bias2nd=early("bias2nd", [P, 4 * D]))
            chain_pass(nc, a, tables, k, 1, ((k["skip"], blocks(tables["skip"])),
                                             (k["w2nd"], a["w2"].rearrange("(c p) n -> p c n", p=P)),
                                             (k["bias2nd"], a["bias2"][None, :].to_broadcast([P, 4 * D]))))
            node_blocks(nc, a, tables, k, "middle")
        edge_pass(nc, a, tables, k, 2)
        edges.close()
        k.update(x1=keep("x1", [P, NB, D]), skip=keep("skip2", [P, NB, D]))
        chain_pass(nc, a, tables, k, 2, ((k["skip"], blocks(tables["skip"])), (k["x1"], blocks(a["x"]))),
                   add=(k["x1"], k["skip"]))
        k.update(w1=keep("w1", [P, XN, 2, XH]), w2=keep("w2", [P, XN, HC, D]), b1=keep("b1", [P, XN, XH]),
                 b2=keep("b2", [P, XN, D]), scores=keep("scores", [P, NB, XN]),
                 perm=keep("perm", [P, TX], U32), expert=keep("expert", [1, TX], I32))
        last_blocks(nc, a, tables, k)
        route(nc, k)
        experts(nc, a, tables, k)


def semaphores(nc, ctx, prefix):
    mine = []

    def clear():
        nc.clear_and_free_semaphores(mine)
        nc.all_engine_barrier()
    ctx.callback(clear)

    def sem(name):
        mine.append(nc.alloc_semaphore(prefix + name))
        return mine[-1]
    return sem


def setup_and_first(nc, a, tables, k):
    with ExitStack() as ctx:
        sb = lambda name, shape, dt=F32: ctx.enter_context(nc.sbuf_tensor("su_" + name, shape, dt))
        sem = lambda name: ctx.enter_context(nc.semaphore("su_" + name))
        dcol = sb("dcol", [P, T], I32)
        drow = sb("drow", [4 * G, HALVES, P], I32)
        node_i, node = sb("node_i", [P, NB], I32), sb("node", [P, NB])
        ends, ended = sb("ends", [P, T]), sb("ended", [P, 2, T])
        tile, idx = sb("tile", [P, NB]), sb("idx", [P, 2], U32)
        inside, upto = sb("inside", [P, 2, P], I32), sb("upto", [P, 2, P])
        part = sb("part", [P, NB])
        down, wrap = sb("down", [P, P]), sb("wrap", [P, P])
        cum = sb("cum", [P, NB + 1])
        cnt, g1, t1, t2 = sb("cnt", [P, NB]), sb("g1", [P, NB]), sb("t1", [P, NB]), sb("t2", [P, NB])
        ti, tf = sb("ti", [P, NB], I32), sb("tf", [P, NB])
        null = sb("null", [1, ROW])
        dlb, dlc = sb("dlb", [P, T], I32), sb("dlc", [CR, CH], I32)
        same = sb("same", [CR, CH, T])
        ps = ctx.enter_context(nc.psum_tensor("su_ps", [P, 512], F32))
        s_last, s_in, s_pool, s_v, s_ended, s_flags, s_idx, s_counted, s_cum, s_prev, s_null, s_nulled, s_ppassed = (
            sem(n) for n in ("lastLoaded", "loaded", "pool", "vec", "ended", "flags", "idx", "counted", "cum",
                             "prev", "null", "nulled", "ppassed"))
        s_rows = [sem(f"rows{i}") for i in range(2)]
        FLAGS = 2

        def at(j):
            return slice(j, j + 1) if isinstance(j, int) else ds(j, 1)

        def load_last(sp):
            sp.dma_start(dlb[:], a["dst_last"][None, :].to_broadcast([P, T])).then_inc(s_last, 16)
            sp.dma_start(dlc[:], a["dst_last_cols"]).then_inc(s_last, 16)

        def load(sp):
            for h in range(H):
                sp.dma_start(drow[h * G:(h + 1) * G], a["dst"][0:EDGES].rearrange("(u t e) -> t u e", t=G, e=P)
                             ).then_inc(s_in, 16)
            sp.dma_start(dcol[:], a["dst_cols"]).then_inc(s_in, 16)

        def store(sp):
            sp.wait_ge(s_null, 2)
            sp.dma_start(tables["part"][NULL:NULL + 1], null[:]).then_inc(s_nulled, 16)
            sp.wait_ge(s_nulled, 16)

        def pool_work(pool):
            c = Chain(pool, s_pool)
            c.after(nc.gpsimd.memset(k["ident"][:], 0.0))
            c.after(nc.gpsimd.affine_select(out=k["ident"][:], in_=k["ident"][:], compare_op=ALU.not_equal,
                                            fill=1.0, base=0, pattern=[[-1, P]], channel_multiplier=1))
            c.after(nc.gpsimd.iota(node_i[:], pattern=[[P, NB]], base=0, channel_multiplier=1,
                                   allow_small_or_imprecise_dtypes=True))
            c.after(nc.gpsimd.memset(k["chain_mask"][:], 1.0))
            c.after(nc.gpsimd.affine_select(out=k["chain_mask"][:], in_=k["chain_mask"][:],
                                            compare_op=ALU.is_ge, fill=0.0, base=0,
                                            pattern=[[-CR, CH], [1, T]], channel_multiplier=-1))
            c.after(nc.gpsimd.memset(k["ones"][:], 1.0))
            c.after(nc.gpsimd.affine_select(out=k["tri"][:], in_=k["ones"][:], compare_op=ALU.is_ge, fill=0.0,
                                            base=0, pattern=[[1, P]], channel_multiplier=-1))
            c.after(nc.gpsimd.memset(down[:], 0.0))
            c.after(nc.gpsimd.affine_select(out=down[:], in_=down[:], compare_op=ALU.not_equal, fill=1.0,
                                            base=1, pattern=[[-1, P]], channel_multiplier=1))
            c.after(nc.gpsimd.memset(wrap[:], 0.0))
            c.after(nc.gpsimd.affine_select(out=wrap[:], in_=wrap[:], compare_op=ALU.not_equal, fill=1.0,
                                            base=-(P - 1), pattern=[[-1, P]], channel_multiplier=1))
            c.after(nc.gpsimd.memset(k["head_row"][:], 0.0))
            c.after(nc.gpsimd.affine_select(out=k["head_row"][:], in_=k["head_row"][:], compare_op=ALU.not_equal,
                                            fill=1.0, base=0, pattern=[[-1, H], [0, CR]], channel_multiplier=1))
            assert c.n == 13

            def step(j, s, use):
                pool.wait_ge(s_ended, j + 1)
                if later(j):
                    pool.wait_ge(s_counted, j - 1)
                nc.gpsimd.tensor_copy(idx[:, s:s + 1], tile[:, at(j)]).then_inc(s_idx, 1)
                wait_alone(pool, s_idx, j + 1, s_ppassed)
                nc.gpsimd.indirect_dma_start(inside[:, s], None, a["dst"].rearrange("(t e) -> t e", e=P),
                                             bass.IndirectOffsetOnAxis(idx[:, s:s + 1], 0)).then_inc(s_rows[s], 16)
            each(pool, step)

        def vector_start(v):
            c = Chain(v, s_v)
            nc.vector.memset(null[:, 0:MAXAT], 0.0).then_inc(s_null, 1)
            nc.vector.memset(null[:, MAXAT:ROW], LOW).then_inc(s_null, 1)
            nc.vector.memset(k["new_fwd"][:, :, 0:1], 0.0)
            nc.vector.memset(k["new_bwd"][:, :, 0:1], 0.0)
            nc.vector.memset(k["chain_new"][:, 0:1], 0.0)
            c.after(nc.vector.memset(cum[:, 0:1], 0.0))
            v.wait_ge(s_pool, 3)
            c.after(nc.vector.tensor_copy(node[:], node_i[:]))
            v.wait_ge(s_last, 32)
            c.after(nc.vector.tensor_copy(ends[:], dlb[:]))
            c.after(nc.vector.tensor_tensor(same[:], dlb[0:CR, None, :].to_broadcast([CR, CH, T]),
                                            dlc[:].unsqueeze(2).to_broadcast([CR, CH, T]), ALU.is_equal))
            v.wait_ge(s_pool, 5)
            c.after(nc.vector.tensor_tensor(k["chain_mask"][:], k["chain_mask"][:], same[:], ALU.mult))
            c.after(nc.vector.tensor_tensor(k["chain_new"][:, 1:T], dlb[0:H, 1:T], dlb[0:H, 0:T - 1],
                                            ALU.not_equal))
            c.after(nc.vector.tensor_scalar(k["chain_new"][:, 1:T], k["chain_new"][:, 1:T], LOW, None, ALU.mult))
            return c

        def count_inside(v, j, s, use):
            v.wait_ge(s_rows[s], use * 16)
            nc.vector.tensor_scalar(upto[:, s], inside[:, s], node[:, at(j)], 0.0, ALU.is_le, ALU.add,
                                    accum_out=part[:, at(j)]).then_inc(s_counted, 1)

        def flags(v, u, n, base):
            c = Chain(v, s_flags)
            c.base = base
            halves = slice(u, u + n) if isinstance(u, int) else ds(u, n)
            fwd = k["new_fwd"][:, halves, 1:P]
            c.after(nc.vector.tensor_tensor(fwd, drow[:, halves, 1:P], drow[:, halves, 0:P - 1], ALU.not_equal))
            c.after(nc.vector.tensor_scalar(fwd, fwd, LOW, None, ALU.mult))
            assert c.n == FLAGS

        def vector_step(v, j, s, use):
            if isinstance(j, int) and j == 0:
                v.wait_ge(s_in, 16 * 5)
            if later(j):
                v.wait_ge(s_ended, j - 1)
            nc.vector.tensor_scalar(ended[:, s], ends[:], node[:, at(j)], 0.0, ALU.is_le, ALU.add,
                                    accum_out=tile[:, at(j)]).then_inc(s_ended, 1)
            flags(v, j, 1, j * FLAGS)
            if later(j):
                count_inside(v, j - 2, s, use - 1)

        def vector_end(v, c):
            count_inside(v, NB - 2, 1, NB // 2)
            count_inside(v, NB - 1, 0, NB // 2 + 1)
            flags(v, NB, HALVES - NB, NB * FLAGS)
            v.wait_ge(s_counted, NB)
            v.wait_ge(s_ended, NB)
            nc.vector.scalar_tensor_tensor(out=cum[:, 1:NB + 1], in0=tile[:], scalar=float(P), in1=part[:],
                                           op0=ALU.mult, op1=ALU.add).then_inc(s_cum, 1)
            c.after(nc.vector.tensor_copy(k["dst_col"][:], dcol[:]))
            c.after(nc.vector.tensor_copy(k["new_bwd"][:, :, 1:P], k["new_fwd"][:, :, P - 1:0:-1]))
            v.wait_ge(s_prev, 1)
            c.after(nc.vector.tensor_tensor(cnt[:], cum[:, 1:NB + 1], ps[:, 0:NB], ALU.subtract))
            c.after(nc.vector.tensor_scalar(g1[:], cnt[:], 0.0, None, ALU.is_gt))
            c.after(nc.vector.tensor_scalar(t1[:], cum[:, 1:NB + 1], -1.0, None, ALU.add))
            c.after(nc.vector.tensor_scalar(t1[:], t1[:], -float(NULL), None, ALU.add))
            c.after(nc.vector.tensor_tensor(t1[:], t1[:], g1[:], ALU.mult))
            c.after(nc.vector.tensor_scalar(t1[:], t1[:], float(NULL), None, ALU.add))
            c.after(nc.vector.tensor_copy(k["rows"][:, :, 0], t1[:]))
            c.after(nc.vector.tensor_scalar(t2[:], cum[:, 1:NB + 1], -1.0, 0.0, ALU.add, ALU.max))
            c.after(nc.vector.tensor_copy(ti[:], t2[:]))
            c.after(nc.vector.tensor_single_scalar(ti[:], ti[:], 7, ALU.arith_shift_right))
            c.after(nc.vector.tensor_copy(tf[:], ti[:]))
            c.after(nc.vector.scalar_tensor_tensor(out=t2[:], in0=tf[:], scalar=float(P), in1=ps[:, 0:NB],
                                                   op0=ALU.mult, op1=ALU.is_gt))
            c.after(nc.vector.tensor_tensor(t2[:], t2[:], g1[:], ALU.mult))
            c.after(nc.vector.tensor_tensor(t2[:], t2[:], tf[:], ALU.mult))
            c.after(nc.vector.tensor_scalar(t2[:], t2[:], float(NULL), None, ALU.add))
            c.after(nc.vector.tensor_copy(k["rows"][:, :, 1], t2[:]))

        def tensor_start(te):
            te.wait_ge(s_pool, 2)

        def tensor_end(te):
            te.wait_ge(s_cum, 1)
            te.wait_ge(s_pool, 13)
            nc.tensor.matmul(ps[:, 0:NB], down[:], cum[:, 1:NB + 1], start=True, stop=False)
            nc.tensor.matmul(ps[:, 0:NB], wrap[:], cum[:, 0:NB], start=False, stop=True).then_inc(s_prev, 1)

        node_blocks(nc, a, tables, k, "first", {
            "load_last": load_last, "load": load, "store": store, "pool_work": pool_work, "vector_start": vector_start,
            "vector_step": vector_step, "vector_end": vector_end, "tensor_start": tensor_start,
            "tensor_end": tensor_end})


def each(eng, step, n=NB, ring=2, peel=1):
    for j in range(peel * ring + 1):
        step(j, j % ring, j // ring + 1)
    with eng.Fori(peel, (n - 1) // ring - 1) as it:
        for i in range(ring):
            step(it * ring + (1 + i), (1 + i) % ring, it + ((1 + i) // ring + 1))
    for j in range(n - ring, n):
        step(j, j % ring, j // ring + 1)


def later(j, ring=2):
    return not isinstance(j, int) or j >= ring


def block_of(ap, j):
    if isinstance(j, int):
        return ap[:, j]
    return ap[:, ds(j, 1)].rearrange("p o d -> p (o d)")


def blocks(table):
    return table.rearrange("(b p) d -> p b d", p=P)


def rows_of(table, j):
    return table[ds(j * P, P)] if not isinstance(j, int) else table[j * P:(j + 1) * P]


def node_blocks(nc, a, tables, k, kind, beside=None):
    gather, norm = kind == "middle", kind == "first"
    with ExitStack() as ctx:
        sb = lambda name, shape, dt=F32: ctx.enter_context(nc.sbuf_tensor(kind + "_" + name, shape, dt))
        sem = lambda name: ctx.enter_context(nc.semaphore(kind + "_" + name))
        ps_turn = ctx.enter_context(nc.psum_tensor(kind + "_turn", [P, 2, 512], F32))
        ps_out = ctx.enter_context(nc.psum_tensor(kind + "_out", [P, 2, 2, 512], F32))
        z, zT = sb("z", [P, 2, D]), sb("zT", [P, 2, 2, P])
        s_w, s_vec, s_z, s_turn, s_zT, s_mm, s_out = (
            sem(n) for n in ("weights", "vec", "z", "turned", "zT", "products", "outs"))
        s_in = [sem(f"in{i}") for i in range(2)]
        s_passed, s_ppassed = sem("passed"), sem("ppassed")
        if gather:
            skip, part = k["skip"], sb("part", [P, 2, 2, ROW])
            idx = sb("idx", [P, 2, 2], U32)
            mx, dm, sc = sb("mx", [P, H]), sb("dm", [P, 2, H]), sb("sc", [P, 2, H])
            scaled, den = sb("scaled", [P, 2, H, HW]), sb("den", [P, H])
            joined = sb("joined", [P, D])
            s_idx, s_dm, s_sc = sem("idx"), sem("dm"), sem("sc")
            s_part = [sem(f"part{i}") for i in range(2)]
        if norm:
            xin = sb("x", [P, NB, D])
            stats, mv, rs, std = sb("stats", [P, 6]), sb("mv", [P, 2]), sb("rs", [P, 1]), sb("std", [P, 1])
            s_var, s_std = sem("var"), sem("std")
        w, bias = (sb("w", [P, 2, 4 * D]), sb("bias", [P, 4 * D])) if norm else (k["w2nd"], k["bias2nd"])
        outs = sb("outs", [P, 2, 4 * D])
        s_st = [sem(f"stored{i}") for i in range(2)]
        FRONT = {"first": 3, "middle": 6}[kind]
        block = ctx.enter_context(nc.Block())

        @block.sync
        def _(sp):
            if norm:
                beside["load_last"](sp)
                sp.dma_start(xin[:, 0:3], blocks(a["x"])[:, 0:3]).then_inc(s_in[0], 16)
                sp.dma_start(w[:], a["w1"].rearrange("(c p) n -> p c n", p=P)).then_inc(s_w, 16)
                sp.dma_start(bias[:], a["bias1"][None, :].to_broadcast([P, 4 * D])).then_inc(s_w, 16)
                beside["load"](sp)
                sp.dma_start(xin[:, 3:NB], blocks(a["x"])[:, 3:NB]).then_inc(s_in[1], 16)

            def store(j, s):
                sp.wait_ge(s_out, j + 1)
                for t, c0, c1 in (("kv", 0, 2 * D), ("q", 2 * D, 3 * D), ("skip", 3 * D, 4 * D)):
                    sp.dma_start(rows_of(tables[t], j), outs[:, s, c0:c1]).then_inc(s_st[s], 16)

            each(sp, lambda j, s, use: store(j, s))
            sp.wait_ge(s_st[0], 48 * (NB // 2 + 1))
            sp.wait_ge(s_st[1], 48 * (NB // 2))
            if beside:
                beside["store"](sp)

        @block.gpsimd
        def _(pool):
            if beside:
                beside["pool_work"](pool)
            if gather:
                def step(j, s, use):
                    if later(j):
                        pool.wait_ge(s_vec, j * FRONT - (2 * FRONT - 2))
                    col = slice(j, j + 1) if isinstance(j, int) else ds(j, 1)
                    nc.gpsimd.tensor_copy(idx[:, s], k["rows"][:, col].rearrange("p o r -> p (o r)")
                                          ).then_inc(s_idx, 1)
                    wait_alone(pool, s_idx, j + 1, s_ppassed)
                    for r in range(2):
                        nc.gpsimd.indirect_dma_start(
                            part[:, s, r], None, tables["part"],
                            bass.IndirectOffsetOnAxis(idx[:, s, r:r + 1], 0)).then_inc(s_part[s], 16)
                each(pool, step)

        @block.vector
        def _(v):
            c = Chain(v, s_vec, s_passed)

            def begin(j, s, use):
                c.base, c.n = j * FRONT, 0
                if norm:
                    if isinstance(j, int) and j == 0:
                        v.wait_ge(s_in[0], 16)
                    c.after(nc.vector.bn_stats(stats[:], block_of(xin, j)), alone=True)
                    c.after(nc.vector.bn_aggr(mv[:], stats[:]))
                    nc.vector.tensor_scalar(rs[:], mv[:, 1:2], EPS, None, ALU.add).then_inc(s_var, 1)
                else:
                    v.wait_ge(s_part[s], use * 32)
                    c.after(nc.vector.tensor_tensor(mx[:], part[:, s, 0, MAXAT:ROW], part[:, s, 1, MAXAT:ROW],
                                                    ALU.max))
                    nc.vector.tensor_tensor(dm[:], part[:, s, :, MAXAT:ROW],
                                            mx[:, None, :].to_broadcast([P, 2, H]), ALU.subtract
                                            ).then_inc(s_dm, 1)

            def finish(j, s, use):
                if later(j):
                    v.wait_ge(s_turn, j - 1)
                if gather:
                    v.wait_ge(s_sc, j + 1)
                    c.after(nc.vector.tensor_tensor(
                        scaled[:], part[:, s, :, 0:MAXAT].rearrange("p r (h c) -> p r h c", h=H),
                        sc[:].unsqueeze(3).to_broadcast([P, 2, H, HW]), ALU.mult))
                    c.after(nc.vector.tensor_tensor(scaled[:, 0], scaled[:, 0], scaled[:, 1], ALU.add))
                    c.after(nc.vector.tensor_scalar(den[:], scaled[:, 0, :, C], 1e-16, None, ALU.add))
                    c.after(nc.vector.reciprocal(den[:], den[:]))
                    c.after(nc.vector.tensor_tensor(
                        joined[:].rearrange("p (h c) -> p h c", h=H), scaled[:, 0, :, 0:C],
                        den[:].unsqueeze(2).to_broadcast([P, H, C]), ALU.mult))
                    nc.vector.tensor_tensor(z[:, s], joined[:], block_of(skip, j), ALU.add).then_inc(s_z, 1)
                else:
                    v.wait_ge(s_std, j + 1)
                    c.after(nc.vector.reciprocal(rs[:], std[:]))
                    nc.vector.tensor_scalar(z[:, s], block_of(xin, j), mv[:, 0:1], rs[:, 0:1], ALU.subtract, ALU.mult
                                            ).then_inc(s_z, 1)
                assert c.n == FRONT, c.n

            def back(j, s, use):
                v.wait_ge(s_mm, j + 1)
                if later(j):
                    v.wait_ge(s_st[s], (use - 1) * 48)
                nc.vector.tensor_tensor(outs[:, s], ps_out[:, s].rearrange("p b n -> p (b n)"), bias[:], ALU.add
                                        ).then_inc(s_out, 1)
                if beside:
                    beside["vector_step"](v, j, s, use)

            own = beside["vector_start"](v) if beside else None
            def blocks_on(j, s, use):
                begin(j, s, use)
                if later(j, 3):
                    back(j - 3, 1 - s, use - 2 + s)
                finish(j, s, use)
                if norm and isinstance(j, int) and j == 1:
                    v.wait_ge(s_w, 32)
                    v.wait_ge(s_in[1], 16)
            each(v, blocks_on, peel=2)
            for j in range(NB - 3, NB):
                back(j, j % 2, j // 2 + 1)
            if beside:
                beside["vector_end"](v, own)

        @block.scalar
        def _(act):
            def step(j, s, use):
                if gather:
                    act.wait_ge(s_dm, j + 1)
                    nc.scalar.activation(sc[:], dm[:], ACT.Exp, scale=INV).then_inc(s_sc, 1)
                if norm:
                    act.wait_ge(s_var, j + 1)
                    nc.scalar.activation(std[:], rs[:], ACT.Sqrt).then_inc(s_std, 1)
                act.wait_ge(s_turn, j + 1)
                turned = ps_turn[:, s, 0:D].rearrange("p (c n) -> p c n", c=2)
                if later(j):
                    act.wait_ge(s_mm, j - 1)
                nc.scalar.activation(zT[:, s], turned, ACT.Relu if kind == "middle" else ACT.Copy
                                     ).then_inc(s_zT, 1)
            each(act, step)

        @block.tensor
        def _(te):
            def turn(j, s):
                te.wait_ge(s_z, j + 1)
                if later(j):
                    te.wait_ge(s_zT, j - 1)
                nc.tensor.transpose(ps_turn[:, s, 0:P], z[:, s, 0:P], k["ident"][:])
                nc.tensor.transpose(ps_turn[:, s, P:D], z[:, s, P:D], k["ident"][:]).then_inc(s_turn, 1)

            def products(j, s):
                te.wait_ge(s_zT, j + 1)
                if later(j):
                    te.wait_ge(s_out, j - 1)
                for b in range(2):
                    for c in range(2):
                        mm = nc.tensor.matmul(ps_out[:, s, b], zT[:, s, c], w[:, c, b * 512:(b + 1) * 512],
                                              start=(c == 0), stop=(c == 1))
                mm.then_inc(s_mm, 1)

            if norm:
                te.wait_ge(s_w, 32)
                beside["tensor_start"](te)
            turn(0, 0)
            turn(1, 1)
            products(0, 0)
            turn(2, 0)
            products(1, 1)
            turn(3, 1)
            products(2, 0)
            with te.Fori(1, (NB - 1) // 2 - 1) as it:
                turn(it * 2 + 2, 0)
                products(it * 2 + 1, 1)
                turn(it * 2 + 3, 1)
                products(it * 2 + 2, 0)
            turn(NB - 1, 0)
            products(NB - 2, 1)
            products(NB - 1, 0)
            if beside:
                beside["tensor_end"](te)


def edge_pass(nc, a, tables, k, layer):
    with ExitStack() as ctx:
        nm = f"e{layer}_"
        sb = lambda name, shape, dt=F32: ctx.enter_context(nc.sbuf_tensor(nm + name, shape, dt))
        sem = semaphores(nc, ctx, nm)
        ps = lambda name, shape: ctx.enter_context(nc.psum_tensor(nm + name, shape, F32))
        ps_e = ps("ps_e", [P, 2, 2, D])
        ps_s = ps("ps_s", [P, 2, 2, 512])
        ps_l, ps_m = ps("ps_l", [P, 512]), ps("ps_m", [P, 512])
        we = sb("we", [P, 2, D])
        ft = sb("ft", [P, 2, 2, G * P])
        si, qi = sb("si", [P, 2, G], I32), sb("qi", [P, 2, G], I32)
        drow = sb("drow", [P, 2, G * P], I32)
        work = sb("work", [P, 2, G, SLOT])
        qg, prod = sb("qg", [P, PAIRS, 2, D]), sb("prod", [P, 2, 2, D])
        lg, mT = sb("lg", [P, 2, H, G]), sb("mT", [4 * G, 2, P])
        diff = sb("diff", [P, H, G])
        seg = sb("seg", [P, 2, 2, P])
        res = sb("res", [P, 2, G, ROW])
        s_w, s_zero, s_e, s_ee, s_prod, s_lg, s_lT, s_scan, s_mT, s_diff, s_w8, s_seg, s_wv, s_sum, s_res, s_max, s_mcol = (
            sem(n) for n in ("weights", "zeroed", "e", "eInSbuf", "prod", "logits", "turned", "scan", "maxT",
                             "diff", "expw", "seg", "weighted", "sums", "res", "maxBack", "maxcol"))
        s_ld = [sem(f"loaded{i}") for i in range(2)]
        s_tpassed, s_ppassed = sem("tpassed"), sem("ppassed")
        s_zero2 = sem("zeroedToo")
        s_dr = [sem(f"drow{i}") for i in range(2)]
        s_g = [sem(f"gathered{i}") for i in range(PAIRS)]
        s_st = [sem(f"stored{i}") for i in range(2)]
        block = ctx.enter_context(nc.Block())
        LD = 16 * (2 * PAIRS + 1)
        AHEAD = 3
        s_first, s_index = sem("firstLoaded"), [sem(f"index{i}") for i in range(2)]
        FIRST = 2

        def loaded(par, half2):
            return half2 * LD + (LD - (16 * (2 * FIRST + 1) if par == 0 else 0))

        def stages(eng, stage):
            stage(0, 0, 0, True, False)
            stage(1, 1, 0, True, True)
            stage(2, 0, 1, True, True)
            with eng.Fori(1, HALVES // 2 - 1) as i:
                stage(i * 2 + 1, 1, i, True, True)
                stage(i * 2 + 2, 0, i + 1, True, True)
            stage(HALVES - 1, 1, HALVES // 2 - 1, True, True)
            stage(HALVES, 0, HALVES // 2, False, True)

        def stored(par, half2):
            return half2 - 1 if par == 0 else half2

        def has_next(u):
            return not (isinstance(u, int) and u == HALVES - 1)

        def pair_slot(par, p):
            return (PAIRS * par + p) % 2

        @block.sync
        def _(sp):
            def cols(ap, u, step, lo, n):
                return ap[:, u * step + lo:u * step + lo + n] if isinstance(u, int) else ap[:, ds(u * step + lo, n)]

            def load_index(u, par):
                sp.dma_start(qi[:, par], cols(a["dst_cols"], u, G, 0, G)).then_inc(s_index[par], 16)
                sp.dma_start(si[:, par], cols(a["src_cols"], u, G, 0, G)).then_inc(s_index[par], 16)

            def load(u, par, parts):
                begins = isinstance(u, int) and u == 0
                if 0 in parts and not begins:
                    load_index(u, par)
                for p in parts:
                    lo, n = p * 2 * P, 2 * P
                    signal = s_first if begins and p < FIRST else s_ld[par]
                    src = lambda r0, r1: cols(a["ft"][r0:r1], u, G * P, lo, n)
                    sp.dma_start(ft[:, par, 0, lo:lo + n], src(0, ED0)).then_inc(signal, 16)
                    sp.dma_start(ft[0:ED1_MANY, par, 1, lo:lo + n], src(ED0, ED0 + ED1_MANY)).then_inc(signal, 16)
                    if p == 0:
                        sp.dma_start(ft[ED1_MANY:ED1, par, 1], cols(a["ft"][ED0 + ED1_MANY:ED], u, G * P, 0, G * P)
                                     ).then_inc(s_first if begins else signal, 16)

            def stage(u, par, half2, has_a, has_c):
                if isinstance(u, int) and u == 0:
                    load_index(0, 0)
                    w_dram = a[f"we{layer}"]
                    sp.wait_ge(s_zero, 2)
                    sp.dma_start(we[:, 0], w_dram[0:ED0]).then_inc(s_w, 16)
                    sp.dma_start(we[0:ED1, 1], w_dram[ED0:ED]).then_inc(s_w, 16)
                    load(0, 0, range(PAIRS))
                    sp.wait_ge(s_zero2, 1)
                if has_c:
                    sp.wait_ge(s_lg, u * PAIRS)
                for p in range(PAIRS):
                    if has_a and has_next(u) and 2 * p < PAIRS:
                        load(u + 1, 1 - par, range(2 * p, min(2 * p + 2, PAIRS)))
                    if has_a:
                        if p == 0 and not (isinstance(u, int) and u < 2):
                            sp.wait_ge(s_seg, (u - 1) * PAIRS)
                        lo, n = p * 2 * P, 2 * P
                        row = a["dst"][u * G * P + lo:u * G * P + lo + n] if isinstance(u, int) else a["dst"][
                            ds(u * (G * P) + lo, n)]
                        sp.dma_start(drow[:, par, lo:lo + n], row[None, :].to_broadcast([P, n])
                                     ).then_inc(s_dr[par], 16)
                    if has_c:
                        sp.wait_ge(s_res, (u - 1) * PAIRS + (p + 1))
                        if p == 0:
                            sp.wait_ge(s_mcol, u)
                        lo, n = (u - 1) * (G * P) + p * 2 * P, 2 * P
                        rows = tables["part"][lo:lo + n] if isinstance(u, int) else tables["part"][ds(lo, n)]
                        sp.dma_start(rows.rearrange("(t p) w -> p t w", p=P), res[:, 1 - par, 2 * p:2 * p + 2]
                                     ).then_inc(s_st[1 - par], 16)

            stages(sp, stage)
            for i in range(2):
                sp.wait_ge(s_st[i], 16 * PAIRS * (HALVES // 2))

        @block.gpsimd
        def _(pool):
            nc.gpsimd.memset(we[:], 0.0).then_inc(s_zero, 1)

            def q_rows(u, par, p):
                pair = u * PAIRS + p
                if not isinstance(u, int) or pair >= PAIRS:
                    wait_alone(pool, s_prod, pair - (PAIRS - 1), s_ppassed)
                for i in range(2):
                    nc.gpsimd.indirect_dma_start(
                        qg[:, p, i], None, tables["q"],
                        bass.IndirectOffsetOnAxis(qi[:, par, 2 * p + i:2 * p + i + 1].bitcast(U32), 0)
                    ).then_inc(s_g[p], 16)

            def kv_rows(u, par, p):
                wait_alone(pool, s_ee, u * PAIRS + (p + 1), s_ppassed)
                for i in range(2):
                    nc.gpsimd.indirect_dma_start(
                        work[:, par, 2 * p + i, KAT:SLOT], None, tables["kv"],
                        bass.IndirectOffsetOnAxis(si[:, par, 2 * p + i:2 * p + i + 1].bitcast(U32), 0),
                        compute_op=ALU.add).then_inc(s_g[p], 16)

            def stage(u, par, half2, has_a, has_c):
                if not has_a:
                    return
                if isinstance(u, int) and u == 0:
                    pool.wait_ge(s_index[0], 32)
                    for p in range(AHEAD):
                        q_rows(0, 0, p)
                for p in range(PAIRS):
                    kv_rows(u, par, p)
                    if p + AHEAD < PAIRS:
                        q_rows(u, par, p + AHEAD)
                    elif has_next(u):
                        if p + AHEAD == PAIRS:
                            wait_alone(pool, s_index[1 - par], half2 * 32 + (32 + 32 * par), s_ppassed)
                        q_rows(u + 1, 1 - par, p + AHEAD - PAIRS)

            stages(pool, stage)

        @block.tensor
        def _(te):
            te.wait_ge(s_w, 32)

            def features(u, par, half2, p):
                pair = u * PAIRS + p
                if not isinstance(u, int) or pair >= 2:
                    te.wait_ge(s_ee, pair - 1)
                for i in range(2):
                    t = 2 * p + i
                    for c in range(2):
                        mm = nc.tensor.matmul(ps_e[:, pair_slot(par, p), i], ft[:, par, c, t * P:(t + 1) * P],
                                              we[:, c], start=(c == 0), stop=(c == 1))
                mm.then_inc(s_e, 1)

            def sums(u, par, p):
                pair = (u - 1) * PAIRS + p
                slot = pair_slot(1 - par, p)
                te.wait_ge(s_seg, pair + 1)
                te.wait_ge(s_wv, pair + 1)
                if not isinstance(u, int) or pair >= 2:
                    te.wait_ge(s_res, pair - 1)
                for i in range(2):
                    mm = nc.tensor.matmul(ps_s[:, slot, i, 0:MAXAT], seg[:, slot, i],
                                          work[:, 1 - par, 2 * p + i, 0:MAXAT], start=True, stop=True)
                mm.then_inc(s_sum, 1)

            def stage(u, par, half2, has_a, has_c):
                if isinstance(u, int) and u == 0:
                    te.wait_ge(s_first, 16 * (2 * FIRST + 1))
                    features(0, 0, 0, 0)
                    features(0, 0, 0, 1)
                    te.wait_ge(s_ld[0], loaded(0, 0))
                if has_c:
                    wait_alone(te, s_lg, u * PAIRS, s_tpassed)
                    nc.tensor.transpose(ps_l[0:4 * G, 0:P], lg[:, 1 - par].rearrange("p h t -> p (h t)"),
                                        k["ident"][:]).then_inc(s_lT, 1)
                    te.wait_ge(s_mcol, u - 1)
                    wait_alone(te, s_mT, u, s_tpassed)
                    nc.tensor.transpose(ps_m[:, 0:4 * G], mT[:, 1], k["ident"][0:4 * G, 0:4 * G]).then_inc(s_max, 1)
                for p in range(PAIRS):
                    if has_a and p + 2 < PAIRS:
                        features(u, par, half2, p + 2)
                    elif has_a and has_next(u):
                        if p + 2 == PAIRS:
                            te.wait_ge(s_ld[1 - par], loaded(1 - par, half2 + par))
                        features(u + 1, 1 - par, half2 + par, p + 2 - PAIRS)
                    if has_c:
                        sums(u, par, p)

            stages(te, stage)

        @block.scalar
        def _(act):
            def copy_e(u, par, p):
                pair = u * PAIRS + p
                act.wait_ge(s_e, pair + 1)
                if not isinstance(u, int) or u >= 2:
                    act.wait_ge(s_sum, pair - 2 * PAIRS + 1)
                nc.scalar.copy(
                    work[:, par, 2 * p:2 * p + 2, KAT:SLOT].rearrange("p t (o d) -> p t o d", o=2),
                    ps_e[:, pair_slot(par, p), :, None, :].to_broadcast([P, 2, 2, D])).then_inc(s_ee, 1)

            def stage(u, par, half2, has_a, has_c):
                if isinstance(u, int) and u == 0:
                    copy_e(0, 0, 0)
                    copy_e(0, 0, 1)
                if has_c:
                    act.wait_ge(s_diff, u)
                    nc.scalar.activation(work[:, 1 - par, :, C:MAXAT:HW], diff[:].rearrange("p h t -> p t h"),
                                         ACT.Exp, scale=INV).then_inc(s_w8, 1)
                for p in range(PAIRS):
                    if has_a and p + 2 < PAIRS:
                        copy_e(u, par, p + 2)
                    elif has_a and has_next(u):
                        copy_e(u + 1, 1 - par, p + 2 - PAIRS)
                    if has_c:
                        pair = (u - 1) * PAIRS + p
                        act.wait_ge(s_sum, pair + 1)
                        if p == 0 and not (isinstance(u, int) and u < 3):
                            act.wait_ge(s_st[1 - par], stored(par, half2) * (16 * PAIRS))
                        nc.scalar.copy(res[:, 1 - par, 2 * p:2 * p + 2, 0:MAXAT],
                                       ps_s[:, pair_slot(1 - par, p), :, 0:MAXAT]).then_inc(s_res, 1)

            stages(act, stage)

        @block.vector
        def _(v):
            nc.vector.memset(ft[:, 0, 1], 0.0).then_inc(s_zero, 1)
            nc.vector.memset(ft[:, 1, 1], 0.0).then_inc(s_zero2, 1)

            def logits(u, par, p):
                pair = u * PAIRS + p
                slot = pair_slot(par, p)
                v.wait_ge(s_prod, pair + 1)
                nc.vector.tensor_reduce(lg[:, par, :, 2 * p:2 * p + 2].rearrange("p h t -> p t h"),
                                        prod[:, slot].rearrange("p t (h c) -> p t h c", h=H), AX.X, ALU.add
                                        ).then_inc(s_lg, 1)

            def product(u, par, half2, p):
                slot = pair_slot(par, p)
                v.wait_ge(s_g[p], u * 64 + 64)
                if not isinstance(u, int) or u * PAIRS + p >= 2:
                    v.wait_ge(s_lg, u * PAIRS + p - 1)
                nc.vector.tensor_tensor(prod[:, slot], work[:, par, 2 * p:2 * p + 2, KAT:VAT], qg[:, p], ALU.mult
                                        ).then_inc(s_prod, 1)

            def maxima(u, par, half2):
                half = slice(u - 1, u) if isinstance(u, int) else ds(u - 1, 1)
                new_f = k["new_fwd"][:, half].rearrange("p o e -> p (o e)")
                new_b = k["new_bwd"][:, half].rearrange("p o e -> p (o e)")
                v.wait_ge(s_lT, u)
                nc.vector.tensor_tensor_scan(mT[:, 0, ::-1], new_f, ps_l[0:4 * G, 0:P], LOW, ALU.add, ALU.max
                                             ).then_inc(s_scan, 1)
                v.wait_ge(s_scan, u)
                nc.vector.tensor_tensor_scan(mT[:, 1, ::-1], new_b, mT[:, 0], LOW, ALU.add, ALU.max
                                             ).then_inc(s_mT, 1)
                v.wait_ge(s_max, u)
                col = ps_m[:, 0:4 * G].rearrange("p (h t) -> p h t", h=H)
                nc.vector.tensor_tensor(diff[:], lg[:, 1 - par], col, ALU.subtract).then_inc(s_diff, 1)
                if not (isinstance(u, int) and u < 3):
                    v.wait_ge(s_st[1 - par], stored(par, half2) * (16 * PAIRS))
                nc.vector.tensor_copy(res[:, 1 - par, :, MAXAT:ROW], col.rearrange("p h t -> p t h")
                                      ).then_inc(s_mcol, 1)

            def weigh(u, par, p):
                pair = (u - 1) * PAIRS + p
                slot = pair_slot(1 - par, p)
                n = (u - 1) * G + 2 * p
                own = k["dst_col"][:, n:n + 2] if isinstance(u, int) else k["dst_col"][:, ds(n, 2)]
                if not isinstance(u, int) or pair >= 2:
                    v.wait_ge(s_sum, pair - 1)
                nc.vector.tensor_tensor(
                    seg[:, slot], drow[:, 1 - par, 2 * p * P:(2 * p + 2) * P].rearrange("p (t e) -> p t e", t=2),
                    own.unsqueeze(2).to_broadcast([P, 2, P]), ALU.is_equal).then_inc(s_seg, 1)
                rows = work[:, 1 - par, 2 * p:2 * p + 2, 0:MAXAT].rearrange("p t (h c) -> p t h c", h=H)
                nc.vector.tensor_tensor(
                    rows[:, :, :, 0:C], work[:, 1 - par, 2 * p:2 * p + 2, VAT:SLOT].rearrange(
                        "p t (h c) -> p t h c", h=H),
                    rows[:, :, :, C:HW].to_broadcast([P, 2, H, C]), ALU.mult).then_inc(s_wv, 1)

            def stage(u, par, half2, has_a, has_c):
                if has_c:
                    maxima(u, par, half2)
                    v.wait_ge(s_w8, u)
                    v.wait_ge(s_dr[1 - par], dr_use(par, half2) * (16 * PAIRS))
                for p in range(PAIRS):
                    if has_c:
                        weigh(u, par, p)
                    if has_a:
                        product(u, par, half2, p)
                        if p >= 1:
                            logits(u, par, p - 1)
                if has_a:
                    logits(u, par, PAIRS - 1)

            def dr_use(par, half2):
                return half2 if par == 0 else half2 + 1

            stages(v, stage)


def chain_pass(nc, a, tables, k, layer, ahead, add=None):
    with ExitStack() as ctx:
        nm = f"c{layer}_"
        sb = lambda name, shape, dt=F32: ctx.enter_context(nc.sbuf_tensor(nm + name, shape, dt))
        sem = lambda name: ctx.enter_context(nc.semaphore(nm + name))
        ps = lambda name, shape: ctx.enter_context(nc.psum_tensor(nm + name, shape, F32))
        last = sb("last", [CR, CH, ROW])
        run = sb("run", [H, T])
        wgt = sb("wgt", [CR, H, CH, T])
        out = sb("out", [CR, CH, ROW])
        ps_t, ps_r = ps("ps_t", [P, 512]), ps("ps_r", [P, 512])
        ps_b, ps_o = ps("ps_b", [P, 2, 512]), ps("ps_o", [P, CH, 512])
        s_in, s_t, s_run, s_b, s_r, s_arg, s_exp, s_wgt, s_o, s_out, s_m, s_st = (
            sem(n) for n in ("in", "turned", "run", "spread", "back", "arg", "exp", "wgt", "sums", "out", "m", "st"))
        s_ahead = sem("ahead")
        block = ctx.enter_context(nc.Block())

        @block.sync
        def _(sp):
            rows = tables["part"][0:EDGES].rearrange("(c r p) w -> p r c w", c=CH, p=P)
            sp.dma_start(last[:], rows[P - 1]).then_inc(s_in, 16)
            for buffer, source in ahead:
                sp.dma_start(buffer[:], source).then_inc(s_ahead, 16)
            sp.wait_ge(s_out, CH)
            sp.wait_ge(s_m, 1)
            sp.dma_start(tables["part"][NULL + 1:NULL + 1 + T].rearrange("(c r) w -> r c w", c=CH), out[:]
                         ).then_inc(s_st, 16)
            sp.wait_ge(s_st, 16)
            sp.wait_ge(s_ahead, 16 * len(ahead))

        @block.tensor
        def _(te):
            te.wait_ge(s_in, 16)
            for c in range(CH):
                tr = nc.tensor.transpose(ps_t[0:H, c * CR:(c + 1) * CR], last[:, c, MAXAT:ROW],
                                         k["ident"][0:CR, 0:CR])
            tr.then_inc(s_t, 1)
            te.wait_ge(s_run, 1)
            for c in range(CH):
                tr = nc.tensor.transpose(ps_r[0:CR, c * H:(c + 1) * H], run[:, c * CR:(c + 1) * CR],
                                         k["ident"][0:H, 0:H])
            tr.then_inc(s_r, 1)
            def spread(h):
                if h >= 2:
                    te.wait_ge(s_arg, h - 1)
                nc.tensor.matmul(ps_b[0:CR, h % 2, 0:T], k["head_row"][:, h], run[:], start=True, stop=True
                                 ).then_inc(s_b, 1)

            spread(0)
            spread(1)
            for h in range(H):
                if h + 2 < H:
                    spread(h + 2)
                te.wait_ge(s_wgt, h + 1)
                for c in range(CH):
                    for e in range(c + 1):
                        mm = nc.tensor.matmul(ps_o[0:CR, c, h * HW:(h + 1) * HW],
                                              wgt[:, h, e, c * CR:(c + 1) * CR],
                                              last[:, e, h * HW:(h + 1) * HW], start=(e == 0), stop=(e == c))
                    if h == H - 1:
                        mm.then_inc(s_o, 1)

        @block.vector
        def _(v):
            v.wait_ge(s_t, 1)
            nc.vector.tensor_tensor_scan(run[:], k["chain_new"][:], ps_t[0:H, 0:T], LOW, ALU.add, ALU.max
                                         ).then_inc(s_run, 1)
            v.wait_ge(s_r, 1)
            nc.vector.tensor_copy(out[:, :, MAXAT:ROW], ps_r[0:CR, 0:CH * H].rearrange("p (c h) -> p c h", c=CH)
                                  ).then_inc(s_m, 1)

            def mask(h):
                v.wait_ge(s_exp, h + 1)
                for e in range(CH):
                    ins = nc.vector.tensor_tensor(wgt[:, h, e, e * CR:T], wgt[:, h, e, e * CR:T],
                                                  k["chain_mask"][:, e, e * CR:T], ALU.mult)
                ins.then_inc(s_wgt, 1)

            for h in range(H):
                v.wait_ge(s_b, h + 1)
                for e in range(CH):
                    ins = nc.vector.tensor_scalar(wgt[:, h, e, e * CR:T], ps_b[0:CR, h % 2, e * CR:T],
                                                  last[:, e, MAXAT + h:MAXAT + h + 1], 0.0,
                                                  ALU.subtract, ALU.max)
                ins.then_inc(s_arg, 1)
                if h:
                    mask(h - 1)
            mask(H - 1)
            if add:
                v.wait_ge(s_ahead, 16 * len(ahead))
                nc.vector.tensor_tensor(add[0][:], add[0][:], add[1][:], ALU.add)

        @block.scalar
        def _(act):
            for h in range(H):
                act.wait_ge(s_arg, h + 1)
                for e in range(CH):
                    ins = nc.scalar.activation(wgt[:, h, e, e * CR:T], wgt[:, h, e, e * CR:T], ACT.Exp, scale=-INV)
                ins.then_inc(s_exp, 1)
            for c in range(CH):
                act.wait_ge(s_o, c + 1)
                nc.scalar.copy(out[:, c, 0:MAXAT], ps_o[0:CR, c, 0:MAXAT]).then_inc(s_out, 1)


def last_blocks(nc, a, tables, k):
    RING = 4
    with ExitStack() as ctx:
        sb = lambda name, shape, dt=F32: ctx.enter_context(nc.sbuf_tensor("l_" + name, shape, dt))
        sem = lambda name: ctx.enter_context(nc.semaphore("l_" + name))
        x1, z = k["x1"], sb("z", [P, RING, D])
        part, idx = sb("part", [P, 2, 2, 2, ROW]), sb("idx", [P, 2, 2, 2], U32)
        mx, dm, sc = sb("mx", [P, 2, 2, H]), sb("dm", [P, 2, 2, 2, H]), sb("sc", [P, 2, 2, 2, H])
        scaled, den, joined = sb("scaled", [P, 2, 2, H, HW]), sb("den", [P, 2, H]), sb("joined", [P, 2, D])
        stats, mv = sb("stats", [P, 2, 6]), sb("mv", [P, 2, 2])
        moments, var, rs = sb("moments", [P, NB, 2]), sb("var", [P, NB]), sb("rs", [P, NB])
        zT, wg, bg, zero = sb("zT", [P, 2, 2, P]), sb("wg", [P, 2, XN]), sb("bg", [P, XN]), sb("zero", [P, D])
        ps_turn = ctx.enter_context(nc.psum_tensor("l_turn", [P, 2, 512], F32))
        ps_sc = ctx.enter_context(nc.psum_tensor("l_scores", [P, 2, 512], F32))
        s_w, s_wx, s_idx, s_max, s_dm, s_sc, s_join, s_x1, s_var, s_std, s_rs, s_z, s_turn, s_zT, s_mm, s_score, s_zero, s_st = (
            sem(n) for n in ("weights", "expertWeights", "idx", "max", "dm", "sc", "join", "x1", "var", "std",
                             "rs", "z", "turned", "zT", "products", "score", "zero", "stored"))
        s_mv = sem("mv")
        s_passed, s_ppassed = sem("passed"), sem("ppassed")
        s_part = [sem(f"part{i}") for i in range(2)]
        s_zst = [sem(f"zStored{i}") for i in range(RING)]
        NPAIR = NB // 2 + 1
        JOIN = 7
        CHUNK = 5
        block = ctx.enter_context(nc.Block())

        def width(p):
            return 1 if isinstance(p, int) and p == NPAIR - 1 else 2

        def pair_of(ap, p):
            return ap[:, 2 * p:2 * p + width(p)] if isinstance(p, int) else ap[:, ds(p * 2, 2)]

        @block.sync
        def _(sp):
            sp.dma_start(wg[:], a["wg"].rearrange("(c p) n -> p c n", p=P)).then_inc(s_w, 16)
            sp.dma_start(bg[:], a["bg"][None, :].to_broadcast([P, XN])).then_inc(s_w, 16)
            def store_x1(i):
                sp.wait_ge(s_x1, (CHUNK * (i + 1) + 1) // 2)
                sp.dma_start(blocks(tables["acc"][0:NP])[:, i * CHUNK:(i + 1) * CHUNK],
                             x1[:, i * CHUNK:(i + 1) * CHUNK]).then_inc(s_st, 16)

            for e in range(XN):
                sp.wait_ge(s_x1, e + 1)
                sp.dma_start(k["w1"][:, e], a["w1x"][e].rearrange("(c p) h -> p c h", p=P)).then_inc(s_wx, 16)
                sp.dma_start(k["w2"][:, e], a["w2x"][e].rearrange("(c p) d -> p c d", p=P)).then_inc(s_wx, 16)
                sp.dma_start(k["b1"][:, e], a["b1"][e:e + 1].to_broadcast([P, XH])).then_inc(s_wx, 16)
                sp.dma_start(k["b2"][:, e], a["b2"][e:e + 1].to_broadcast([P, D])).then_inc(s_wx, 16)
                if e in (2, 4, 7):
                    store_x1((2, 4, 7).index(e))
            sp.wait_ge(s_zero, 1)
            sp.dma_start(tables["acc"][NP:NP + P], zero[:]).then_inc(s_st, 16)
            sp.dma_start(tables["z"][NP:NP + P], zero[:]).then_inc(s_st, 16)
            for i in range(3, NB // CHUNK):
                store_x1(i)

            def store(j, s, use):
                sp.wait_ge(s_z, j + 1)
                sp.dma_start(rows_of(tables["z"], j), z[:, s]).then_inc(s_zst[s], 16)
            each(sp, store, NB, RING)
            for s in range(RING):
                sp.wait_ge(s_zst[s], 16 * len(range(s, NB, RING)))
            sp.wait_ge(s_st, 16 * (2 + NB // CHUNK))
            sp.wait_ge(s_wx, 16 * 4 * XN)

        @block.gpsimd
        def _(pool):
            nc.gpsimd.memset(zero[:], 0.0).then_inc(s_zero, 1)

            def step(p, s, use):
                if later(p):
                    pool.wait_ge(s_join, p * JOIN - (2 * JOIN - 1))
                n = width(p)
                nc.gpsimd.tensor_copy(idx[:, s, 0:n], pair_of(k["rows"], p)).then_inc(s_idx, 1)
                wait_alone(pool, s_idx, p + 1, s_ppassed)
                for i in range(n):
                    for r in range(2):
                        nc.gpsimd.indirect_dma_start(part[:, s, i, r], None, tables["part"],
                                                     bass.IndirectOffsetOnAxis(idx[:, s, i, r:r + 1], 0)
                                                     ).then_inc(s_part[s], 16)
            each(pool, step, NPAIR)

        @block.vector
        def _(v):
            c, m = Chain(v, s_join, s_passed), Chain(v, s_max)

            def spread(p, s, use):
                w = width(p)
                v.wait_ge(s_part[s], use * 64 if w == 2 else (use - 1) * 64 + 32)
                m.base, m.n = p, 0
                m.after(nc.vector.tensor_tensor(mx[:, s, 0:w], part[:, s, 0:w, 0, MAXAT:ROW],
                                                part[:, s, 0:w, 1, MAXAT:ROW], ALU.max))
                nc.vector.tensor_tensor(dm[:, s, 0:w], part[:, s, 0:w, :, MAXAT:ROW],
                                        mx[:, s, 0:w, None, :].to_broadcast([P, w, 2, H]), ALU.subtract
                                        ).then_inc(s_dm, 1)

            def step(p, s, use):
                w = width(p)
                c.base, c.n = p * JOIN, 0
                v.wait_ge(s_sc, p + 1)
                c.after(nc.vector.tensor_tensor(
                    scaled[:, 0:w].rearrange("p b r h c -> p (b r) h c"),
                    part[:, s, 0:w, :, 0:MAXAT].rearrange("p b r (h c) -> p (b r) h c", h=H),
                    sc[:, s, 0:w].rearrange("p b r h -> p (b r) h").unsqueeze(3).to_broadcast([P, 2 * w, H, HW]),
                    ALU.mult))
                c.after(nc.vector.tensor_tensor(scaled[:, 0:w, 0], scaled[:, 0:w, 0], scaled[:, 0:w, 1], ALU.add))
                c.after(nc.vector.tensor_scalar(den[:, 0:w], scaled[:, 0:w, 0, :, C], 1e-16, None, ALU.add))
                c.after(nc.vector.reciprocal(den[:, 0:w], den[:, 0:w]))
                c.after(nc.vector.tensor_tensor(
                    joined[:, 0:w].rearrange("p b (h c) -> p b h c", h=H), scaled[:, 0:w, 0, :, 0:C],
                    den[:, 0:w].unsqueeze(3).to_broadcast([P, w, H, C]), ALU.mult))
                rows = pair_of(x1, p)
                c.after(nc.vector.tensor_tensor(rows, joined[:, 0:w], rows, ALU.add), alone=True)
                if not (isinstance(p, int) and p == NPAIR - 1):
                    spread(p + 1, 1 - s, use + s)
                for i in range(w):
                    ins = nc.vector.bn_stats(stats[:, i], block_of(x1, p * 2 + i))
                c.after(ins, alone=True)
                for i in range(w):
                    ins = nc.vector.bn_aggr(mv[:, i], stats[:, i])
                ins.then_inc(s_mv, 1)
                v.wait_ge(s_mv, p + 1)
                assert c.n == JOIN
                nc.vector.tensor_copy(pair_of(moments, p), mv[:, 0:w]).then_inc(s_x1, 1)

            spread(0, 0, 1)
            each(v, step, NPAIR)

            v.wait_ge(s_x1, NPAIR)
            nc.vector.tensor_scalar(var[:], moments[:, :, 1], EPS, None, ALU.add).then_inc(s_var, 1)
            v.wait_ge(s_std, 1)
            nc.vector.reciprocal(rs[:], rs[:]).then_inc(s_rs, 1)
            v.wait_ge(s_rs, 1)
            v.wait_ge(s_w, 32)

            def norm(j, s, use):
                if later(j, RING):
                    v.wait_ge(s_turn, j - (RING - 1))
                    v.wait_ge(s_zst[s], (use - 1) * 16)
                at = slice(j, j + 1) if isinstance(j, int) else ds(j, 1)
                nc.vector.tensor_scalar(z[:, s], block_of(x1, j), moments[:, at, 0], rs[:, at],
                                        ALU.subtract, ALU.mult).then_inc(s_z, 1)

            def score(j, s):
                v.wait_ge(s_mm, j + 1)
                nc.vector.tensor_tensor(block_of(k["scores"], j), ps_sc[:, s, 0:XN], bg[:], ALU.add
                                        ).then_inc(s_score, 1)

            def sweep(j, s, use):
                norm(j, s, use)
                if later(j):
                    score(j - 2, s % 2)
            each(v, sweep, NB, RING)
            score(NB - 2, 1)
            score(NB - 1, 0)
            v.wait_ge(s_score, NB)

        @block.scalar
        def _(act):
            def rescale(p, s, use):
                w = width(p)
                act.wait_ge(s_dm, p + 1)
                nc.scalar.activation(sc[:, s, 0:w], dm[:, s, 0:w], ACT.Exp, scale=INV).then_inc(s_sc, 1)
            each(act, rescale, NPAIR)
            act.wait_ge(s_var, 1)
            nc.scalar.activation(rs[:], var[:], ACT.Sqrt).then_inc(s_std, 1)

            def step(j, s, use):
                act.wait_ge(s_turn, j + 1)
                if later(j):
                    act.wait_ge(s_mm, j - 1)
                nc.scalar.copy(zT[:, s], ps_turn[:, s, 0:D].rearrange("p (c n) -> p c n", c=2)).then_inc(s_zT, 1)
            each(act, step)

        @block.tensor
        def _(te):
            def turn(j, slot):
                s = slot % 2
                te.wait_ge(s_z, j + 1)
                if later(j):
                    te.wait_ge(s_zT, j - 1)
                nc.tensor.transpose(ps_turn[:, s, 0:P], z[:, slot, 0:P], k["ident"][:])
                nc.tensor.transpose(ps_turn[:, s, P:D], z[:, slot, P:D], k["ident"][:]).then_inc(s_turn, 1)

            def products(j, s):
                te.wait_ge(s_zT, j + 1)
                if later(j):
                    te.wait_ge(s_score, j - 1)
                for c in range(2):
                    mm = nc.tensor.matmul(ps_sc[:, s, 0:XN], zT[:, s, c], wg[:, c], start=(c == 0), stop=(c == 1))
                mm.then_inc(s_mm, 1)

            te.wait_ge(s_w, 32)

            def step(j, s, use):
                turn(j, s)
                if not isinstance(j, int) or j >= 1:
                    products(j - 1, 1 - s % 2)
            each(te, step, NB, RING)
            products(NB - 1, 0)


def route(nc, k):
    with ExitStack() as ctx:
        sb = lambda name, shape, dt=F32: ctx.enter_context(nc.sbuf_tensor("r_" + name, shape, dt))
        sem = lambda name: ctx.enter_context(nc.semaphore("r_" + name))
        ps_pre, ps_tot, ps_perm = (ctx.enter_context(nc.psum_tensor("r_ps" + n, [P, 512], F32))
                                   for n in ("pre", "tot", "perm"))
        best, cand, low = sb("best", [P, NB]), sb("cand", [P, NB, XN]), sb("low", [P, NB])
        hit, rest = sb("hit", [P, 2, NB, XN]), sb("rest", [P, NB, XN])
        goes = sb("goes", [P, NB, XN])
        keep, tot = sb("keep", [P, XN, NB]), sb("tot", [P, XN, NB])
        upto, place = sb("upto", [P, XN, NB]), sb("place", [P, XN, NB])
        tiles_i = sb("tiles_i", [P, XN], I32)
        tiles, ends, begin, zero = (sb(n, [P, XN]) for n in ("tiles", "ends", "begin", "zero"))
        slots, slots_i = sb("slots", [P, 2, NB]), sb("slots_i", [P, 2, NB], I32)
        lo_i, hi_i = sb("lo_i", [P, 2, NB], I32), sb("hi_i", [P, 2, NB], I32)
        lo, hi = sb("lo", [P, 2, NB]), sb("hi", [P, 2, NB])
        hot = k["x1"][:].rearrange("p b (r n) -> p r b n", r=2)[:, :, :, 0:TX]
        halves = k["skip"][:].bitcast(BF16)
        hot_lo = halves[:, :, 0:2 * P].rearrange("p b (r n) -> p r b n", r=2)
        hot_hi = halves[:, :, 2 * P:2 * P + 4 * TX].rearrange("p b (r n) -> p r b n", r=2)
        at_e, at_t, at_p = sb("at_e", [P, XN]), sb("at_t", [P, TX]), sb("at_p", [P, P])
        node_lo, node_hi, pad = sb("node_lo", [P, 1]), sb("node_hi", [P, NB]), sb("pad", [P, 1])
        both = sb("both", [P, TX])
        after, expert = sb("after", [1, TX, XN - 1]), sb("expert", [1, TX])
        none, perm = sb("none", [P, TX]), sb("permf", [P, TX])
        s_pool, s_v, s_goes, s_cum, s_hot, s_perm = (
            sem(n) for n in ("pool", "vec", "goes", "cum", "hot", "perm"))
        BIG = 65536.0
        block = ctx.enter_context(nc.Block())

        @block.gpsimd
        def _(pool):
            iota = lambda out, pattern, base, ch: nc.gpsimd.iota(
                out, pattern=pattern, base=base, channel_multiplier=ch,
                allow_small_or_imprecise_dtypes=True).then_inc(s_pool, 1)
            iota(at_e[:], [[1, XN]], 0, 0)
            iota(at_t[:], [[1, TX]], 0, 0)
            iota(at_p[:], [[1, P]], 0, 0)
            iota(node_lo[:], [[1, 1]], 1, 1)
            iota(node_hi[:], [[P, NB]], 0, 0)
            iota(pad[:], [[1, 1]], NP + 1, 1)
            nc.gpsimd.memset(keep[:, :, 1:NB], 1.0).then_inc(s_pool, 1)
            nc.gpsimd.memset(keep[:, :, 0:1], 0.0).then_inc(s_pool, 1)
            nc.gpsimd.memset(zero[:], 0.0).then_inc(s_pool, 1)

        @block.vector
        def _(v):
            c = Chain(v, s_v)
            tt, ts = nc.vector.tensor_tensor, nc.vector.tensor_scalar
            over_b = lambda ap: ap.unsqueeze(2).to_broadcast([P, NB, XN])
            v.wait_ge(s_pool, 9)
            score = k["scores"]
            for r in range(2):
                c.after(nc.vector.tensor_reduce(best[:], score[:], AX.X, ALU.max))
                c.after(tt(cand[:], score[:], over_b(best[:]), ALU.is_equal))
                c.after(nc.vector.scalar_tensor_tensor(
                    out=cand[:], in0=cand[:], scalar=-100.0, in1=at_e[:, None, :].to_broadcast([P, NB, XN]),
                    op0=ALU.mult, op1=ALU.add))
                c.after(nc.vector.tensor_reduce(low[:], cand[:], AX.X, ALU.min))
                c.after(tt(hit[:, r], cand[:], over_b(low[:]), ALU.is_equal))
                if r == 0:
                    c.after(nc.vector.scalar_tensor_tensor(out=rest[:], in0=hit[:, 0], scalar=-HUGE, in1=score[:],
                                                           op0=ALU.mult, op1=ALU.add))
                    score = rest
            tt(goes[:], hit[:, 0], hit[:, 1], ALU.add).then_inc(s_goes, 1)
            v.wait_ge(s_cum, 2)
            by_e = lambda ap: ap.rearrange("p b e -> p e b")
            from_ps = lambda ps: by_e(ps[:, 0:NB * XN].rearrange("p (b e) -> p b e", e=XN))
            flat = lambda t: t[:].rearrange("p e b -> p (e b)")
            c.after(nc.vector.tensor_copy(tot[:], from_ps(ps_tot)))
            c.after(nc.vector.tensor_tensor_scan(flat(upto), flat(keep), flat(tot), 0.0, ALU.mult, ALU.add))
            c.after(ts(tiles[:], upto[:, :, NB - 1], float(P - 1), None, ALU.add))
            c.after(nc.vector.tensor_copy(tiles_i[:], tiles[:]))
            c.after(nc.vector.tensor_single_scalar(tiles_i[:], tiles_i[:], 7, ALU.arith_shift_right))
            c.after(nc.vector.tensor_copy(tiles[:], tiles_i[:]))
            c.after(nc.vector.tensor_tensor_scan(ends[:], tiles[:], zero[:], 0.0, ALU.add, ALU.add))
            c.after(tt(begin[:], ends[:], tiles[:], ALU.subtract))
            c.after(ts(begin[:], begin[:], float(P), -1.0, ALU.mult, ALU.add))
            c.after(tt(place[:], upto[:], tot[:], ALU.subtract))
            c.after(tt(place[:], place[:], begin[:].unsqueeze(2).to_broadcast([P, XN, NB]), ALU.add))
            c.after(tt(place[:], place[:], from_ps(ps_pre), ALU.add))
            c.after(tt(place[:], place[:], by_e(goes[:]), ALU.mult))
            c.after(nc.vector.tensor_reduce(slots[:, 1], place[:].rearrange("p e b -> p b e"), AX.X, ALU.max))
            c.after(nc.vector.scalar_tensor_tensor(out=place[:], in0=by_e(goes[:]), scalar=-BIG, in1=place[:],
                                                   op0=ALU.mult, op1=ALU.add))
            c.after(nc.vector.tensor_reduce(slots[:, 0], place[:].rearrange("p e b -> p b e"), AX.X, ALU.min))
            c.after(ts(slots[:, 0], slots[:, 0], BIG, None, ALU.add))
            c.after(nc.vector.tensor_copy(slots_i[:], slots[:]))
            c.after(nc.vector.tensor_single_scalar(lo_i[:], slots_i[:], P - 1, ALU.bitwise_and))
            c.after(nc.vector.tensor_single_scalar(hi_i[:], slots_i[:], 7, ALU.arith_shift_right))
            c.after(nc.vector.tensor_copy(lo[:], lo_i[:]))
            c.after(nc.vector.tensor_copy(hi[:], hi_i[:]))
            for r in range(2):
                tt(hot_lo[:, r], lo[:, r].unsqueeze(2).to_broadcast([P, NB, P]),
                   at_p[:, None, :].to_broadcast([P, NB, P]), ALU.is_equal).then_inc(s_hot, 1)
                c.after(tt(hot[:, r], hi[:, r].unsqueeze(2).to_broadcast([P, NB, TX]),
                           at_t[:, None, :].to_broadcast([P, NB, TX]), ALU.is_equal))
                ts(hot_hi[:, r, :, 0:TX], hot[:, r], node_lo[:, 0:1], None, ALU.mult).then_inc(s_hot, 1)
                tt(hot_hi[:, r, :, TX:2 * TX], hot[:, r], node_hi[:].unsqueeze(2).to_broadcast([P, NB, TX]),
                   ALU.mult).then_inc(s_hot, 1)
            c.after(tt(after[:], at_t[0:1].unsqueeze(2).to_broadcast([1, TX, XN - 1]),
                       ends[0:1, None, 0:XN - 1].to_broadcast([1, TX, XN - 1]), ALU.is_ge))
            c.after(nc.vector.tensor_reduce(expert[:], after[:], AX.X, ALU.add))
            c.after(nc.vector.tensor_copy(k["expert"][:], expert[:]))
            v.wait_ge(s_perm, 1)
            c.after(nc.vector.tensor_copy(perm[:], ps_perm[:, 0:TX]))
            c.after(tt(both[:], perm[:], ps_perm[:, TX:2 * TX], ALU.add))
            c.after(ts(none[:], both[:], 0.0, pad[:, 0:1], ALU.is_equal, ALU.mult))
            c.after(nc.vector.scalar_tensor_tensor(out=perm[:], in0=both[:], scalar=-1.0, in1=none[:],
                                                   op0=ALU.add, op1=ALU.add))
            c.after(nc.vector.tensor_copy(k["perm"][:], perm[:]))

        @block.tensor
        def _(te):
            te.wait_ge(s_goes, 1)
            goes_f = goes[:].rearrange("p b e -> p (b e)")
            nc.tensor.matmul(ps_pre[:, 0:NB * XN], k["tri"][:], goes_f, start=True, stop=True).then_inc(s_cum, 1)
            nc.tensor.matmul(ps_tot[:, 0:NB * XN], k["ones"][:], goes_f, start=True, stop=True).then_inc(s_cum, 1)
            for r in range(2):
                te.wait_ge(s_hot, 3 * r + 3)
                for b in range(NB):
                    mm = nc.tensor.matmul(ps_perm[:, 0:2 * TX], hot_lo[:, r, b], hot_hi[:, r, b],
                                          start=(r == 0 and b == 0), stop=(r == 1 and b == NB - 1))
            mm.then_inc(s_perm, 1)


def experts(nc, a, tables, k):
    with ExitStack() as ctx:
        sb = lambda name, shape, dt=F32: ctx.enter_context(nc.sbuf_tensor("x_" + name, shape, dt))
        sem = lambda name: ctx.enter_context(nc.semaphore("x_" + name))
        ps = lambda name: ctx.enter_context(nc.psum_tensor("x_" + name, [P, 2, 512], F32))
        RING = 4
        gi, si = sb("gi", [P, RING], U32), sb("si", [P, 2], U32)
        zg, zT = sb("zg", [P, RING, D]), sb("zT", [P, 2, 2, P])
        pre, hid, y = sb("pre", [P, 2, XH]), sb("hid", [P, 2, XH]), sb("y", [P, 2, D])
        ps_z, ps_h, ps_t, ps_y = ps("ps_z"), ps("ps_h"), ps("ps_t"), ps("ps_y")
        s_gi, s_si, s_tz, s_zT, s_h, s_pre, s_th, s_hid, s_mm, s_y, s_add, s_out, s_ppassed = (
            sem(n) for n in ("gi", "si", "turnedZ", "zT", "h", "pre", "turnedH", "hid", "products", "y", "added",
                             "out", "ppassed"))
        s_g = [sem(f"gathered{i}") for i in range(RING)]
        block = ctx.enter_context(nc.Block())

        def has_second_next(j):
            return not isinstance(j, int) or j + 2 < TX

        def has_previous(j):
            return not isinstance(j, int) or j >= 1

        def expert_of(eng, j):
            col = slice(j, j + 1) if isinstance(j, int) else ds(j, 1)
            return eng.value_load(k["expert"][0:1, col], min_val=0, max_val=XN - 1)

        @block.gpsimd
        def _(pool):
            def column(j):
                return k["perm"][:, j:j + 1] if isinstance(j, int) else k["perm"][:, ds(j, 1)]

            def gather(j, s):
                nc.gpsimd.tensor_copy(gi[:, s:s + 1], column(j)).then_inc(s_gi, 1)
                wait_alone(pool, s_gi, j + 1, s_ppassed)
                nc.gpsimd.indirect_dma_start(zg[:, s], None, tables["z"],
                                             bass.IndirectOffsetOnAxis(gi[:, s:s + 1], 0)).then_inc(s_g[s], 16)

            def add(j, s):
                if has_previous(j):
                    wait_alone(pool, s_add, j * 16, s_ppassed)
                nc.gpsimd.tensor_copy(si[:, s:s + 1], column(j)).then_inc(s_si, 1)
                wait_alone(pool, s_si, j + 1, s_ppassed)
                wait_alone(pool, s_y, j + 1, s_ppassed)
                nc.gpsimd.indirect_dma_start(tables["acc"], bass.IndirectOffsetOnAxis(si[:, s:s + 1], 0),
                                             y[:, s], None, compute_op=ALU.add).then_inc(s_add, 16)

            def step(j, s, use):
                if not isinstance(j, int) or j + RING < TX:
                    pool.wait_ge(s_tz, j + 1)
                    gather(j + RING, s)
                if has_previous(j):
                    add(j - 1, 1 - s % 2)
            for j in range(RING):
                gather(j, j)
            each(pool, step, TX, RING)
            add(TX - 1, (TX - 1) % 2)

        @block.tensor
        def _(te):
            def turn_z(j, slot, use):
                s = slot % 2
                te.wait_ge(s_g[slot], use * 16)
                if later(j):
                    te.wait_ge(s_zT, j - 1)
                for c in range(2):
                    tr = nc.tensor.transpose(ps_z[:, s, c * P:(c + 1) * P], zg[:, slot, c * P:(c + 1) * P],
                                             k["ident"][:])
                tr.then_inc(s_tz, 1)

            def hidden(j, s):
                e = expert_of(te, j)
                te.wait_ge(s_zT, j + 1)
                if later(j):
                    te.wait_ge(s_pre, j - 1)
                for c in range(2):
                    mm = nc.tensor.matmul(ps_h[:, s, 0:XH], zT[:, s, c],
                                          k["w1"][:, ds(e, 1), c].rearrange("p o h -> p (o h)"),
                                          start=(c == 0), stop=(c == 1))
                mm.then_inc(s_h, 1)

            def turn_hidden(j, s):
                te.wait_ge(s_pre, j + 1)
                if later(j):
                    te.wait_ge(s_hid, j - 1)
                for c in range(HC):
                    tr = nc.tensor.transpose(ps_t[:, s, c * P:(c + 1) * P], pre[:, s, c * P:(c + 1) * P],
                                             k["ident"][:])
                tr.then_inc(s_th, 1)

            def outputs(j, s):
                e = expert_of(te, j)
                te.wait_ge(s_hid, j + 1)
                if later(j):
                    te.wait_ge(s_y, j - 1)
                for c in range(HC):
                    mm = nc.tensor.matmul(ps_y[:, s, 0:D], hid[:, s, c * P:(c + 1) * P],
                                          k["w2"][:, ds(e, 1), c].rearrange("p o d -> p (o d)"),
                                          start=(c == 0), stop=(c == HC - 1))
                mm.then_inc(s_mm, 1)

            def step(j, slot, use):
                s = slot % 2
                hidden(j, s)
                if has_previous(j):
                    outputs(j - 1, 1 - s)
                turn_hidden(j, s)
                if has_second_next(j):
                    turn_z(j + 2, (slot + 2) % RING, use + (slot + 2) // RING)
            turn_z(0, 0, 1)
            turn_z(1, 1, 1)
            each(te, step, TX, RING)
            outputs(TX - 1, (TX - 1) % 2)

        @block.scalar
        def _(act):
            def copy_z(j, s):
                act.wait_ge(s_tz, j + 1)
                if later(j):
                    act.wait_ge(s_h, j - 1)
                nc.scalar.copy(zT[:, s], ps_z[:, s, 0:D].rearrange("p (c n) -> p c n", c=2)).then_inc(s_zT, 1)

            def step(j, s, use):
                act.wait_ge(s_th, j + 1)
                if later(j):
                    act.wait_ge(s_mm, j - 1)
                nc.scalar.activation(hid[:, s], ps_t[:, s, 0:XH], ACT.Gelu).then_inc(s_hid, 1)
                if has_second_next(j):
                    copy_z(j + 2, s)
            copy_z(0, 0)
            copy_z(1, 1)
            each(act, step, TX)

        @block.vector
        def _(v):
            def results(j, s):
                e = expert_of(v, j)
                v.wait_ge(s_mm, j + 1)
                if later(j):
                    v.wait_ge(s_add, j * 16 - 16)
                nc.vector.tensor_tensor(y[:, s], ps_y[:, s, 0:D], k["b2"][:, ds(e, 1)].rearrange("p o d -> p (o d)"),
                                        ALU.add).then_inc(s_y, 1)

            def step(j, s, use):
                e = expert_of(v, j)
                v.wait_ge(s_h, j + 1)
                if later(j):
                    v.wait_ge(s_th, j - 1)
                nc.vector.tensor_tensor(pre[:, s], ps_h[:, s, 0:XH], k["b1"][:, ds(e, 1)].rearrange("p o h -> p (o h)"),
                                        ALU.add).then_inc(s_pre, 1)
                if has_previous(j):
                    results(j - 1, 1 - s)
            each(v, step, TX)
            results(TX - 1, (TX - 1) % 2)

        @block.sync
        def _(sp):
            sp.wait_ge(s_add, 16 * TX)
            sp.dma_start(a["out"], tables["acc"][0:N]).then_inc(s_out, 16)
            sp.wait_ge(s_out, 16)


def kernel(x, src, dst, edge_attr_194, **w):
    import concourse.bacc as bacc
    from concourse.bass_utils import run_bass_kernel_spmd

    g, f = (lambda n: np.asarray(w["L0_gnn_" + n])), (lambda n: np.asarray(w["L0_ffn_" + n]))
    x, src, dst, attr = (np.asarray(v) for v in (x, src, dst, edge_attr_194))
    src_p = np.concatenate([src, np.zeros(EDGES - E_REAL, src.dtype)])
    dst_p = np.concatenate([dst, np.full(EDGES - E_REAL, NP - 1, dst.dtype)])
    arrays = {
        "x": np.pad(x, ((0, NP - N), (0, 0))),
        "dst": np.concatenate([dst_p, np.full(P, NP, dst.dtype)]),
        "dst_last": dst_p[P - 1::P],
        "dst_last_cols": dst_p[P - 1::P].reshape(CH, CR).T,
        "src_cols": src_p.reshape(T, P).T,
        "dst_cols": dst_p.reshape(T, P).T,
        "ft": np.pad(attr.T, ((0, 0), (0, EDGES - E_REAL))),
        "wg": f("Wg"), "bg": f("bg"), "b2": f("b2"), "w1x": f("W1"), "w2x": f("W2"),
        "b1": f("b1"),
    }
    for l in (1, 2):
        arrays[f"w{l}"] = np.concatenate([g(f"W{m}{l}") for m in "kvqs"], axis=1)
        arrays[f"bias{l}"] = np.concatenate([g(f"b{m}{l}") for m in "kvqs"])
        arrays[f"we{l}"] = g(f"We{l}")
    nc = bacc.Bacc("TRN2", target_bir_lowering=False, num_devices=1)
    arrays = {"in_" + n: np.ascontiguousarray(v) for n, v in arrays.items()}
    aps = {n[3:]: nc.dram_tensor(n, v.shape, mybir.dt.from_np(v.dtype), kind="ExternalInput").ap()
           for n, v in arrays.items()}
    aps["out"] = nc.dram_tensor("out", (N, D), F32, kind="ExternalOutput").ap()
    kernel_program(nc, aps)
    r = run_bass_kernel_spmd(nc, [arrays], core_ids=[0])
    return r.results[0]["out"]
```
